# Optimizing a Trainium2 kernel written in Bass

```python
import numpy as np
import jax
import jax.numpy as jnp

def _softmax(x, axis=-1):
    return jax.nn.softmax(x, axis=axis)

def _gelu(x):
    return jax.nn.gelu(x, approximate=True)

def _silu(x):
    return jax.nn.silu(x)

def _sigmoid(x):
    return jax.nn.sigmoid(x)

def _layernorm(x, axis=-1, eps=1e-05):
    m = jnp.mean(x, axis=axis, keepdims=True)
    v = jnp.var(x, axis=axis, keepdims=True)
    return (x - m) / jnp.sqrt(v + eps)

def _scatter_add(tgt, idx, src, axis=0):
    return tgt.at[idx].add(src)

def _segment_sum(src, seg, n):
    return jax.ops.segment_sum(src, seg, n)
kernel_name = 'mk_adaln_ffn_d1_seqx_r4_beae27'

def setup_inputs(seed: int=0):
    np.random.seed(seed)
    _w = jnp.asarray

    def _rec_inputs():
        import jax
        import jax.numpy as jnp
        _rk = jax.random.key(seed)
        x = -0.0003929 + 0.9999 * jax.random.normal(jax.random.fold_in(_rk, 1), (8, 256, 512), jnp.float32)
        _lenS = 256 - jax.random.randint(jax.random.fold_in(_rk, 7), (8,), 0, max(1, 256 // 4) + 1, jnp.int32)
        _lenS2 = 256 - jax.random.randint(jax.random.fold_in(_rk, 8), (8,), 0, max(1, 256 // 4) + 1, jnp.int32)
        cond_2048 = 0.00782532 + 1.00527 * jax.random.normal(jax.random.fold_in(_rk, 11), (8, 512), jnp.float32)
        return (x, cond_2048)
    x, cond_2048 = _rec_inputs()

    def _L0_cond_setup():
        import jax, jax.numpy as jnp
        import numpy as np
        HEADS = 16
        EPS = 1e-06

        def _rms_norm(x, g):
            xf = x.astype(jnp.float32)
            y = xf * jax.lax.rsqrt(jnp.mean(xf * xf, axis=-1, keepdims=True) + EPS)
            return y.astype(x.dtype) * g
        key = jax.random.key(seed)
        ks = jax.random.split(key, 6)
        b, n, dim, emb_dim = (4, 512, 512, 512)
        d_head = dim // HEADS
        return {'x': jax.random.normal(ks[0], (b, n, dim), jnp.float32), 'emb': jax.random.normal(ks[1], (b, 1, emb_dim), jnp.float32), 'W_emb': jax.random.normal(ks[2], (emb_dim, 2 * dim), jnp.float32) * emb_dim ** (-0.5), 'b_emb': jnp.zeros((2 * dim,), jnp.float32), 'g_norm': jnp.ones((dim,), jnp.float32), 'W_qkv': jax.random.normal(ks[3], (dim, 3 * dim), jnp.float32) * dim ** (-0.5), 'g_q': jnp.ones((d_head,), jnp.float32), 'g_k': jnp.ones((d_head,), jnp.float32), 'W_out': jax.random.normal(ks[4], (dim, dim), jnp.float32) * dim ** (-0.5)}
    _L0_cond_all = _L0_cond_setup()
    _L0_cond_in = {k: v for k, v in _L0_cond_all.items() if k in ('W_emb', 'b_emb', 'g_norm', 'W_qkv', 'g_q', 'g_k', 'W_out')}
    del _L0_cond_all

    def _L0_ffn_setup():
        import jax, jax.numpy as jnp
        import numpy as np
        H = 512
        I = 256
        E = 32
        K = 4
        N_SHARED = 1
        EPS = 1e-06

        def _rmsnorm(x, w, eps=EPS):
            var = jnp.mean(jnp.square(x), axis=-1, keepdims=True)
            return x * jax.lax.rsqrt(var + eps) * w

        def _moe_core(x, gate_w, w13, w2):
            T = x.shape[0]
            N = T * K
            C = 2 * N // E
            logits = jnp.einsum('th,eh->te', x.astype(jnp.float32), gate_w.astype(jnp.float32))
            scores = jax.nn.softmax(logits, axis=-1)
            topk_w, topk_ids = jax.lax.top_k(scores, K)
            topk_w = topk_w / jnp.sum(topk_w, axis=-1, keepdims=True)
            flat_ids = topk_ids.reshape(-1)
            flat_w = topk_w.reshape(-1)
            order = jnp.argsort(flat_ids)
            sorted_eid = flat_ids[order]
            tok = order // K
            counts = jnp.zeros((E,), jnp.int32).at[flat_ids].add(1)
            starts = jnp.cumsum(counts) - counts
            pos = jnp.arange(N) - starts[sorted_eid]
            buf = jnp.zeros((E, C, x.shape[1]), x.dtype).at[sorted_eid, pos].set(x[tok], mode='drop')
            gu = jnp.einsum('ech,ehf->ecf', buf, w13)
            g, u = jnp.split(gu, 2, axis=-1)
            act = jax.nn.silu(g) * u
            eo = jnp.einsum('eci,eih->ech', act, w2)
            out_slots = eo[sorted_eid, pos]
            routed = jnp.zeros_like(x).at[tok].add(out_slots * flat_w[order][:, None])
            return routed
        key = jax.random.key(seed)
        ks = jax.random.split(key, 8)
        s = 1.0 / np.sqrt(H)
        si = 1.0 / np.sqrt(I)
        return {'hidden_states': jax.random.normal(ks[0], (1, 1024, H), jnp.float32), 'norm_w': jnp.ones((H,), jnp.float32), 'gate_w': jax.random.normal(ks[1], (E, H), jnp.float32) * s, 'w13': jax.random.normal(ks[2], (E, H, 2 * I), jnp.float32) * s, 'w2': jax.random.normal(ks[3], (E, I, H), jnp.float32) * si, 'shared_gate_w': jax.random.normal(ks[4], (H, I * N_SHARED), jnp.float32) * s, 'shared_up_w': jax.random.normal(ks[5], (H, I * N_SHARED), jnp.float32) * s, 'shared_down_w': jax.random.normal(ks[6], (I * N_SHARED, H), jnp.float32) * si}
    _L0_ffn_all = _L0_ffn_setup()
    _L0_ffn_in = {k: v for k, v in _L0_ffn_all.items() if k in ('norm_w', 'gate_w', 'w13', 'w2', 'shared_gate_w', 'shared_up_w', 'shared_down_w')}
    del _L0_ffn_all
    return {'x': x, 'cond_2048': cond_2048, 'L0_cond_W_emb': _L0_cond_in['W_emb'], 'L0_cond_b_emb': _L0_cond_in['b_emb'], 'L0_cond_g_norm': _L0_cond_in['g_norm'], 'L0_cond_W_qkv': _L0_cond_in['W_qkv'], 'L0_cond_g_q': _L0_cond_in['g_q'], 'L0_cond_g_k': _L0_cond_in['g_k'], 'L0_cond_W_out': _L0_cond_in['W_out'], 'L0_ffn_norm_w': _L0_ffn_in['norm_w'], 'L0_ffn_gate_w': _L0_ffn_in['gate_w'], 'L0_ffn_w13': _L0_ffn_in['w13'], 'L0_ffn_w2': _L0_ffn_in['w2'], 'L0_ffn_shared_gate_w': _L0_ffn_in['shared_gate_w'], 'L0_ffn_shared_up_w': _L0_ffn_in['shared_up_w'], 'L0_ffn_shared_down_w': _L0_ffn_in['shared_down_w']}

def reference(x, cond_2048, L0_cond_W_emb, L0_cond_b_emb, L0_cond_g_norm, L0_cond_W_qkv, L0_cond_g_q, L0_cond_g_k, L0_cond_W_out, L0_ffn_norm_w, L0_ffn_gate_w, L0_ffn_w13, L0_ffn_w2, L0_ffn_shared_gate_w, L0_ffn_shared_up_w, L0_ffn_shared_down_w):
    import jax
    import jax.numpy as jnp

    def _L0_cond_ref(x, emb, W_emb, b_emb, g_norm, W_qkv, g_q, g_k, W_out):
        import jax, jax.numpy as jnp
        import numpy as np
        HEADS = 16
        EPS = 1e-06

        def _rms_norm(x, g):
            xf = x.astype(jnp.float32)
            y = xf * jax.lax.rsqrt(jnp.mean(xf * xf, axis=-1, keepdims=True) + EPS)
            return y.astype(x.dtype) * g
        b, n, dim = x.shape
        h = HEADS
        d = dim // h
        scale_shift = emb @ W_emb + b_emb
        scale, shift = jnp.split(scale_shift, 2, axis=-1)
        xn = _rms_norm(x, g_norm) * (1.0 + scale) + shift
        qkv = xn @ W_qkv
        qkv = qkv.reshape(b, n, 3, h, d)
        q, k, v = jnp.moveaxis(qkv, 2, 0)
        q = jnp.swapaxes(q, 1, 2)
        k = jnp.swapaxes(k, 1, 2)
        v = jnp.swapaxes(v, 1, 2)
        q = _rms_norm(q, g_q)
        k = _rms_norm(k, g_k)
        logits = jnp.einsum('bhqd,bhkd->bhqk', q, k) * d ** (-0.5)
        attn = jax.nn.softmax(logits, axis=-1)
        o = jnp.einsum('bhqk,bhkd->bhqd', attn, v)
        o = jnp.swapaxes(o, 1, 2).reshape(b, n, dim)
        return o + o @ W_out

    def _L0_ffn_ref(hidden_states, norm_w, gate_w, w13, w2, shared_gate_w, shared_up_w, shared_down_w):
        import jax, jax.numpy as jnp
        import numpy as np
        H = 512
        I = 256
        E = 32
        K = 4
        N_SHARED = 1
        EPS = 1e-06

        def _rmsnorm(x, w, eps=EPS):
            var = jnp.mean(jnp.square(x), axis=-1, keepdims=True)
            return x * jax.lax.rsqrt(var + eps) * w

        def _moe_core(x, gate_w, w13, w2):
            T = x.shape[0]
            N = T * K
            C = 2 * N // E
            logits = jnp.einsum('th,eh->te', x.astype(jnp.float32), gate_w.astype(jnp.float32))
            scores = jax.nn.softmax(logits, axis=-1)
            topk_w, topk_ids = jax.lax.top_k(scores, K)
            topk_w = topk_w / jnp.sum(topk_w, axis=-1, keepdims=True)
            flat_ids = topk_ids.reshape(-1)
            flat_w = topk_w.reshape(-1)
            order = jnp.argsort(flat_ids)
            sorted_eid = flat_ids[order]
            tok = order // K
            counts = jnp.zeros((E,), jnp.int32).at[flat_ids].add(1)
            starts = jnp.cumsum(counts) - counts
            pos = jnp.arange(N) - starts[sorted_eid]
            buf = jnp.zeros((E, C, x.shape[1]), x.dtype).at[sorted_eid, pos].set(x[tok], mode='drop')
            gu = jnp.einsum('ech,ehf->ecf', buf, w13)
            g, u = jnp.split(gu, 2, axis=-1)
            act = jax.nn.silu(g) * u
            eo = jnp.einsum('eci,eih->ech', act, w2)
            out_slots = eo[sorted_eid, pos]
            routed = jnp.zeros_like(x).at[tok].add(out_slots * flat_w[order][:, None])
            return routed
        B, S, Hd = hidden_states.shape
        residual = hidden_states
        h = _rmsnorm(hidden_states, norm_w)
        x = h.reshape(-1, Hd)
        routed = _moe_core(x, gate_w, w13, w2)
        shared = jax.nn.silu(x @ shared_gate_w) * (x @ shared_up_w) @ shared_down_w
        out = residual + (routed + shared).reshape(B, S, Hd)
        return out
    x = x + _L0_ffn_ref(_L0_cond_ref(x, cond_2048[:, None, :], L0_cond_W_emb, L0_cond_b_emb, L0_cond_g_norm, L0_cond_W_qkv, L0_cond_g_q, L0_cond_g_k, L0_cond_W_out), L0_ffn_norm_w, L0_ffn_gate_w, L0_ffn_w13, L0_ffn_w2, L0_ffn_shared_gate_w, L0_ffn_shared_up_w, L0_ffn_shared_down_w)
    return x

_drawn_inputs = setup_inputs


def setup_inputs(seed=0):
    import zlib

    import numpy as np

    out = dict(_drawn_inputs(seed))
    spreads = {'L0_cond_b_emb': (0.0, 0.1),
     'L0_cond_g_norm': (1.0, 0.2),
     'L0_cond_g_q': (1.0, 0.2),
     'L0_cond_g_k': (1.0, 0.2),
     'L0_ffn_norm_w': (1.0, 0.2)}
    factors = {}
    for name, (base, spread) in spreads.items():
        noise = np.random.default_rng([zlib.crc32(name.encode()), seed]).standard_normal(out[name].shape)
        drawn = base * np.exp(spread * noise) if base else spread * noise
        out[name] = jnp.asarray(drawn.astype(out[name].dtype))
    for name, factor in factors.items():
        out[name] = (out[name] * factor).astype(out[name].dtype)
    return out
```

```python
from contextlib import ExitStack

import concourse.bass as bass
from concourse import mybir

F32 = mybir.dt.float32
I32 = mybir.dt.int32
U32 = mybir.dt.uint32
ALU = mybir.AluOpType
ACT = mybir.ActivationFunctionType
AX_X = mybir.AxisListType.X

P = 128
NB, SEQ, D = 8, 256, 512
KC = D // P
HEADS, DH = 16, 32
TPB = SEQ // P
NT = NB * TPB
NTOK = NB * SEQ
HPG = P // DH
UNITS = TPB * HEADS // HPG
E, I, TOPK = 32, 256, 4
IC = I // P
CAP = 2 * NTOK * TOPK // E
CH = CAP // P
SH = NTOK // CAP
W1N, W2N = KC * 2 * I, IC * D
WN = W1N + W2N
WBUF = 3
EPS = 1e-6
SKIP = 1 << 20

BIG = [("k", 1, 0), ("op", -1, 1), ("q", 1, 0), ("v", 1, 0), ("k", 1, 1), ("op", 0, 0), ("q", 1, 1), ("v", 1, 1)]
SMALL = [
    [("oT", -1, 1, 0)],
    [("xT", 1, 1, 0), ("qT", 0, 1, 1)],
    [("rt", -1, 0, 1), ("nT", -1, 1, 0)],
    [("rt", -1, 1, 0)],
    [("oT", 0, 0, 0)],
    [("xT", 2, 0, 0), ("qT", 1, 0, 1)],
    [("nT", 0, 0, 0)],
    [("kT", 1, 0, 0), ("kT", 1, 1, 1)],
]
XS = {0: (1, 1), 4: (2, 0)}
KQ_ORDER = {("k", 0): 0, ("q", 0): 1, ("k", 1): 2, ("q", 1): 3}


def exists(b, off, first, last, before_last):
    if off == -1:
        return not first
    if off == 1:
        return not last
    if off == 2:
        return not (last or before_last)
    return True


def head_of(u, i):
    return 2 * (u % KC // 2) + i // 2, 2 * (u % 2) + i % 2


def wait(eng, sem, value):
    if isinstance(value, int) and value <= 0:
        return
    eng.wait_ge(sem, value)


def adaln_moe_kernel(nc, x, cond, W_emb, b_emb, g_norm, W_qkv, g_q, g_k, W_out, norm_w, gate_w, w13, w2,
                     w_gate, w_up, w_down, out):
    xn_d = nc.dram_tensor("xn_scratch", [NTOK, D], F32).ap()
    tab_d = nc.dram_tensor("slot_table", [E * CAP, 1], I32).ap()
    eo_d = nc.dram_tensor("expert_rows", [NTOK + E * CAP, D], F32).ap()

    x_t = x.rearrange("b (t p) d -> (b t) p d", p=P)
    out_t = out.rearrange("b (t p) d -> (b t) p d", p=P)
    xn_t = xn_d.rearrange("(t p) d -> t p d", p=P)
    eo_t = eo_d.rearrange("(t p) d -> t p d", p=P)

    with ExitStack() as ctx:
        def sb(name, shape, dt=F32):
            return ctx.enter_context(nc.sbuf_tensor(name, shape, dt))

        def pb(name, shape):
            return ctx.enter_context(nc.psum_tensor(name, shape, F32))

        def sem(name):
            return ctx.enter_context(nc.semaphore(name))

        x_all = sb("x_all", [P, NT, D])
        wqkv = sb("wqkv", [P, KC, 3 * D])
        wout = sb("wout", [P, KC, D])
        wbuf = sb("wbuf", [P, WBUF, WN])
        wemb = wbuf[:, :, :].rearrange("p a n -> p (a n)")[:, 0:KC * 2 * D].rearrange("p (k n) -> p k n", k=KC)
        emb = sb("emb", [NB, D])
        embT = sb("embT", [P, KC, NB])
        bemb = sb("bemb", [P, 2 * KC])
        gnorm = sb("gnorm", [P, KC])
        ss_emb = sb("ss_emb", [P, 2 * KC, NB])
        scale_m = sb("scale_m", [P, NB, KC])
        shift_m = sb("shift_m", [P, NB, KC])
        gqk = sb("gqk", [P, 3])
        nw = sb("nw", [P, D])
        gate_rows = sb("gate_rows", [E, D])
        gateT = sb("gateT", [P, KC, E])
        ident = sb("ident", [P, P])
        tri = sb("tri", [P, P])
        ones = sb("ones", [P, P])
        iota_e = sb("iota_e", [P, E])
        tok_id = sb("tok_id", [P, NT], I32)
        zeros_f = sb("zeros_f", [P, 2, D])
        zeros_i = sb("zeros_i", [P, P], I32)
        xsq = sb("xsq", [P, D])
        ssx = sb("ssx", [P, 2])
        rsx = sb("rsx", [P, 2])
        xs = sb("xs", [P, 2, D])
        xmT = sb("xmT", [P, 2, KC, P])
        sq = sb("sq", [P, D])
        ss = sb("ss", [P, HEADS])
        rs = sb("rs", [P, HEADS])
        eps_x, eps_h, eps_kq = sb("eps_x", [P, 1]), sb("eps_h", [P, 1]), sb("eps_kq", [P, HEADS])
        minus_half = sb("minus_half", [P, HEADS])
        qk_hat = sb("qk_hat", [P, 4, D])
        qT = sb("qT", [P, 2, KC, P])
        kT = sb("kT", [P, KC, 2, P])
        v_sb = sb("v_sb", [P, 2, 2 * D])
        nmax = sb("nmax", [P, 2, HPG])
        sums = sb("sums", [P, 2, HPG])
        rsums = sb("rsums", [P, 2, HPG])
        probs = sb("probs", [P, 2, HPG, SEQ])
        probsT = sb("probsT", [P, HPG, 2, P])
        o_sb = sb("o_sb", [P, 2, D])
        oT = sb("oT", [P, KC, P])
        hsq = sb("hsq", [P, D])
        ssh = sb("ssh", [P, 2])
        rsh = sb("rsh", [P, 2])
        xn = sb("xn", [P, 2, D])
        xnT = sb("xnT", [P, KC, P])
        lg = sb("lg", [P, NT, E])
        top8 = sb("top8", [P, NT, 8])
        idx8 = sb("idx8", [P, NT, 8], U32)
        idxf = sb("idxf", [P, NT, TOPK])
        wexp = sb("wexp", [P, NT, TOPK])
        wsum = sb("wsum", [P, NT])
        wrec = sb("wrec", [P, NT])
        w_all = sb("w_all", [P, NT, TOPK])
        onehot = probs[:, :, :, :].rearrange("p a i n -> p (a i n)").rearrange("p (t k e) -> p t k e", t=NT, k=TOPK)
        mask = sb("mask", [P, NT, E])
        carry = sb("carry", [P, NT + 1, E])
        pos = sb("pos", [P, NT, E])
        posk = sb("posk", [P, NT, TOPK])
        over = sb("over", [P, NT, TOPK])
        slot = sb("slot", [P, NT, TOPK])
        slot_i = sb("slot_i", [P, NT, TOPK], I32)
        scat = sb("scat", [P, NT, TOPK])
        scat_i = sb("scat_i", [P, NT, TOPK], I32)
        cnt = sb("cnt", [1, 2, 3, E])
        meta_f = sb("meta_f", [1, E, 4])
        meta = sb("meta", [1, E, 4], I32)
        tab_i = sb("tab_i", [P, P], I32)
        tab_f = sb("tab_f", [P, P])
        idx_all = sb("idx_all", [P, P], I32)
        idx_cur = sb("idx_cur", [P, CH], I32)
        scat_cur = sb("scat_cur", [P, 4, TOPK], I32)
        tok_cur = sb("tok_cur", [P, 4], I32)
        xrows = wqkv[:, :, 0:D]
        xTs = sb("xTs", [P, KC, P])
        sg = sb("sg", [P, I])
        hid = sb("hid", [P, I])
        hidT = sb("hidT", [P, IC, P])
        orow = sb("orow", [P, D])
        rows_c = wbuf[:, :, :].rearrange("p a n -> p (a n)")[:, 0:2 * 4 * D].rearrange("p (a k n) -> p a k n", a=2, k=4)
        rows_s = xrows[:, 0:2, :]
        slot_cur = sb("slot_cur", [P, 2, TOPK], I32)

        psS = pb("psS", [P, 2, 2, 2, SEQ])
        psP = pb("psP", [P, 2, KC, P])
        psO = pb("psO", [P, D])
        psF = pb("psF", [P, D])
        psG1 = psS[:, 0, 0, :, :].rearrange("p a n -> p (a n)")
        psXT = psS[:, 0, 1, :, :].rearrange("p a (c n) -> p (a c) n", n=P)
        psG2 = psS[:, 1, 0, :, :].rearrange("p a n -> p (a n)")
        psHT = psS[:, 1, 1, 0, :].rearrange("p (c n) -> p c n", n=P)

        x_loaded = sem("x_loaded")
        emb_loaded, wemb_loaded, wqkv_loaded, wout_loaded = (sem(f"{n}_loaded") for n in ("emb", "wemb", "wqkv", "wout"))
        small_loaded, gate_loaded = sem("small_loaded"), sem("gate_loaded")
        zeros_set, ident_raw, consts_ready, table_cleared = sem("zeros_set"), sem("ident_raw"), sem("consts_ready"), sem("table_cleared")
        embT_ps, embT_sb, ss_ps, ss_added, mod_step, mod_ready = (sem(n) for n in ("embT_ps", "embT_sb", "ss_ps", "ss_added", "mod_step", "mod_ready"))
        gateT_ps, gateT_sb, wout_ready, gqk_step, nw_ready = (sem(n) for n in ("gateT_ps", "gateT_sb", "wout_ready", "gqk_step", "nw_ready"))
        xsq_done, rsx_done, xs_ready, xT_ps, xT_sb = (sem(n) for n in ("xsq_done", "rsx_done", "xs_ready", "xT_ps", "xT_sb"))
        kq_ps, kq_sq, kq_ss, kq_rs, kq_hat, v_ps, v_ready = (sem(n) for n in ("kq_ps", "kq_sq", "kq_ss", "kq_rs", "kq_hat", "v_ps", "v_ready"))
        qT_ps, qT_ready, kT_ps, kT_ready = (sem(n) for n in ("qT_ps", "qT_ready", "kT_ps", "kT_ready"))
        scores_ready, max_ready, exp_done, sums_read = (sem(n) for n in ("scores_ready", "max_ready", "exp_done", "sums_read"))
        pT_ps, pT_sb0, pT_sb1, pv_done, o_ready = (sem(n) for n in ("pT_ps", "pT_sb0", "pT_sb1", "pv_done", "o_ready"))
        oT_ps, oT_ready, h_ps, hsq_done, rsh_done, xn_ready, h_added = (sem(n) for n in ("oT_ps", "oT_ready", "h_ps", "hsq_done", "rsh_done", "xn_ready", "h_added"))
        nT_ps, nT_ready, rt_ps, lg_ready, xn_stored = (sem(n) for n in ("nT_ps", "nT_ready", "rt_ps", "lg_ready", "xn_stored"))
        top_done, rt_step, wexp_in, wexp_done, mask_ready, pos_ps, w_ready = (sem(n) for n in ("top_done", "rt_step", "wexp_in", "wexp_done", "mask_ready", "pos_ps", "w_ready"))
        scat_ready, meta_ready, scattered, tab_loaded, tabf_ready, tabT_ps, idx_ready = (sem(n) for n in ("scat_ready", "meta_ready", "scattered", "tab_loaded", "tabf_ready", "tabT_ps", "idx_ready"))
        rows_in = [sem(f"rows_in{c}") for c in range(CH)]
        idx_copied, w_loaded = sem("idx_copied"), sem("w_loaded")
        xt_done, xTs_ready, g1_done, sg_ready, hid_ready, ht_done, hidT_ready, g2_done, orow_ready, orow_stored, orow_free = (
            sem(n) for n in ("xt_done", "xTs_ready", "g1_done", "sg_ready", "hid_ready", "ht_done", "hidT_ready", "g2_done", "orow_ready", "orow_stored", "orow_free"))
        slot_copied, acc_step, acc_done = sem("slot_copied"), sem("acc_step"), sem("acc_done")
        rows_c_in = [sem(f"rows_c_in{a}") for a in range(2)]
        rows_s_in = [sem(f"rows_s_in{a}") for a in range(2)]
        out_stored = sem("out_stored")
        eo_zeroed, pool_passed, xn_free = sem("eo_zeroed"), sem("pool_passed"), sem("xn_free")
        x_eps, h_eps, kq_eps = sem("x_eps"), sem("h_eps"), sem("kq_eps")
        ws_loaded, eo_complete, gqk_ready, scat_copied, slots_ready, cnt_step, w_step = (
            sem(n) for n in ("ws_loaded", "eo_complete", "gqk_ready", "scat_copied", "slots_ready", "cnt_step", "w_step"))

        block = ctx.enter_context(nc.Block())

        def batches(eng, body):
            body(0, True, False, False)
            with eng.Fori(1, NB - 2) as b:
                body(b, False, False, False)
            body(NB - 2, False, False, True)
            body(NB - 1, False, True, False)

        def experts(eng, body):
            body(0, None, False)
            with eng.Fori(1, SH) as j:
                body(j, None, False)
            with eng.Fori(0, E - 1) as e:
                body(e + SH, e, False)
            body(E - 1 + SH, E - 1, True)

        def steps_of(eng, j, e):
            if e is None:
                return j * CH - 1, j * CH, CH
            before = eng.value_load(meta[0:1, e, 0:1], min_val=SH * CH - 1, max_val=(SH + E) * CH)
            return before, before + 1, eng.value_load(meta[0:1, e, 1:2], min_val=2, max_val=CH)

        def n_kq(b):
            return 4 * b

        @block.sync
        def _(sp):
            sp.dma_start(x_all[:, 0:TPB, :], x_t[0:TPB].rearrange("t p d -> p t d")).then_inc(x_loaded, 16)
            sp.dma_start(emb[:, :], cond).then_inc(emb_loaded, 16)
            sp.dma_start(wemb, W_emb.rearrange("(k p) n -> p k n", p=P)).then_inc(wemb_loaded, 16)
            sp.dma_start(wqkv[:, :, :], W_qkv.rearrange("(k p) n -> p k n", p=P)).then_inc(wqkv_loaded, 16)
            sp.dma_start(wout[:, :, :], W_out.rearrange("(k p) n -> p k n", p=P)).then_inc(wout_loaded, 16)
            for b in range(1, NB):
                sp.wait_ge(x_loaded, 16 * b)
                sp.dma_start(x_all[:, TPB * b:TPB * (b + 1), :],
                             x_t[TPB * b:TPB * (b + 1)].rearrange("t p d -> p t d")).then_inc(x_loaded, 16)

            def load_expert(e):
                dst = wbuf[:, (e + 1) % WBUF, :]
                sp.dma_start(dst[:, 0:W1N].rearrange("p (k n) -> p k n", k=KC),
                             w13[e].rearrange("(k p) n -> p k n", p=P)).then_inc(w_loaded, 16)
                sp.dma_start(dst[:, W1N:WN].rearrange("p (k n) -> p k n", k=IC),
                             w2[e].rearrange("(k p) n -> p k n", p=P)).then_inc(w_loaded, 16)

            sp.wait_ge(ss_ps, 1)
            w1_shared = wbuf[:, 0, 0:W1N].rearrange("p (k n) -> p k n", k=KC)
            sp.dma_start(w1_shared[:, :, 0:I], w_gate.rearrange("(k p) n -> p k n", p=P)).then_inc(ws_loaded, 16)
            sp.dma_start(w1_shared[:, :, I:2 * I], w_up.rearrange("(k p) n -> p k n", p=P)).then_inc(ws_loaded, 16)
            sp.dma_start(wbuf[:, 0, W1N:WN].rearrange("p (k n) -> p k n", k=IC),
                         w_down.rearrange("(k p) n -> p k n", p=P)).then_inc(ws_loaded, 16)
            load_expert(0)
            sp.wait_ge(w_loaded, 32)
            load_expert(1)

            sp.wait_ge(zeros_set, 2)
            eo_cap = eo_d[NTOK:NTOK + E * CAP, :].rearrange("(e c p) d -> e p c d", c=CH, p=P)
            with sp.Fori(0, E) as e:
                sp.dma_start(eo_cap[e, :, 2:CH, :], zeros_f[:, :, :]).then_inc(eo_zeroed, 16)
            sp.wait_ge(eo_zeroed, 16 * E)

            with sp.Fori(0, NB) as b:
                for t in range(TPB):
                    sp.wait_ge(xn_ready, TPB * b + t + 1)
                    sp.dma_start(xn_t[TPB * b + t], xn[:, t, :]).then_inc(xn_stored, 16)
                    sp.wait_ge(xn_stored, 16 * (TPB * b + t + 1))
                    sp.sem_inc(xn_free, 1)

            def store(step, row_tile):
                sp.wait_ge(orow_ready, step + 1)
                sp.dma_start(eo_t[row_tile], orow[:, :]).then_inc(orow_stored, 16)
                sp.wait_ge(orow_stored, 16 * (step + 1))
                sp.sem_inc(orow_free, 1)

            def body(j, e, fetch):
                before, s, n = steps_of(sp, j, e)
                if e is None:
                    for c in range(CH):
                        store(s + c, j * CH + c)
                    return
                if fetch:
                    sp.wait_ge(g2_done, s)
                    sp.wait_ge(w_loaded, 32 * (e + 2))
                    load_expert(e + 2)
                store(s, j * CH)
                store(s + 1, j * CH + 1)
                with sp.If(n > 2):
                    store(s + 2, j * CH + 2)
                    with sp.If(n > 3):
                        store(s + 3, j * CH + 3)
                    with sp.Else():
                        pass
                with sp.Else():
                    pass

            body(0, None, False)
            with sp.Fori(1, SH) as j:
                body(j, None, False)
            sp.wait_ge(meta_ready, 1)
            with sp.Fori(0, E - 2) as e:
                body(e + SH, e, True)
            for e in (E - 2, E - 1):
                body(e + SH, e, False)
            sp.sem_inc(eo_complete, 1)

            def load_shared(tile, a):
                sp.dma_start(rows_s[:, a, :], eo_t[tile]).then_inc(rows_s_in[a], 16)

            for a in range(2):
                load_shared(a, a)

            def finish(i, more):
                for a in range(2):
                    sp.wait_ge(acc_done, 2 * i + a + 1)
                    sp.dma_start(out_t[2 * i + a], x_all[:, 2 * i + a, :]).then_inc(out_stored, 16)
                    if more:
                        load_shared(2 * i + 2 + a, a)

            with sp.Fori(0, NT // 2 - 1) as i:
                finish(i, True)
            finish(NT // 2 - 1, False)
            sp.wait_ge(out_stored, 16 * NT)

        @block.gpsimd
        def _(pool):
            def pool_wait(sem, value):
                wait(pool, sem, value)
                if not isinstance(value, int):
                    pool.sem_inc(pool_passed, 1)

            pool.memset(zeros_i[:, :], 0).then_inc(zeros_set, 1)
            pool.memset(zeros_f[:, :, :], 0.0).then_inc(zeros_set, 1)
            pool.memset(ident[:, :], 0.0).then_inc(ident_raw, 1)
            pool.memset(ones[:, :], 1.0).then_inc(ident_raw, 1)
            pool.iota(iota_e[:, :], [[1, E]], base=0, channel_multiplier=0,
                      allow_small_or_imprecise_dtypes=True).then_inc(ident_raw, 1)
            pool.iota(tok_id[:, :], [[P, NT]], base=0, channel_multiplier=1).then_inc(ident_raw, 1)
            pool.memset(minus_half[:, :], -0.5).then_inc(ident_raw, 1)
            pool_wait(ident_raw, 5)
            pool.affine_select(out=ident[:, :], in_=ident[:, :], compare_op=ALU.not_equal, fill=1.0, base=0,
                               pattern=[[-1, P]], channel_multiplier=1).then_inc(consts_ready, 1)
            pool.affine_select(out=tri[:, :], in_=ones[:, :], compare_op=ALU.is_ge, fill=0.0, base=-1,
                               pattern=[[1, P]], channel_multiplier=-1).then_inc(consts_ready, 1)
            pool.dma_start(bemb[:, :], b_emb.rearrange("(k p) -> p k", p=P),
                           allow_slow_non_contiguous=True).then_inc(small_loaded, 16)
            pool.dma_start(gnorm[:, :], g_norm.rearrange("(k p) -> p k", p=P),
                           allow_slow_non_contiguous=True).then_inc(small_loaded, 16)
            for i in range(HPG):
                pool.dma_start(gqk[i * DH:(i + 1) * DH, 0:1], g_q.rearrange("(p a) -> p a", a=1)).then_inc(small_loaded, 16)
                pool.dma_start(gqk[i * DH:(i + 1) * DH, 1:2], g_k.rearrange("(p a) -> p a", a=1)).then_inc(small_loaded, 16)
            pool.dma_start(nw[:, :], norm_w.rearrange("(a d) -> a d", a=1).to_broadcast([P, D])).then_inc(small_loaded, 16)
            pool.dma_start(gate_rows[:, :], gate_w).then_inc(gate_loaded, 16)
            pool_wait(zeros_set, 2)
            pool.dma_start(tab_d.rearrange("(p n) a -> p (n a)", p=P), zeros_i[:, :]).then_inc(table_cleared, 16)

            def rsqrt(out, squares, width, plus_eps, eps_added, done, n):
                pool_wait(done, n)
                pool.tensor_scalar(plus_eps[:, :], squares, width * EPS, None, ALU.add).then_inc(eps_added, 1)
                pool_wait(eps_added, n + 1)
                pool.tensor_tensor(out, plus_eps[:, :], minus_half[:, 0:plus_eps.shape[1]], ALU.pow).then_inc(done, 1)

            def input_rs(b, t):
                tile = TPB * b + t
                pool_wait(xsq_done, tile + 1)
                pool_wait(xs_ready, tile - 1)
                rsqrt(rsx[:, t:t + 1], ssx[:, t:t + 1], D, eps_x, x_eps, rsx_done, tile)

            def product_rs(kind, b, t):
                tile = TPB * b + t
                if kind == "op":
                    pool_wait(hsq_done, tile + 1)
                    pool_wait(xn_ready, tile - 1)
                    rsqrt(rsh[:, t:t + 1], ssh[:, t:t + 1], D, eps_h, h_eps, rsh_done, tile)
                elif kind != "v":
                    n = n_kq(b) + KQ_ORDER[kind, t]
                    pool_wait(kq_ss, n + 1)
                    pool_wait(kq_hat, n)
                    rsqrt(rs[:, :], ss[:, :], DH, eps_kq, kq_eps, kq_rs, n)

            input_rs(0, 0)
            input_rs(0, 1)
            input_rs(1, 0)
            for t in range(TPB):
                for kind in "kqv":
                    product_rs(kind, 0, t)

            def body(b, first, last, before_last):
                for u in range(UNITS):
                    kind, off, t = BIG[u]
                    if exists(b, off, first, last, before_last):
                        product_rs(kind, b + off, t)
                    if u in XS and exists(b, XS[u][0], first, last, before_last):
                        input_rs(b + XS[u][0], XS[u][1])

            batches(pool, body)
            product_rs("op", NB - 1, 1)

            def shared_rows(j):
                for c in range(CH):
                    if not (isinstance(j, int) and j == 0):
                        pool_wait(xt_done, (j - 1) * CH + c + 1)
                    pool.dma_start(xrows[:, c, :], xn_t[j * CH + c]).then_inc(rows_in[c], 16)

            pool_wait(xn_stored, 16 * NT)
            shared_rows(0)
            shared_rows(1)
            pool_wait(scat_ready, 1)
            pool_wait(table_cleared, 16)
            GROUP = 4
            with pool.Fori(0, NT // GROUP) as i:
                pool.tensor_copy(scat_cur[:, :, :], scat_i[:, bass.ds(i * GROUP, GROUP), :]).then_inc(scat_copied, 1)
                pool.tensor_copy(tok_cur[:, :], tok_id[:, bass.ds(i * GROUP, GROUP)]).then_inc(scat_copied, 1)
                pool_wait(scat_copied, 2 * i + 2)
                for g in range(GROUP):
                    for k in range(TOPK):
                        pool.indirect_dma_start(
                            out=tab_d, out_offset=bass.IndirectOffsetOnAxis(ap=scat_cur[:, g, k:k + 1], axis=0),
                            in_=tok_cur[:, g:g + 1], in_offset=None,
                            bounds_check=E * CAP - 1, oob_is_err=False).then_inc(scattered, 16)
                pool_wait(scattered, 16 * GROUP * TOPK * (i + 1))
            pool.dma_start(tab_i[:, :], tab_d.rearrange("(p n) a -> p (n a)", p=P)).then_inc(tab_loaded, 16)
            shared_rows(2)
            shared_rows(3)

            def gather(e):
                pool_wait(rows_in[CH - 1], 16 * (SH + e))
                pool.tensor_copy(idx_cur[:, :], idx_all[:, bass.ds(e * CH, CH)]).then_inc(idx_copied, 1)
                pool_wait(idx_copied, e + 1)
                if isinstance(e, int) and e == 0:
                    prev = (SH - 1) * CH - 1
                else:
                    prev = pool.value_load(meta[0:1, e - 1, 0:1], min_val=SH * CH - 1, max_val=(SH + E) * CH)
                before = pool.value_load(meta[0:1, e, 0:1], min_val=SH * CH - 1, max_val=(SH + E) * CH)
                for c in range(CH):
                    pool_wait(xt_done, (prev + c + 2) if c < 2 else before + 1)
                    pool.indirect_dma_start(
                        out=xrows[:, c, :], out_offset=None, in_=xn_d,
                        in_offset=bass.IndirectOffsetOnAxis(ap=idx_cur[:, c:c + 1], axis=0)).then_inc(rows_in[c], 16)

            pool_wait(idx_ready, 1)
            pool_wait(meta_ready, 1)
            gather(0)
            with pool.Fori(1, E) as e:
                gather(e)

            pool_wait(eo_complete, 1)

            def gather_slots(i, a, tile):
                if i is not None:
                    pool_wait(acc_done, 2 * i + a + 1)
                pool.tensor_copy(slot_cur[:, a, :], slot_i[:, tile, :]).then_inc(slot_copied, 1)
                pool_wait(slot_copied, tile + 1)
                for k in range(TOPK):
                    pool.indirect_dma_start(
                        out=rows_c[:, a, k, :], out_offset=None, in_=eo_d,
                        in_offset=bass.IndirectOffsetOnAxis(ap=slot_cur[:, a, k:k + 1], axis=0)).then_inc(rows_c_in[a], 16)

            gather_slots(None, 0, 0)
            gather_slots(None, 1, 1)
            with pool.Fori(0, NT // 2 - 1) as i:
                for a in range(2):
                    gather_slots(i, a, 2 * i + 2 + a)

        @block.tensor
        def _(pe):
            def transposes(dst, src, k=KC, rows=P, width=P):
                for i in range(k):
                    last = pe.transpose(dst[:, i, 0:rows], src[:, i * width:(i + 1) * width], ident[0:rows, 0:rows])
                return last

            pe.wait_ge(consts_ready, 2)
            pe.wait_ge(emb_loaded, 16)
            transposes(psP[:, 0, :, :], emb[:, :], rows=NB).then_inc(embT_ps, 1)
            pe.wait_ge(gate_loaded, 16)
            transposes(psP[:, 1, :, :], gate_rows[:, :], rows=E).then_inc(gateT_ps, 1)
            pe.wait_ge(embT_sb, 1)
            pe.wait_ge(wemb_loaded, 16)
            for j in range(2 * KC):
                for k in range(KC):
                    mm = pe.matmul(psF[:, j * NB:(j + 1) * NB], wemb[:, k, j * P:(j + 1) * P], embT[:, k, :],
                                   start=(k == 0), stop=(k == KC - 1))
            mm.then_inc(ss_ps, 1)

            def scores(b, u):
                t, n = u // KC, UNITS * b + u
                wait(pe, qT_ready, TPB * b + t + 1)
                wait(pe, kT_ready, TPB * (b + 1))
                wait(pe, exp_done, n - 1)
                for i in range(HPG):
                    g, row = head_of(u, i)
                    rows = slice(row * DH, (row + 1) * DH)
                    mm = pe.matmul(psS[:, u % 2, i % 2, i // 2, :], qT[rows, t, g, :],
                                   kT[rows, g, :, :].rearrange("p t n -> p (t n)"), start=True, stop=True)
                mm.then_inc(scores_ready, 1)

            def small(task, b, u, in_loop=True):
                kind, off, t, bank = task
                tile = TPB * (b + off) + t
                n = UNITS * b + u
                if in_loop and bank is not None:
                    wait(pe, pT_sb0 if bank == 0 else pT_sb1, n + 1)
                if kind == "xT":
                    wait(pe, xs_ready, tile + 1)
                    transposes(psP[:, bank, :, :], xs[:, t, :]).then_inc(xT_ps, 1)
                if kind == "oT":
                    wait(pe, o_ready, KC * (tile + 1))
                    transposes(psP[:, bank, :, :], o_sb[:, t, :]).then_inc(oT_ps, 1)
                if kind == "nT":
                    wait(pe, xn_ready, tile + 1)
                    transposes(psP[:, bank, :, :], xn[:, t, :]).then_inc(nT_ps, 1)
                if kind == "qT":
                    wait(pe, kq_hat, n_kq(b + off) + KQ_ORDER["q", t] + 1)
                    transposes(psP[:, bank, :, :], qk_hat[:, KQ_ORDER["q", t], :]).then_inc(qT_ps, 1)
                if kind == "kT":
                    wait(pe, kq_hat, n_kq(b + off) + KQ_ORDER["k", t] + 1)
                    transposes(psP[:, bank, :, :], qk_hat[:, KQ_ORDER["k", t], :]).then_inc(kT_ps, 1)
                if kind == "rt":
                    wait(pe, nT_ready, tile + 1)
                    wait(pe, lg_ready, tile)
                    for k in range(KC):
                        mm = pe.matmul(psP[:, bank, 0, 0:E], xnT[:, k, :], gateT[:, k, :], start=(k == 0), stop=(k == KC - 1))
                    mm.then_inc(rt_ps, 1)

            def product(lhsT, rhs):
                for k in range(KC):
                    mm = pe.matmul(psF[:, :], lhsT[:, k, :], rhs[:, k, :], start=(k == 0), stop=(k == KC - 1))
                return mm

            def big(task, b, psF_free):
                kind, off, t = task
                tile = TPB * (b + off) + t
                for s, v in psF_free:
                    wait(pe, s, v)
                if kind == "op":
                    wait(pe, oT_ready, tile + 1)
                    product(oT, wout).then_inc(h_ps, 1)
                else:
                    wait(pe, xT_sb, tile + 1)
                    j = "qkv".index(kind)
                    product(xmT[:, t, :, :], wqkv[:, :, j * D:(j + 1) * D]).then_inc(v_ps if kind == "v" else kq_ps, 1)

            def psF_copied(b, u, first, last):
                while True:
                    u -= 1
                    if u < 0:
                        return [(v_ready, TPB * (b + 1))]
                    kind, off, t = BIG[u]
                    if not exists(b, off, first, last, False):
                        continue
                    if kind == "op":
                        return [(h_added, TPB * (b + off) + t + 1)]
                    if kind == "v":
                        return [(v_ready, TPB * (b + off) + t + 1)]
                    return [(kq_hat, n_kq(b + off) + KQ_ORDER[kind, t] + 1)]

            pe.wait_ge(ss_added, 1)
            pe.wait_ge(gateT_sb, 1)
            for t in range(TPB):
                small(("xT", 0, t, t), 0, 0, in_loop=False)
            pe.wait_ge(wqkv_loaded, 16)
            before = []
            for t in range(TPB):
                for kind in "kqv":
                    big((kind, 0, t), 0, before)
                    before = [(v_ready, t + 1)] if kind == "v" else [(kq_hat, KQ_ORDER[kind, t] + 1)]
                if t == 0:
                    pe.wait_ge(xT_sb, 2)
                    small(("xT", 1, 0, 0), 0, 0, in_loop=False)
                    small(("qT", 0, 0, 1), 0, 0, in_loop=False)
            pe.wait_ge(xT_sb, 3)
            pe.wait_ge(qT_ready, 1)
            small(("kT", 0, 0, 0), 0, 0, in_loop=False)
            small(("kT", 0, 1, 1), 0, 0, in_loop=False)
            pe.wait_ge(wout_ready, 1)

            def body(b, first, last, before_last):
                def transposed_probs(u):
                    n = UNITS * b + u
                    wait(pe, exp_done, n + 1)
                    if u:
                        for kind, off, t, bank in SMALL[u - 1]:
                            if bank is not None and exists(b, off, first, last, before_last):
                                done = {"oT": oT_ready, "xT": xT_sb, "nT": nT_ready, "qT": qT_ready, "kT": kT_ready, "rt": lg_ready}[kind]
                                wait(pe, done, TPB * (b + off) + t + 1)
                    for i in range(HPG):
                        for c in range(TPB):
                            tr = pe.transpose(psP[:, i // 2, (i % 2) * 2 + c, :], probs[:, u % 2, i, c * P:(c + 1) * P], ident[:, :])
                    tr.then_inc(pT_ps, 1)

                def product_of(u):
                    if exists(b, BIG[u][1], first, last, before_last):
                        big(BIG[u], b, psF_copied(b, u, first, last))

                scores(b, 0)
                for u in range(UNITS):
                    n = UNITS * b + u
                    if u + 1 < UNITS:
                        scores(b, u + 1)
                    if u == 0:
                        product_of(u)
                        transposed_probs(u)
                    else:
                        transposed_probs(u)
                        product_of(u)
                    for task in SMALL[u]:
                        if exists(b, task[1], first, last, before_last):
                            small(task, b, u)
                    wait(pe, o_ready, n)
                    wait(pe, pT_sb0, n + 1)
                    wait(pe, pT_sb1, n + 1)
                    wait(pe, v_ready, TPB * (b + 1))
                    for i in range(HPG):
                        g, row = head_of(u, i)
                        h = g * HPG + row
                        at = i * DH
                        for c in range(TPB):
                            mm = pe.matmul(psO[:, at:at + DH], probsT[:, i, c, :],
                                           v_sb[:, b % 2, c * D + h * DH:c * D + (h + 1) * DH],
                                           start=(c == 0), stop=(c == TPB - 1))
                    mm.then_inc(pv_done, 1)

            batches(pe, body)
            small(("oT", -1, 1, 0), NB, 0, in_loop=False)
            big(("op", -1, 1), NB, [(h_added, NT - 1)])
            small(("rt", -1, 0, 1), NB, 0, in_loop=False)
            small(("nT", -1, 1, 0), NB, 0, in_loop=False)
            small(("rt", -1, 1, 0), NB, 0, in_loop=False)

            def step_gate_up(k, w):
                wait(pe, xTs_ready, k + 1)
                for c in range(KC):
                    mm = pe.matmul(psG1, xTs[:, c, :], w[:, c * 2 * I:(c + 1) * 2 * I], start=(c == 0), stop=(c == KC - 1))
                mm.then_inc(g1_done, 1)

            def step_rows(c, count):
                wait(pe, rows_in[c], 16 * count)
                transposes(psXT, xrows[:, c, :]).then_inc(xt_done, 1)

            def step_down(k, w):
                if isinstance(k, int) and k < 0:
                    return
                wait(pe, hidT_ready, k + 1)
                wait(pe, orow_ready, k)
                for c in range(IC):
                    mm = pe.matmul(psG2, hidT[:, c, :], w[:, W1N + c * D:W1N + (c + 1) * D], start=(c == 0), stop=(c == IC - 1))
                mm.then_inc(g2_done, 1)

            def step_hidden(k):
                wait(pe, hid_ready, k + 1)
                transposes(psHT, hid[:, :], k=IC).then_inc(ht_done, 1)

            def expert(j, e, last):
                before, s, n = steps_of(pe, j, e)
                if e is None:
                    w = w_before = wbuf[:, 0, :]
                else:
                    w, w_before = wbuf[:, (e + 1) % WBUF, :], wbuf[:, e % WBUF, :]
                    pe.wait_ge(w_loaded, 32 * (e + 1))
                    if isinstance(e, int) and e == 0:
                        w_before = wbuf[:, 0, :]

                def tail(c):
                    if not last:
                        step_rows(0, j + 2)
                    step_down(before + c, w if c else w_before)
                    step_hidden(s + c)

                def middle(c):
                    step_rows(c + 1, j + 1)
                    step_down(before + c, w if c else w_before)
                    step_hidden(s + c)

                step_gate_up(s, w)
                middle(0)
                step_gate_up(s + 1, w)
                if e is None:
                    middle(1)
                    step_gate_up(s + 2, w)
                    middle(2)
                    step_gate_up(s + 3, w)
                    tail(3)
                    return
                with pe.If(n > 2):
                    middle(1)
                    step_gate_up(s + 2, w)
                    with pe.If(n > 3):
                        middle(2)
                        step_gate_up(s + 3, w)
                        tail(3)
                    with pe.Else():
                        tail(2)
                with pe.Else():
                    tail(1)
                if last:
                    step_down(before + n, w)

            step_rows(0, 1)
            pe.wait_ge(ws_loaded, 48)
            expert(0, None, False)
            pe.wait_ge(mask_ready, 1)
            pe.matmul(psF[:, :], tri[:, :], mask[:, :, :].rearrange("p t e -> p (t e)"), start=True, stop=True)
            pe.matmul(psO[:, :], ones[:, :], mask[:, :, :].rearrange("p t e -> p (t e)"), start=True, stop=True).then_inc(pos_ps, 1)
            with pe.Fori(1, SH - 1) as j:
                expert(j, None, False)
            expert(SH - 1, None, True)
            pe.wait_ge(tabf_ready, 1)
            pe.transpose(psP[:, 0, 0, :], tab_f[:, :], ident[:, :]).then_inc(tabT_ps, 1)
            pe.wait_ge(meta_ready, 1)
            step_rows(0, SH + 1)
            with pe.Fori(0, E - 1) as e:
                expert(e + SH, e, False)
            expert(E - 1 + SH, E - 1, True)

        @block.scalar
        def _(act):
            def input_square(b, t):
                tile = TPB * b + t
                wait(act, x_loaded, 16 * (b + 1))
                wait(act, rsx_done, tile - 1)
                wait(act, xsq_done, tile)
                act.activation(xsq[:, :], x_all[:, tile, :], ACT.Square, accum_out=ssx[:, t:t + 1]).then_inc(xsq_done, 1)

            def product_read(kind, b, t):
                tile = TPB * b + t
                if kind == "v":
                    wait(act, v_ps, tile + 1)
                    act.activation(v_sb[:, b % 2, t * D:(t + 1) * D], psF[:, :], ACT.Copy).then_inc(v_ready, 1)
                elif kind == "op":
                    wait(act, h_ps, tile + 1)
                    wait(act, rsh_done, tile - 1)
                    wait(act, hsq_done, tile)
                    act.activation(hsq[:, :], psF[:, :], ACT.Square, accum_out=ssh[:, t:t + 1]).then_inc(hsq_done, 1)
                else:
                    n = n_kq(b) + KQ_ORDER[kind, t]
                    wait(act, kq_ps, n + 1)
                    wait(act, kq_ss, n)
                    act.activation(sq[:, :], psF[:, :], ACT.Square).then_inc(kq_sq, 1)

            def small_read(kind, b, t, bank):
                tile = TPB * b + t
                if kind == "oT":
                    wait(act, oT_ps, tile + 1)
                    act.activation(oT[:, :, :], psP[:, bank, :, :], ACT.Copy).then_inc(oT_ready, 1)
                if kind == "nT":
                    wait(act, nT_ps, tile + 1)
                    act.activation(xnT[:, :, :], psP[:, bank, :, :], ACT.Copy).then_inc(nT_ready, 1)
                if kind == "qT":
                    wait(act, qT_ps, tile + 1)
                    act.activation(qT[:, t, :, :], psP[:, bank, :, :], ACT.Copy, scale=gqk[:, 2:3]).then_inc(qT_ready, 1)
                if kind == "kT" and t == 1:
                    wait(act, kT_ps, tile + 1)
                    act.activation(kT[:, :, t, :], psP[:, bank, :, :], ACT.Copy).then_inc(kT_ready, 1)

            input_square(0, 0)
            input_square(0, 1)
            act.wait_ge(embT_ps, 1)
            act.activation(embT[:, :, :], psP[:, 0, :, 0:NB], ACT.Copy).then_inc(embT_sb, 1)
            act.wait_ge(gateT_ps, 1)
            act.activation(gateT[:, :, :], psP[:, 1, :, 0:E], ACT.Copy).then_inc(gateT_sb, 1)
            input_square(1, 0)
            act.wait_ge(gqk_ready, 1)
            for t in range(TPB):
                for kind in "kqv":
                    product_read(kind, 0, t)
                if t == 0:
                    small_read("qT", 0, 0, 1)
            small_read("kT", 0, 1, 1)

            def body(b, first, last, before_last):
                def exps(u):
                    n = UNITS * b + u
                    wait(act, max_ready, n + 1)
                    wait(act, pT_ps, n - 1)
                    wait(act, sums_read, n - 1)
                    for i in range(HPG):
                        ex = act.activation(probs[:, u % 2, i, :], psS[:, u % 2, i % 2, i // 2, :], ACT.Exp,
                                            bias=nmax[:, u % 2, i:i + 1], accum_out=sums[:, u % 2, i:i + 1])
                    ex.then_inc(exp_done, 1)

                def probs_read(u):
                    wait(act, pT_ps, UNITS * b + u + 1)
                    act.activation(probsT[:, 2:4, :, :].rearrange("p i c n -> p (i c) n"), psP[:, 1, :, :], ACT.Copy).then_inc(pT_sb1, 1)

                def product_task(u):
                    kind, off, t = BIG[u]
                    if exists(b, off, first, last, before_last):
                        product_read(kind, b + off, t)

                exps(0)
                for u in range(UNITS):
                    if u == 0:
                        exps(u + 1)
                        product_task(u)
                        probs_read(u)
                    else:
                        probs_read(u)
                        if u + 1 < UNITS:
                            exps(u + 1)
                        product_task(u)
                    for kind, off, t, bank in SMALL[u]:
                        if exists(b, off, first, last, before_last):
                            small_read(kind, b + off, t, bank)
                    if u in XS and exists(b, XS[u][0], first, last, before_last):
                        input_square(b + XS[u][0], XS[u][1])

            batches(act, body)
            small_read("oT", NB - 1, 1, 0)
            product_read("op", NB - 1, 1)
            small_read("nT", NB - 1, 1, 0)
            act.wait_ge(wexp_in, 1)
            act.activation(wexp[:, :, :], wexp[:, :, :], ACT.Exp).then_inc(wexp_done, 1)

            def rows_turned(k):
                act.wait_ge(xt_done, k + 1)
                act.activation(xTs[:, :, :], psXT, ACT.Copy).then_inc(xTs_ready, 1)

            def step(k, more=True):
                act.wait_ge(g1_done, k + 1)
                act.activation(sg[:, :], psG1[:, 0:I], ACT.Silu).then_inc(sg_ready, 1)
                if more:
                    rows_turned(k + 1)

            def expert(j, e, last):
                before, s, n = steps_of(act, j, e)
                step(s)
                if e is None:
                    for c in range(1, CH):
                        step(s + c, not (last and c == CH - 1))
                    return
                with act.If(n > 2):
                    step(s + 1)
                    with act.If(n > 3):
                        step(s + 2)
                        step(s + 3, not last)
                    with act.Else():
                        step(s + 2, not last)
                with act.Else():
                    step(s + 1, not last)

            rows_turned(0)
            expert(0, None, False)
            with act.Fori(1, SH - 1) as j:
                expert(j, None, False)
            expert(SH - 1, None, True)
            rows_turned(SH * CH)
            act.wait_ge(meta_ready, 1)
            with act.Fori(0, E - 1) as e:
                expert(e + SH, e, False)
            expert(E - 1 + SH, E - 1, True)

        @block.vector
        def _(dve):
            def input_scale(b, t):
                tile = TPB * b + t
                wait(dve, rsx_done, tile + 1)
                wait(dve, xT_ps, tile - 1)
                dve.tensor_scalar(xs[:, t, :], x_all[:, tile, :], rsx[:, t:t + 1], None, ALU.mult).then_inc(xs_ready, 1)

            def product_read(kind, b, t):
                tile = TPB * b + t
                if kind == "v":
                    return
                if kind == "op":
                    wait(dve, rsh_done, tile + 1)
                    wait(dve, xn_free, tile - 1)
                    wait(dve, nT_ps, tile - 1)
                    dve.scalar_tensor_tensor(out=xn[:, t, :], in0=psF[:, :], scalar=rsh[:, t:t + 1], in1=nw[:, :],
                                             op0=ALU.mult, op1=ALU.mult).then_inc(xn_ready, 1)
                    dve.tensor_tensor(x_all[:, tile, :], psF[:, :], x_all[:, tile, :], ALU.add).then_inc(h_added, 1)
                    return
                m = KQ_ORDER[kind, t]
                n = n_kq(b) + m
                wait(dve, kq_sq, n + 1)
                wait(dve, kq_rs, n)
                dve.reduce_sum(ss[:, :], sq[:, :].rearrange("p (h d) -> p h d", d=DH), AX_X).then_inc(kq_ss, 1)
                wait(dve, kq_rs, n + 1)
                wait(dve, qT_ps if kind == "q" else kT_ps, TPB * (b - 1) + t + 1)
                dve.tensor_tensor(qk_hat[:, m, :].rearrange("p (h d) -> p h d", d=DH), psF[:, :].rearrange("p (h d) -> p h d", d=DH),
                                  rs[:, :].unsqueeze(2).to_broadcast([P, HEADS, DH]), ALU.mult).then_inc(kq_hat, 1)

            def small_read(kind, b, t, bank):
                tile = TPB * b + t
                if kind == "xT":
                    wait(dve, xT_ps, tile + 1)
                    for k in range(KC):
                        ts = dve.tensor_scalar(xmT[:, t, k, :], psP[:, bank, k, :], scale_m[:, b, k:k + 1],
                                               shift_m[:, b, k:k + 1], ALU.mult, ALU.add)
                    ts.then_inc(xT_sb, 1)
                if kind == "kT" and t == 0:
                    wait(dve, kT_ps, tile + 1)
                    dve.tensor_copy(kT[:, :, t, :], psP[:, bank, :, :]).then_inc(kT_ready, 1)
                if kind == "rt":
                    wait(dve, rt_ps, tile + 1)
                    dve.tensor_copy(lg[:, tile, :], psP[:, bank, 0, 0:E]).then_inc(lg_ready, 1)

            input_scale(0, 0)
            input_scale(0, 1)
            dve.wait_ge(small_loaded, 16 * (3 + 2 * HPG))
            dve.wait_ge(ss_ps, 1)
            dve.tensor_tensor(ss_emb[:, :, :], psF[:, 0:2 * KC * NB].rearrange("p (j b) -> p j b", b=NB),
                              bemb[:, :].unsqueeze(2).to_broadcast([P, 2 * KC, NB]), ALU.add).then_inc(ss_added, 1)
            dve.tensor_scalar(gnorm[:, :], gnorm[:, :], float(D) ** 0.5, None, ALU.mult).then_inc(mod_step, 1)
            dve.wait_ge(ss_added, 1)
            dve.wait_ge(mod_step, 1)
            dve.scalar_tensor_tensor(out=scale_m[:, :, :], in0=ss_emb[:, 0:KC, :].rearrange("p k b -> p b k"), scalar=1.0,
                                     in1=gnorm[:, :].unsqueeze(1).to_broadcast([P, NB, KC]),
                                     op0=ALU.add, op1=ALU.mult).then_inc(mod_ready, 1)
            dve.tensor_copy(shift_m[:, :, :], ss_emb[:, KC:2 * KC, :].rearrange("p k b -> p b k")).then_inc(mod_ready, 1)
            dve.tensor_scalar(nw[:, :], nw[:, :], float(D) ** 0.5, None, ALU.mult).then_inc(nw_ready, 1)
            dve.scalar_tensor_tensor(out=gqk[:, 2:3], in0=gqk[:, 0:1], scalar=float(DH) ** 0.5, in1=gqk[:, 1:2],
                                     op0=ALU.mult, op1=ALU.mult).then_inc(gqk_ready, 1)
            dve.wait_ge(mod_ready, 2)
            dve.wait_ge(nw_ready, 1)
            small_read("xT", 0, 0, 0)
            small_read("xT", 0, 1, 1)
            input_scale(1, 0)
            for t in range(TPB):
                for kind in "kqv":
                    product_read(kind, 0, t)
                if t == 0:
                    small_read("xT", 1, 0, 0)
            dve.wait_ge(wout_loaded, 16)
            dve.wait_ge(consts_ready, 2)
            for k in range(KC):
                tt = dve.tensor_tensor(wout[:, k, k * P:(k + 1) * P], wout[:, k, k * P:(k + 1) * P], ident[:, :], ALU.add)
            tt.then_inc(wout_ready, 1)
            small_read("kT", 0, 0, 0)

            def body(b, first, last, before_last):
                def row_max(u):
                    n = UNITS * b + u
                    wait(dve, scores_ready, n + 1)
                    wait(dve, exp_done, n - 1)
                    dve.tensor_reduce(nmax[:, u % 2, :].rearrange("p (g r) -> p g r", g=2),
                                      psS[:, u % 2, :, :, :].rearrange("p r g n -> p g r n"), AX_X, ALU.max,
                                      negate=True).then_inc(max_ready, 1)

                def probs_read(u):
                    wait(dve, pT_ps, UNITS * b + u + 1)
                    dve.tensor_copy(probsT[:, 0:2, :, :].rearrange("p i c n -> p (i c) n"), psP[:, 0, :, :]).then_inc(pT_sb0, 1)

                def product_task(u):
                    kind, off, t = BIG[u]
                    if exists(b, off, first, last, before_last):
                        product_read(kind, b + off, t)

                row_max(0)
                for u in range(UNITS):
                    n = UNITS * b + u
                    if u + 1 < UNITS:
                        row_max(u + 1)
                    if u == 0:
                        product_task(u)
                        probs_read(u)
                    else:
                        probs_read(u)
                        product_task(u)
                    for kind, off, t, bank in SMALL[u]:
                        if exists(b, off, first, last, before_last):
                            small_read(kind, b + off, t, bank)
                    t = u // KC
                    tile = TPB * b + t
                    wait(dve, exp_done, n + 1)
                    dve.reciprocal(rsums[:, u % 2, :], sums[:, u % 2, :]).then_inc(sums_read, 1)
                    wait(dve, sums_read, n + 1)
                    wait(dve, pv_done, n + 1)
                    wait(dve, oT_ps, tile - 1)
                    g0, row0 = head_of(u, 0)
                    heads = o_sb[:, t, :].rearrange("p (g r d) -> p g r d", g=KC, d=DH)[:, g0:g0 + 2, row0:row0 + 2, :]
                    dve.tensor_tensor(heads, psO[:, 0:HPG * DH].rearrange("p (g r d) -> p g r d", g=2, d=DH),
                                      rsums[:, u % 2, :].rearrange("p (g r) -> p g r", g=2).unsqueeze(3).to_broadcast([P, 2, 2, DH]),
                                      ALU.mult).then_inc(o_ready, 1)
                    if u in XS and exists(b, XS[u][0], first, last, before_last):
                        input_scale(b + XS[u][0], XS[u][1])

            batches(dve, body)
            product_read("op", NB - 1, 1)
            small_read("rt", NB - 1, 0, 1)
            small_read("rt", NB - 1, 1, 0)

            def hidden(k):
                wait(dve, sg_ready, k + 1)
                dve.tensor_tensor(hid[:, :], psG1[:, I:2 * I], sg[:, :], ALU.mult).then_inc(hid_ready, 1)

            def out_rows(k):
                if isinstance(k, int) and k < 0:
                    return
                wait(dve, g2_done, k + 1)
                wait(dve, orow_free, k)
                dve.tensor_copy(orow[:, :], psG2).then_inc(orow_ready, 1)

            def step(k, k_before):
                hidden(k)
                out_rows(k_before)
                wait(dve, ht_done, k + 1)
                dve.tensor_copy(hidT[:, :, :], psHT).then_inc(hidT_ready, 1)

            dve.wait_ge(lg_ready, NT)
            for t in range(NT):
                mx = dve.max(top8[:, t, :], lg[:, t, :])
            mx.then_inc(top_done, 1)
            dve.wait_ge(top_done, 1)
            for t in range(NT):
                mi = dve.max_index(idx8[:, t, :], top8[:, t, :], lg[:, t, :])
            mi.then_inc(rt_step, 1)
            dve.tensor_tensor(wexp[:, :, :], top8[:, :, 0:TOPK], top8[:, :, 0:1].to_broadcast([P, NT, TOPK]),
                              ALU.subtract).then_inc(wexp_in, 1)
            dve.wait_ge(rt_step, 1)
            dve.tensor_copy(idxf[:, :, :], idx8[:, :, 0:TOPK]).then_inc(rt_step, 1)
            dve.wait_ge(rt_step, 2)
            dve.tensor_tensor(onehot[:, :, :, :].rearrange("p t k e -> p (t k) e"),
                              iota_e[:, :].unsqueeze(1).to_broadcast([P, NT * TOPK, E]),
                              idxf[:, :, :].rearrange("p t k -> p (t k)").unsqueeze(2).to_broadcast([P, NT * TOPK, E]),
                              ALU.is_equal).then_inc(rt_step, 1)
            dve.wait_ge(rt_step, 3)
            dve.reduce_sum(mask[:, :, :], onehot[:, :, :, :].rearrange("p t k e -> p t e k"), AX_X).then_inc(mask_ready, 1)
            dve.memset(carry[:, 0, :], 0.0).then_inc(rt_step, 1)
            for k in range(CH):
                step(k, k - 1)
            dve.wait_ge(pos_ps, 1)
            for t in range(NT):
                dve.wait_ge(rt_step, 4 + t)
                dve.tensor_tensor(carry[:, t + 1, :], carry[:, t, :], psO[:, t * E:(t + 1) * E], ALU.add).then_inc(rt_step, 1)
            done = 4 + NT
            dve.wait_ge(rt_step, done)
            dve.tensor_tensor(pos[:, :, :], psF[:, :].rearrange("p (t e) -> p t e", e=E), carry[:, 0:NT, :], ALU.add).then_inc(rt_step, 1)
            dve.wait_ge(rt_step, done + 1)
            dve.tensor_tensor(onehot[:, :, :, :], onehot[:, :, :, :], pos[:, :, :].unsqueeze(2).to_broadcast([P, NT, TOPK, E]),
                              ALU.mult).then_inc(rt_step, 1)
            dve.wait_ge(rt_step, done + 2)
            dve.reduce_sum(posk[:, :, :], onehot[:, :, :, :], AX_X).then_inc(rt_step, 1)
            dve.wait_ge(rt_step, done + 3)
            dve.tensor_scalar(over[:, :, :], posk[:, :, :], float(CAP), float(SKIP), ALU.is_ge, ALU.mult).then_inc(rt_step, 1)
            dve.tensor_scalar(posk[:, :, :], posk[:, :, :], float(CAP - 1), None, ALU.min).then_inc(rt_step, 1)
            dve.wait_ge(rt_step, done + 5)
            dve.scalar_tensor_tensor(out=slot[:, :, :], in0=idxf[:, :, :], scalar=float(CAP), in1=posk[:, :, :],
                                     op0=ALU.mult, op1=ALU.add).then_inc(rt_step, 1)
            dve.wait_ge(rt_step, done + 6)
            dve.tensor_tensor(scat_i[:, :, :], slot[:, :, :], over[:, :, :], ALU.add).then_inc(scat_ready, 1)
            dve.tensor_scalar(slot_i[:, :, :], slot[:, :, :], float(NTOK), None, ALU.add).then_inc(slots_ready, 1)
            total = carry[0:1, NT, :]
            dve.tensor_scalar(cnt[:, 0, 0, :], total, float(2 * P), None, ALU.is_gt).then_inc(cnt_step, 1)
            dve.tensor_scalar(cnt[:, 0, 1, :], total, float(3 * P), 2.0, ALU.is_gt, ALU.add).then_inc(cnt_step, 1)
            dve.wait_ge(cnt_step, 2)
            dve.tensor_tensor(cnt[:, 0, 2, :], cnt[:, 0, 0, :], cnt[:, 0, 1, :], ALU.add).then_inc(cnt_step, 1)
            dve.wait_ge(cnt_step, 3)
            dve.tensor_copy(meta_f[:, :, 1], cnt[:, 0, 2, :]).then_inc(cnt_step, 1)
            src, dst, steps = cnt[:, 0, 2, :], cnt[:, 1, 0, :], 4
            spare = cnt[:, 1, 1, :]
            sh = 1
            while sh < E:
                dve.wait_ge(cnt_step, steps)
                dve.tensor_copy(dst[:, 0:sh], src[:, 0:sh]).then_inc(cnt_step, 1)
                dve.tensor_tensor(dst[:, sh:E], src[:, sh:E], src[:, 0:E - sh], ALU.add).then_inc(cnt_step, 1)
                steps += 2
                src, dst, spare = dst, spare, (cnt[:, 1, 2, :] if sh == 1 else src)
                sh *= 2
            dve.wait_ge(cnt_step, steps)
            dve.scalar_tensor_tensor(out=meta_f[:, :, 0], in0=src, scalar=float(SH * CH - 1), in1=meta_f[:, :, 1],
                                     op0=ALU.add, op1=ALU.subtract).then_inc(cnt_step, 1)
            dve.wait_ge(cnt_step, steps + 1)
            dve.tensor_copy(meta[:, :, 0:2], meta_f[:, :, 0:2]).then_inc(meta_ready, 1)
            dve.wait_ge(wexp_done, 1)
            dve.reduce_sum(wsum[:, :], wexp[:, :, :], AX_X).then_inc(w_step, 1)
            dve.wait_ge(w_step, 1)
            dve.reciprocal(wrec[:, :], wsum[:, :]).then_inc(w_step, 1)
            dve.wait_ge(w_step, 2)
            dve.tensor_tensor(w_all[:, :, :], wexp[:, :, :], wrec[:, :].unsqueeze(2).to_broadcast([P, NT, TOPK]),
                              ALU.mult).then_inc(w_ready, 1)

            def expert(j, e, last):
                before, s, n = steps_of(dve, j, e)
                step(s, before)
                step(s + 1, s)
                if e is None:
                    step(s + 2, s + 1)
                    step(s + 3, s + 2)
                    return
                with dve.If(n > 2):
                    step(s + 2, s + 1)
                    with dve.If(n > 3):
                        step(s + 3, s + 2)
                    with dve.Else():
                        pass
                with dve.Else():
                    pass
                if last:
                    out_rows(before + n)

            with dve.Fori(1, SH) as j:
                expert(j, None, False)
            dve.wait_ge(tab_loaded, 16)
            dve.tensor_copy(tab_f[:, :], tab_i[:, :]).then_inc(tabf_ready, 1)
            dve.wait_ge(tabT_ps, 1)
            dve.tensor_copy(idx_all[:, :], psP[:, 0, 0, :]).then_inc(idx_ready, 1)
            dve.wait_ge(meta_ready, 1)
            with dve.Fori(0, E - 1) as e:
                expert(e + SH, e, False)
            expert(E - 1 + SH, E - 1, True)

            dve.wait_ge(w_ready, 1)
            with dve.Fori(0, NT // 2) as i:
                for a in range(2):
                    tile = 2 * i + a
                    dve.wait_ge(rows_s_in[a], 16 * (i + 1))
                    dve.tensor_tensor(x_all[:, tile, :], x_all[:, tile, :], rows_s[:, a, :], ALU.add).then_inc(acc_step, 1)
                    dve.wait_ge(rows_c_in[a], 16 * TOPK * (i + 1))
                    for k in range(TOPK):
                        dve.wait_ge(acc_step, TOPK * tile + k + 1)
                        add = dve.scalar_tensor_tensor(out=x_all[:, tile, :], in0=rows_c[:, a, k, :], scalar=w_all[:, tile, k:k + 1],
                                                       in1=x_all[:, tile, :], op0=ALU.mult, op1=ALU.add)
                        add.then_inc(acc_step if k < TOPK - 1 else acc_done, 1)


_INS = ["x", "cond_2048", "L0_cond_W_emb", "L0_cond_b_emb", "L0_cond_g_norm", "L0_cond_W_qkv", "L0_cond_g_q", "L0_cond_g_k",
        "L0_cond_W_out", "L0_ffn_norm_w", "L0_ffn_gate_w", "L0_ffn_w13", "L0_ffn_w2", "L0_ffn_shared_gate_w",
        "L0_ffn_shared_up_w", "L0_ffn_shared_down_w"]


def kernel(**inputs):
    import numpy as np
    from concourse import bacc
    from concourse.bass_utils import run_bass_kernel_spmd

    nc = bacc.Bacc("TRN2", target_bir_lowering=False, num_devices=1)
    arrays, args = {}, []
    for name in _INS:
        a = np.ascontiguousarray(inputs[name])
        arrays[f"in_{name}"] = a
        args.append(nc.dram_tensor(f"in_{name}", a.shape, mybir.dt.from_np(a.dtype), kind="ExternalInput").ap())
    out = nc.dram_tensor("out_rows", (NB, SEQ, D), F32, kind="ExternalOutput").ap()
    adaln_moe_kernel(nc, *args, out)
    r = run_bass_kernel_spmd(nc, [arrays], core_ids=[0])
    return r.results[0]["out_rows"]
```

```python
from contextlib import ExitStack

import concourse.bass as bass
from concourse import mybir

F32 = mybir.dt.float32
F32R = mybir.dt.float32r
I32 = mybir.dt.int32
U32 = mybir.dt.uint32
ALU = mybir.AluOpType
ACT = mybir.ActivationFunctionType
AX_X = mybir.AxisListType.X

P = 128
NB, SEQ, D = 8, 256, 512
KC = D // P
HEADS, DH = 16, 32
TPB = SEQ // P
NT = NB * TPB
NTOK = NB * SEQ
HPC = P // DH
HPU = 2
UNITS = HEADS // HPU
BLK = HPU * TPB
E, I, TOPK = 32, 256, 4
IC = I // P
CAP = 2 * NTOK * TOPK // E
CH = CAP // P
SH = NTOK // CAP
W1N, W2N = KC * 2 * I, IC * D
WN = W1N + W2N
WBUF = 3
OBUF = 4
FIRST, LAST, MID1, MID2 = range(OBUF)
PIECE = D
PIECES = WN // PIECE
PIECES1 = W1N // PIECE
EPS = 1e-6
SKIP = 1 << 20

BIG = [("op", -1, 0), ("op", -1, 1), ("k", 1, 0), ("q", 1, 0), ("k", 1, 1), ("q", 1, 1), ("v", 1, 0), ("v", 1, 1)]
SMALL = [
    [("qk", 0, 1, 0)],
    [("qk", 0, 2, 0), ("xT", 1, 1, 1)],
    [("qk", 0, 3, 0), ("nT", -1, 0, 1)],
    [("rt", -1, 0, 0), ("nT", -1, 1, 1)],
    [("rt", -1, 1, 0)],
    [("pos", -1, 0, 0)],
    [],
    [("qk", 1, 0, 0), ("xT", 2, 0, 1)],
]
XS = {0: (1, 1), 6: (2, 0)}
ROUTE_CHOICES, ROUTE_SCATTER = 4, 6
ROUTE_STEPS, POS_READ = 8, 4
KQ_ORDER = {("k", 0): 0, ("q", 0): 1, ("k", 1): 2, ("q", 1): 3}


def exists(b, off, first, last, before_last):
    if off == -1:
        return not first
    if off == 1:
        return not last
    if off == 2:
        return not (last or before_last)
    return True


def two_before(tile, t):
    return tile if t == 0 else tile - 1


def head_of(u, a):
    return u // 2, 2 * (u % 2) + a


def wait(eng, sem, value):
    if isinstance(value, int) and value <= 0:
        return
    eng.wait_ge(sem, value)


def adaln_moe_kernel(nc, x, cond, W_emb, b_emb, g_norm, W_qkv, g_q, g_k, W_out, norm_w, gate_w, w13, w2,
                     w_gate, w_up, w_down, out):
    xn_d = nc.dram_tensor("xn_scratch", [NTOK, D], F32).ap()
    tab_d = nc.dram_tensor("slot_table", [E * CAP, 1], I32).ap()
    eo_d = nc.dram_tensor("expert_rows", [NTOK + E * CAP, D], F32).ap()

    x_t = x.rearrange("b (t p) d -> (b t) p d", p=P)
    out_t = out.rearrange("b (t p) d -> (b t) p d", p=P)
    xn_t = xn_d.rearrange("(t p) d -> t p d", p=P)
    eo_t = eo_d.rearrange("(t p) d -> t p d", p=P)

    with ExitStack() as ctx:
        def sb(name, shape, dt=F32):
            return ctx.enter_context(nc.sbuf_tensor(name, shape, dt))

        def pb(name, shape):
            return ctx.enter_context(nc.psum_tensor(name, shape, F32))

        def sem(name):
            return ctx.enter_context(nc.semaphore(name))

        x_all = sb("x_all", [P, NT, D])
        wbuf = sb("wbuf", [P, WBUF, WN])
        wemb = wbuf[:, :, :].rearrange("p a n -> p (a n)")[:, 0:KC * 2 * D].rearrange("p (k n) -> p k n", k=KC)
        emb = sb("emb", [NB, D])
        embT = sb("embT", [P, KC, NB])
        bemb = sb("bemb", [P, 2 * KC])
        gnorm = sb("gnorm", [P, KC])
        ss_emb = sb("ss_emb", [P, 2 * KC, NB])
        scale_m = sb("scale_m", [P, NB, KC])
        shift_m = sb("shift_m", [P, NB, KC])
        gqk = sb("gqk", [P, 3])
        nw = sb("nw", [P, D])
        gate_rows = sb("gate_rows", [E, D])
        gateT = sb("gateT", [P, KC, E])
        ident = sb("ident", [P, P])
        tri = sb("tri", [P, P])
        ones = sb("ones", [P, P])
        iota_e = sb("iota_e", [P, E])
        tok_id = sb("tok_id", [P, NT], I32)
        zeros_f = sb("zeros_f", [P, 2, D])
        zeros_i = sb("zeros_i", [P, P], I32)
        xsq = sb("xsq", [P, D])
        ssx = sb("ssx", [P, 2])
        rsx = sb("rsx", [P, 2])
        sq = sb("sq", [P, D])
        ss = sb("ss", [P, HEADS])
        rs = sb("rs", [P, 2, HEADS])
        eps_x, eps_h, eps_kq = sb("eps_x", [P, 1]), sb("eps_h", [P, 1]), sb("eps_kq", [P, HEADS])
        minus_half = sb("minus_half", [P, HEADS])
        kq_sb = sb("kq_sb", [P, 2, D])
        nmax = sb("nmax", [P, 2, BLK])
        sums = sb("sums", [P, 2, BLK])
        rsums = sb("rsums", [P, 2, BLK])
        probs = sb("probs", [P, 2, BLK, SEQ])
        probsT = sb("probsT", [P, HPU, TPB, SEQ])
        oT = sb("oT", [P, TPB, KC, P])
        h_sb = sb("h_sb", [P, 2, D])
        hsq = sb("hsq", [P, D])
        ssh = sb("ssh", [P, 2])
        rsh = sb("rsh", [P, 2])
        xn = sb("xn", [P, 2, D])
        xnT = sb("xnT", [P, KC, P])
        lg = sb("lg", [P, TPB, E])
        top8 = sb("top8", [P, TPB, 8])
        idx8 = sb("idx8", [P, TPB, 8], U32)
        idxf = sb("idxf", [P, TPB, TOPK])
        wexp = sb("wexp", [P, NT, TOPK])
        wsum = sb("wsum", [P, NT])
        wrec = sb("wrec", [P, NT])
        w_all = sb("w_all", [P, NT, TOPK])
        onehot = sb("onehot", [P, TPB, TOPK, E])
        mask = sb("mask", [P, TPB, E])
        cum = sb("cum", [P, TPB, E])
        posk = sb("posk", [P, TPB, TOPK])
        over = sb("over", [P, TPB, TOPK])
        slot = sb("slot", [P, TPB, TOPK])
        slot_i = sb("slot_i", [P, NT, TOPK], I32)
        cnt = sb("cnt", [1, 3, 2, E])
        cnt_sum = sb("cnt_sum", [1, 2, E])
        meta_f = sb("meta_f", [1, E, 4])
        meta = sb("meta", [1, E, 4], I32)
        tab_i = sb("tab_i", [P, P], I32)
        tab_f = sb("tab_f", [P, P])
        idx_all = sb("idx_all", [P, P], I32)
        idx_cur = sb("idx_cur", [P, CH], I32)
        scat_cur = sb("scat_cur", [P, TPB, TOPK], I32)
        tok_cur = sb("tok_cur", [P, TPB], I32)
        xT_hi = sb("xT_hi", [P, KC, P], F32R)
        xT_lo = sb("xT_lo", [P, KC, P], F32R)
        sg = sb("sg", [P, I])
        hid = sb("hid", [P, I])
        hidT_hi = sb("hidT_hi", [P, IC, P], F32R)
        hidT_lo = sb("hidT_lo", [P, IC, P], F32R)
        rows_c = wbuf[:, :, :].rearrange("p a n -> p (a n)")[:, 0:2 * 4 * D].rearrange("p (a k n) -> p a k n", a=2, k=4)
        slot_cur = sb("slot_cur", [P, 2, TOPK], I32)

        def early(name, shape, dt=F32):
            return first_use.enter_context(nc.sbuf_tensor(name, shape, dt))

        with ExitStack() as first_use:
            wqkv = early("wqkv", [P, KC, 3 * D])
            wout = early("wout", [P, KC, D])
            qk_hat = early("qk_hat", [P, 4, D])
            qT = early("qT", [P, TPB, KC, P])
            kT = early("kT", [P, KC, TPB, P])
            xs = early("xs", [P, 2, D])
            xmT = early("xmT", [P, 2, KC, P])
            v_next = early("v_next", [P, TPB, D])
            v_sb = early("v_sb", [P, TPB, D])
        wsplit = sb("wsplit", [P, 2, 2 * WN], F32R)
        xrows = sb("xrows", [P, CH, D])
        orow = sb("orow", [P, OBUF, D])
        rows_s = xrows[:, 0:2, :]

        psS = pb("psS", [P, 2, HPU, TPB, SEQ])
        psP = pb("psP", [P, 2, KC, P])
        psO = pb("psO", [P, D])
        psF = pb("psF", [P, D])
        psG1 = psS[:, 0, 0, :, :].rearrange("p a n -> p (a n)")
        psXT = psS[:, 0, 1, :, :].rearrange("p a (c n) -> p (a c) n", n=P)
        psG2 = psS[:, 1, 0, :, :].rearrange("p a n -> p (a n)")
        psHT = psS[:, 1, 1, 0, :].rearrange("p (c n) -> p c n", n=P)

        x_loaded = sem("x_loaded")
        emb_loaded, wemb_loaded, wqkv_loaded, wout_loaded = (sem(f"{n}_loaded") for n in ("emb", "wemb", "wqkv", "wout"))
        small_loaded, gate_loaded = sem("small_loaded"), sem("gate_loaded")
        zeros_set, ident_raw, consts_ready, table_cleared = sem("zeros_set"), sem("ident_raw"), sem("consts_ready"), sem("table_cleared")
        embT_ps, embT_sb, ss_ps, ss_added, mod_step, mod_ready = (sem(n) for n in ("embT_ps", "embT_sb", "ss_ps", "ss_added", "mod_step", "mod_ready"))
        gateT_ps, gateT_sb, wout_ready, gqk_step, nw_ready = (sem(n) for n in ("gateT_ps", "gateT_sb", "wout_ready", "gqk_step", "nw_ready"))
        xsq_done, rsx_done, xs_ready, xT_ps, xT_sb = (sem(n) for n in ("xsq_done", "rsx_done", "xs_ready", "xT_ps", "xT_sb"))
        kq_ps, kq_sq, kq_ss, kq_rs, kq_hat, v_ps, v_ready = (sem(n) for n in ("kq_ps", "kq_sq", "kq_ss", "kq_rs", "kq_hat", "v_ps", "v_ready"))
        kq_copied, h_copied, v_moved, qk_ps, qk_ready = (sem(n) for n in ("kq_copied", "h_copied", "v_moved", "qk_ps", "qk_ready"))
        scores_ready, max_ready, exp_done, sums_read = (sem(n) for n in ("scores_ready", "max_ready", "exp_done", "sums_read"))
        pT_ps, pT_sb0, pT_sb1, pv_done, probs_ready = (sem(n) for n in ("pT_ps", "pT_sb0", "pT_sb1", "pv_done", "probs_ready"))
        oT_ready, h_ps, hsq_done, rsh_done, xn_ready, h_added = (sem(n) for n in ("oT_ready", "h_ps", "hsq_done", "rsh_done", "xn_ready", "h_added"))
        nT_ps, nT_ready, rt_ps, lg_ready, xn_stored = (sem(n) for n in ("nT_ps", "nT_ready", "rt_ps", "lg_ready", "xn_stored"))
        top_done, rt_step, wexp_in, wexp_done, mask_ready, pos_ps, totals_ps, w_ready = (sem(n) for n in ("top_done", "rt_step", "wexp_in", "wexp_done", "mask_ready", "pos_ps", "totals_ps", "w_ready"))
        scat_ready, meta_ready, scattered, tab_loaded, tabf_ready, tabT_ps, idx_ready = (sem(n) for n in ("scat_ready", "meta_ready", "scattered", "tab_loaded", "tabf_ready", "tabT_ps", "idx_ready"))
        rows_in = [sem(f"rows_in{c}") for c in range(CH)]
        idx_copied, w_loaded = sem("idx_copied"), sem("w_loaded")
        xt_done, xTs_ready, g1_done, sg_ready, hid_ready, ht_done, hidT_ready, g2_done, orow_ready = (
            sem(n) for n in ("xt_done", "xTs_ready", "g1_done", "sg_ready", "hid_ready", "ht_done", "hidT_ready", "g2_done", "orow_ready"))
        orow_stored = [sem(f"orow_stored{i}") for i in range(OBUF)]
        slot_copied, acc_step, acc_done = sem("slot_copied"), sem("acc_step"), sem("acc_done")
        rows_c_in = [sem(f"rows_c_in{a}") for a in range(2)]
        rows_s_in = [sem(f"rows_s_in{a}") for a in range(2)]
        out_stored = sem("out_stored")
        eo_zeroed, pool_passed, xn_free = sem("eo_zeroed"), sem("pool_passed"), sem("xn_free")
        dve_passed = sem("dve_passed")
        x_eps, h_eps, kq_eps = sem("x_eps"), sem("h_eps"), sem("kq_eps")
        w_hi, w_split, xhi_done, hhi_done = (sem(n) for n in ("w_hi", "w_split", "xhi_done", "hhi_done"))
        ws_loaded, eo_complete, gqk_ready, cum_ready, cum_next, slots_ready, cnt_step, w_step = (
            sem(n) for n in ("ws_loaded", "eo_complete", "gqk_ready", "cum_ready", "cum_next", "slots_ready", "cnt_step", "w_step"))

        block = ctx.enter_context(nc.Block())

        def batches(eng, body):
            body(0, True, False, False)
            with eng.Fori(1, NB - 2) as b:
                body(b, False, False, False)
            body(NB - 2, False, False, True)
            body(NB - 1, False, True, False)

        def steps_of(eng, e):
            before = eng.value_load(meta[0:1, e, 0:1], min_val=SH * CH - 1, max_val=(SH + E) * CH)
            return before, before + 1, eng.value_load(meta[0:1, e, 1:2], min_val=1, max_val=CH - 1)

        def loads_of(eng, e, c):
            return eng.value_load(meta[0:1, e, c:c + 1], min_val=SH - 1, max_val=SH + E)

        def piece_of(f, i):
            cols = slice(i * PIECE, (i + 1) * PIECE)
            lows = slice(WN + i * PIECE, WN + (i + 1) * PIECE)
            return wbuf[:, f % WBUF, cols], wsplit[:, f % 2, cols], wsplit[:, f % 2, lows]

        HI_PIECES = (range(0, 3), range(3, 4), range(4, PIECES))
        LO_PIECES = (range(0, 2), range(2, 4), range(4, PIECES))
        NO_PIECES = ((), (), ())

        def n_kq(b):
            return 4 * b

        @block.sync
        def _(sp):
            sp.dma_start(x_all[:, 0:TPB, :], x_t[0:TPB].rearrange("t p d -> p t d")).then_inc(x_loaded, 16)
            sp.dma_start(emb[:, :], cond).then_inc(emb_loaded, 16)
            sp.dma_start(wemb, W_emb.rearrange("(k p) n -> p k n", p=P)).then_inc(wemb_loaded, 16)
            sp.dma_start(wqkv[:, :, :], W_qkv.rearrange("(k p) n -> p k n", p=P)).then_inc(wqkv_loaded, 16)
            sp.dma_start(wout[:, :, :], W_out.rearrange("(k p) n -> p k n", p=P)).then_inc(wout_loaded, 16)
            for b in range(1, NB):
                sp.wait_ge(x_loaded, 16 * b)
                sp.dma_start(x_all[:, TPB * b:TPB * (b + 1), :],
                             x_t[TPB * b:TPB * (b + 1)].rearrange("t p d -> p t d")).then_inc(x_loaded, 16)

            def load_expert(e):
                dst = wbuf[:, (e + 1) % WBUF, :]
                sp.dma_start(dst[:, 0:W1N].rearrange("p (k n) -> p k n", k=KC),
                             w13[e].rearrange("(k p) n -> p k n", p=P)).then_inc(w_loaded, 16)
                sp.dma_start(dst[:, W1N:WN].rearrange("p (k n) -> p k n", k=IC),
                             w2[e].rearrange("(k p) n -> p k n", p=P)).then_inc(w_loaded, 16)

            sp.wait_ge(ss_ps, 1)
            w1_shared = wbuf[:, 0, 0:W1N].rearrange("p (k n) -> p k n", k=KC)
            sp.dma_start(w1_shared[:, :, 0:I], w_gate.rearrange("(k p) n -> p k n", p=P)).then_inc(ws_loaded, 16)
            sp.dma_start(w1_shared[:, :, I:2 * I], w_up.rearrange("(k p) n -> p k n", p=P)).then_inc(ws_loaded, 16)
            sp.dma_start(wbuf[:, 0, W1N:WN].rearrange("p (k n) -> p k n", k=IC),
                         w_down.rearrange("(k p) n -> p k n", p=P)).then_inc(ws_loaded, 16)
            load_expert(0)
            sp.wait_ge(w_loaded, 32)
            load_expert(1)

            sp.wait_ge(zeros_set, 2)
            eo_cap = eo_d[NTOK:NTOK + E * CAP, :].rearrange("(e c p) d -> e p c d", c=CH, p=P)
            with sp.Fori(0, E) as e:
                sp.dma_start(eo_cap[e, :, 2:CH, :], zeros_f[:, :, :]).then_inc(eo_zeroed, 16)
            sp.wait_ge(eo_zeroed, 16 * E)

            with sp.Fori(0, NB) as b:
                for t in range(TPB):
                    sp.wait_ge(xn_ready, TPB * b + t + 1)
                    sp.dma_start(xn_t[TPB * b + t], xn[:, t, :]).then_inc(xn_stored, 16)
                    sp.wait_ge(xn_stored, 16 * (TPB * b + t + 1))
                    sp.sem_inc(xn_free, 1)

            sp.wait_ge(w_split, PIECES)
            sp.wait_ge(w_loaded, 64)
            load_expert(2)

            def store(step, row_tile, buf):
                sp.wait_ge(orow_ready, step + 1)
                sp.dma_start(eo_t[row_tile], orow[:, buf, :]).then_inc(orow_stored[buf], 16)

            def shared(j):
                for c, buf in enumerate((FIRST, MID1, MID2, LAST)):
                    store(j * CH + c, j * CH + c, buf)

            def expert(e, fetch):
                j = SH + e
                before, s, more_steps = steps_of(sp, e)
                if fetch:
                    sp.wait_ge(w_split, PIECES * (e + 2))
                    sp.wait_ge(w_loaded, 32 * (e + 3))
                    load_expert(e + WBUF)
                store(s, j * CH, FIRST)
                with sp.If(more_steps > 1):
                    store(s + 1, j * CH + 1, MID1)
                    with sp.If(more_steps > 2):
                        store(s + 2, j * CH + 2, MID2)
                    with sp.Else():
                        pass
                with sp.Else():
                    pass
                store(s + more_steps, j * CH + more_steps, LAST)

            shared(0)
            with sp.Fori(1, SH) as j:
                shared(j)
            sp.wait_ge(meta_ready, 1)
            with sp.Fori(0, E - WBUF) as e:
                expert(e, True)
            for e in range(E - WBUF, E):
                expert(e, False)
            for buf in (FIRST, LAST):
                sp.wait_ge(orow_stored[buf], 16 * (SH + E))
            mids = [loads_of(sp, E - 1, c) + 1 for c in (2, 3)]
            for buf, count in zip((MID1, MID2), mids):
                sp.wait_ge(orow_stored[buf], 16 * count)
                sp.sem_inc(eo_complete, 1)

            def load_shared(tile, a):
                sp.dma_start(rows_s[:, a, :], eo_t[tile]).then_inc(rows_s_in[a], 16)

            for a in range(2):
                load_shared(a, a)

            def finish(i, more):
                for a in range(2):
                    sp.wait_ge(acc_done, 2 * i + a + 1)
                    sp.dma_start(out_t[2 * i + a], x_all[:, 2 * i + a, :]).then_inc(out_stored, 16)
                    if more:
                        load_shared(2 * i + 2 + a, a)

            with sp.Fori(0, NT // 2 - 1) as i:
                finish(i, True)
            finish(NT // 2 - 1, False)
            sp.wait_ge(out_stored, 16 * NT)

        @block.gpsimd
        def _(pool):
            def pool_wait(sem, value):
                wait(pool, sem, value)
                if not isinstance(value, int):
                    pool.sem_inc(pool_passed, 1)

            pool.memset(zeros_i[:, :], 0).then_inc(zeros_set, 1)
            pool.memset(zeros_f[:, :, :], 0.0).then_inc(zeros_set, 1)
            pool.memset(ident[:, :], 0.0).then_inc(ident_raw, 1)
            pool.memset(ones[:, :], 1.0).then_inc(ident_raw, 1)
            pool.iota(iota_e[:, :], [[1, E]], base=0, channel_multiplier=0,
                      allow_small_or_imprecise_dtypes=True).then_inc(ident_raw, 1)
            pool.iota(tok_id[:, :], [[P, NT]], base=0, channel_multiplier=1).then_inc(ident_raw, 1)
            pool.memset(minus_half[:, :], -0.5).then_inc(ident_raw, 1)
            pool_wait(ident_raw, 5)
            pool.affine_select(out=ident[:, :], in_=ident[:, :], compare_op=ALU.not_equal, fill=1.0, base=0,
                               pattern=[[-1, P]], channel_multiplier=1).then_inc(consts_ready, 1)
            pool.affine_select(out=tri[:, :], in_=ones[:, :], compare_op=ALU.is_ge, fill=0.0, base=-1,
                               pattern=[[1, P]], channel_multiplier=-1).then_inc(consts_ready, 1)
            pool.dma_start(bemb[:, :], b_emb.rearrange("(k p) -> p k", p=P),
                           allow_slow_non_contiguous=True).then_inc(small_loaded, 16)
            pool.dma_start(gnorm[:, :], g_norm.rearrange("(k p) -> p k", p=P),
                           allow_slow_non_contiguous=True).then_inc(small_loaded, 16)
            for i in range(HPC):
                pool.dma_start(gqk[i * DH:(i + 1) * DH, 0:1], g_q.rearrange("(p a) -> p a", a=1)).then_inc(small_loaded, 16)
                pool.dma_start(gqk[i * DH:(i + 1) * DH, 1:2], g_k.rearrange("(p a) -> p a", a=1)).then_inc(small_loaded, 16)
            pool.dma_start(nw[:, :], norm_w.rearrange("(a d) -> a d", a=1).to_broadcast([P, D])).then_inc(small_loaded, 16)
            pool.dma_start(gate_rows[:, :], gate_w).then_inc(gate_loaded, 16)
            pool_wait(zeros_set, 2)
            pool.dma_start(tab_d.rearrange("(p n) a -> p (n a)", p=P), zeros_i[:, :]).then_inc(table_cleared, 16)

            def rsqrt(out, squares, width, plus_eps, eps_added, done, n):
                pool_wait(done, n)
                pool.tensor_scalar(plus_eps[:, :], squares, width * EPS, None, ALU.add).then_inc(eps_added, 1)
                pool_wait(eps_added, n + 1)
                pool.tensor_tensor(out, plus_eps[:, :], minus_half[:, 0:plus_eps.shape[1]], ALU.pow).then_inc(done, 1)

            def input_rs(b, t):
                tile = TPB * b + t
                pool_wait(xsq_done, tile + 1)
                pool_wait(xs_ready, tile - 1)
                rsqrt(rsx[:, t:t + 1], ssx[:, t:t + 1], D, eps_x, x_eps, rsx_done, tile)

            def product_rs(kind, b, t):
                tile = TPB * b + t
                if kind == "op":
                    pool_wait(hsq_done, tile + 1)
                    pool_wait(xn_ready, two_before(tile, t))
                    rsqrt(rsh[:, t:t + 1], ssh[:, t:t + 1], D, eps_h, h_eps, rsh_done, tile)
                elif kind != "v":
                    m = KQ_ORDER[kind, t]
                    n = n_kq(b) + m
                    pool_wait(kq_ss, n + 1)
                    pool_wait(kq_hat, n - 1)
                    rsqrt(rs[:, m % 2, :], ss[:, :], DH, eps_kq, kq_eps, kq_rs, n)

            input_rs(0, 0)
            input_rs(0, 1)
            input_rs(1, 0)
            for kind, _, t in BIG[2:]:
                product_rs(kind, 0, t)

            def shared_rows(j):
                for c in range(CH):
                    if not (isinstance(j, int) and j == 0):
                        pool_wait(xt_done, (j - 1) * CH + c + 1)
                    pool.dma_start(xrows[:, c, :], xn_t[j * CH + c]).then_inc(rows_in[c], 16)

            def scatter(b):
                pool_wait(scat_ready, 2 * (b + 1))
                for g in range(TPB):
                    for k in range(TOPK):
                        pool.indirect_dma_start(
                            out=tab_d, out_offset=bass.IndirectOffsetOnAxis(ap=scat_cur[:, g, k:k + 1], axis=0),
                            in_=tok_cur[:, g:g + 1], in_offset=None,
                            bounds_check=E * CAP - 1, oob_is_err=False).then_inc(scattered, 16)

            pool_wait(table_cleared, 16)

            def body(b, first, last, before_last):
                pool_wait(v_ready, TPB * (b + 1))
                pool_wait(pv_done, UNITS * b)
                pool.tensor_copy(v_sb[:, :, :], v_next[:, :, :]).then_inc(v_moved, 1)
                for u in range(UNITS):
                    if u in XS and exists(b, XS[u][0], first, last, before_last):
                        input_rs(b + XS[u][0], XS[u][1])
                    kind, off, t = BIG[u]
                    if exists(b, off, first, last, before_last):
                        product_rs(kind, b + off, t)
                    if u == ROUTE_SCATTER and not first:
                        scatter(b - 1)
                    if last and u == 0:
                        pool_wait(v_ready, NT)
                        pool_wait(xn_stored, 16 * CH)
                        shared_rows(0)

            batches(pool, body)
            for t in range(TPB):
                product_rs("op", NB - 1, t)

            scatter(NB - 1)
            shared_rows(1)
            pool_wait(scattered, 16 * NT * TOPK)
            pool.dma_start(tab_i[:, :], tab_d.rearrange("(p n) a -> p (n a)", p=P)).then_inc(tab_loaded, 16)
            for j in range(2, SH):
                shared_rows(j)

            def gather(e):
                for c in range(CH):
                    loads = SH + e if c < 2 or isinstance(e, int) else loads_of(pool, e - 1, c) + 1
                    pool_wait(rows_in[c], 16 * loads)
                pool.tensor_copy(idx_cur[:, :], idx_all[:, bass.ds(e * CH, CH)]).then_inc(idx_copied, 1)
                pool_wait(idx_copied, e + 1)
                if isinstance(e, int) and e == 0:
                    prev = (SH - 1) * CH - 1
                else:
                    prev = pool.value_load(meta[0:1, e - 1, 0:1], min_val=SH * CH - 1, max_val=(SH + E) * CH)
                before = pool.value_load(meta[0:1, e, 0:1], min_val=SH * CH - 1, max_val=(SH + E) * CH)
                more_steps = pool.value_load(meta[0:1, e, 1:2], min_val=1, max_val=CH - 1)

                def rows(c):
                    pool_wait(xt_done, (prev + c + 2) if c < 2 else before + 1)
                    pool.indirect_dma_start(
                        out=xrows[:, c, :], out_offset=None, in_=xn_d,
                        in_offset=bass.IndirectOffsetOnAxis(ap=idx_cur[:, c:c + 1], axis=0)).then_inc(rows_in[c], 16)

                rows(0)
                rows(1)
                with pool.If(more_steps > 1):
                    rows(2)
                    with pool.If(more_steps > 2):
                        rows(3)
                    with pool.Else():
                        pass
                with pool.Else():
                    pass

            pool_wait(idx_ready, 1)
            pool_wait(meta_ready, 1)
            gather(0)
            with pool.Fori(1, E) as e:
                gather(e)

            pool_wait(eo_complete, 2)

            def gather_slots(i, a, tile):
                if i is not None:
                    pool_wait(acc_done, 2 * i + a + 1)
                pool.tensor_copy(slot_cur[:, a, :], slot_i[:, tile, :]).then_inc(slot_copied, 1)
                pool_wait(slot_copied, tile + 1)
                for k in range(TOPK):
                    pool.indirect_dma_start(
                        out=rows_c[:, a, k, :], out_offset=None, in_=eo_d,
                        in_offset=bass.IndirectOffsetOnAxis(ap=slot_cur[:, a, k:k + 1], axis=0)).then_inc(rows_c_in[a], 16)

            gather_slots(None, 0, 0)
            gather_slots(None, 1, 1)
            with pool.Fori(0, NT // 2 - 1) as i:
                for a in range(2):
                    gather_slots(i, a, 2 * i + 2 + a)

        @block.tensor
        def _(pe):
            def transposes(dst, src, k=KC, rows=P, width=P):
                for i in range(k):
                    last = pe.transpose(dst[:, i, 0:rows], src[:, i * width:(i + 1) * width], ident[0:rows, 0:rows])
                return last

            pe.wait_ge(consts_ready, 2)
            pe.wait_ge(emb_loaded, 16)
            transposes(psP[:, 0, :, :], emb[:, :], rows=NB).then_inc(embT_ps, 1)
            pe.wait_ge(gate_loaded, 16)
            transposes(psP[:, 1, :, :], gate_rows[:, :], rows=E).then_inc(gateT_ps, 1)
            pe.wait_ge(embT_sb, 1)
            pe.wait_ge(wemb_loaded, 16)
            for j in range(2 * KC):
                for k in range(KC):
                    mm = pe.matmul(psF[:, j * NB:(j + 1) * NB], wemb[:, k, j * P:(j + 1) * P], embT[:, k, :],
                                   start=(k == 0), stop=(k == KC - 1))
            mm.then_inc(ss_ps, 1)

            def scores(b, u):
                n = UNITS * b + u
                wait(pe, qk_ready, KC * b + u // 2 + 1)
                wait(pe, exp_done, n - 1)
                for a in range(HPU):
                    g, row = head_of(u, a)
                    rows = slice(row * DH, (row + 1) * DH)
                    for t in range(TPB):
                        mm = pe.matmul(psS[:, u % 2, a, t, :], qT[rows, t, g, :],
                                       kT[rows, g, :, :].rearrange("p t n -> p (t n)"), start=True, stop=True)
                mm.then_inc(scores_ready, 1)

            def small(task, b, u, in_loop=True):
                kind, off, t, bank = task
                tile = TPB * (b + off) + t
                n = UNITS * b + u
                if in_loop:
                    wait(pe, pT_sb0 if bank == 0 else pT_sb1, n + 1)
                if kind == "xT":
                    wait(pe, xs_ready, tile + 1)
                    transposes(psP[:, bank, :, :], xs[:, t, :]).then_inc(xT_ps, 1)
                if kind == "nT":
                    wait(pe, xn_ready, tile + 1)
                    transposes(psP[:, bank, :, :], xn[:, t, :]).then_inc(nT_ps, 1)
                if kind == "qk":
                    wait(pe, kq_hat, n_kq(b + off) + 4)
                    for i, m in enumerate((KQ_ORDER["q", 0], KQ_ORDER["q", 1], KQ_ORDER["k", 0], KQ_ORDER["k", 1])):
                        tr = pe.transpose(psP[:, bank, i, :], qk_hat[:, m, t * P:(t + 1) * P], ident[:, :])
                    tr.then_inc(qk_ps, 1)
                if kind == "pos":
                    wait(pe, cum_ready, b + off + 1)
                    dst = psP[:, bank, 0, 0:TPB * E]
                    pe.matmul(dst, tri[:, :], mask[:, :, :].rearrange("p t e -> p (t e)"), start=True, stop=False)
                    pe.matmul(dst, ones[:, :], cum[:, :, :].rearrange("p t e -> p (t e)"), start=False, stop=True).then_inc(pos_ps, 1)
                if kind == "rt":
                    wait(pe, nT_ready, tile + 1)
                    wait(pe, lg_ready, tile)
                    for k in range(KC):
                        mm = pe.matmul(psP[:, bank, 0, 0:E], xnT[:, k, :], gateT[:, k, :], start=(k == 0), stop=(k == KC - 1))
                    mm.then_inc(rt_ps, 1)

            def product(lhsT, rhs):
                for k in range(KC):
                    mm = pe.matmul(psF[:, :], lhsT[:, k, :], rhs[:, k, :], start=(k == 0), stop=(k == KC - 1))
                return mm

            def big(task, b, psF_free):
                kind, off, t = task
                tile = TPB * (b + off) + t
                for s, v in psF_free:
                    wait(pe, s, v)
                if kind == "op":
                    wait(pe, oT_ready, KC * (b + off + 1))
                    product(oT[:, t, :, :], wout).then_inc(h_ps, 1)
                else:
                    wait(pe, xT_sb, tile + 1)
                    j = "qkv".index(kind)
                    product(xmT[:, t, :, :], wqkv[:, :, j * D:(j + 1) * D]).then_inc(v_ps if kind == "v" else kq_ps, 1)

            def psF_copied(b, u, first, last):
                while True:
                    u -= 1
                    if u < 0:
                        return [(v_ready, TPB * (b + 1))]
                    kind, off, t = BIG[u]
                    if exists(b, off, first, last, False):
                        return [copy_of(kind, b + off, t)]

            def copy_of(kind, b, t):
                if kind == "op":
                    return h_copied, TPB * b + t + 1
                if kind == "v":
                    return v_ready, TPB * b + t + 1
                return kq_copied, n_kq(b) + KQ_ORDER[kind, t] + 1

            pe.wait_ge(ss_added, 1)
            pe.wait_ge(gateT_sb, 1)
            for t in range(TPB):
                small(("xT", 0, t, t), 0, 0, in_loop=False)
            pe.wait_ge(wqkv_loaded, 16)
            before = []
            for kind, _, t in BIG[2:]:
                big((kind, 0, t), 0, before)
                before = [copy_of(kind, 0, t)]
            small(("xT", 1, 0, 1), 0, 0, in_loop=False)
            small(("qk", 0, 0, 0), 0, 0, in_loop=False)
            pe.wait_ge(wout_ready, 1)

            def body(b, first, last, before_last):
                def transposed_probs(u):
                    n = UNITS * b + u
                    wait(pe, probs_ready, n + 1)
                    if u:
                        held = [(k, b + off, t) for k, off, t, _ in SMALL[u - 1] if exists(b, off, first, last, before_last)]
                    else:
                        held = [("qk", b, 0)] + ([] if last else [("xT", b + 1, 0)])
                    for kind, bb, t in held:
                        if kind == "pos":
                            wait(pe, rt_step, ROUTE_STEPS * bb + POS_READ)
                            continue
                        done = {"xT": xT_sb, "nT": nT_ready, "qk": qk_ready, "rt": lg_ready}[kind]
                        wait(pe, done, (KC if kind == "qk" else TPB) * bb + t + 1)
                    for a in range(HPU):
                        for t in range(TPB):
                            for c in range(TPB):
                                tr = pe.transpose(psP[:, a, c * TPB + t, :], probs[:, u % 2, a * TPB + t, c * P:(c + 1) * P], ident[:, :])
                    tr.then_inc(pT_ps, 1)

                def product_of(u):
                    if exists(b, BIG[u][1], first, last, before_last):
                        big(BIG[u], b, psF_copied(b, u, first, last))

                scores(b, 0)
                for u in range(UNITS):
                    n = UNITS * b + u
                    if u + 1 < UNITS:
                        scores(b, u + 1)
                    if u == 0:
                        product_of(u)
                        transposed_probs(u)
                    else:
                        transposed_probs(u)
                        product_of(u)
                    for task in SMALL[u]:
                        if exists(b, task[1], first, last, before_last):
                            small(task, b, u)
                    wait(pe, pT_sb0, n + 1)
                    wait(pe, pT_sb1, n + 1)
                    wait(pe, v_moved, b + 1)
                    wait(pe, oT_ready, KC * b + u // 2)
                    for a in range(HPU):
                        g, row = head_of(u, a)
                        h = g * HPC + row
                        for c in range(TPB):
                            mm = pe.matmul(psO[row * DH:(row + 1) * DH, 0:SEQ], v_sb[:, c, h * DH:(h + 1) * DH],
                                           probsT[:, a, c, :], start=(c == 0), stop=(c == TPB - 1))
                    mm.then_inc(pv_done, 1)

            batches(pe, body)
            big(("op", -1, 0), NB, [(h_copied, NT - TPB)])
            big(("op", -1, 1), NB, [(h_copied, NT - 1)])
            small(("nT", -1, 0, 1), NB, 0, in_loop=False)
            small(("rt", -1, 0, 0), NB, 0, in_loop=False)
            small(("nT", -1, 1, 1), NB, 0, in_loop=False)
            small(("rt", -1, 1, 0), NB, 0, in_loop=False)
            small(("pos", -1, 0, 1), NB, 0, in_loop=False)
            pe.wait_ge(lg_ready, NT)
            pe.matmul(psP[:, 0, 0, 0:E], ones[:, :], cum[:, TPB - 1, :], start=True, stop=False)
            pe.matmul(psP[:, 0, 0, 0:E], ones[:, :], mask[:, TPB - 1, :], start=False, stop=True).then_inc(totals_ps, 1)

            def split_parts(x_hi, x_lo, base, n):
                for c in range(n):
                    hi, lo = slice(base + c * D, base + (c + 1) * D), slice(WN + base + c * D, WN + base + (c + 1) * D)
                    yield x_hi[:, c, :], hi, c == 0, False
                    yield x_hi[:, c, :], lo, False, False
                    yield x_lo[:, c, :], hi, False, c == n - 1

            def step_gate_up(k, w):
                wait(pe, xTs_ready, k + 1)
                for xT, cols, start, stop in split_parts(xT_hi, xT_lo, 0, KC):
                    mm = pe.matmul(psG1, xT, w[:, cols], start=start, stop=stop)
                mm.then_inc(g1_done, 1)

            def step_rows(c, count):
                wait(pe, rows_in[c], 16 * count)
                transposes(psXT, xrows[:, c, :]).then_inc(xt_done, 1)

            def step_down(k, w):
                if isinstance(k, int) and k < 0:
                    return
                wait(pe, hidT_ready, k + 1)
                wait(pe, orow_ready, k)
                for hT, cols, start, stop in split_parts(hidT_hi, hidT_lo, W1N, IC):
                    mm = pe.matmul(psG2, hT, w[:, cols], start=start, stop=stop)
                mm.then_inc(g2_done, 1)

            def step_hidden(k):
                wait(pe, hid_ready, k + 1)
                transposes(psHT, hid[:, :], k=IC).then_inc(ht_done, 1)

            def rest(k, k_before, rows, w_before, w_wait=None):
                if rows is not None:
                    step_rows(*rows)
                if w_wait is not None:
                    pe.wait_ge(w_split, w_wait)
                step_down(k_before, w_before)
                step_hidden(k)

            def weights(e):
                return wsplit[:, (e + 1) % 2, :], PIECES * (e + 2)

            def first_product(k, e):
                w, split = weights(e)
                pe.wait_ge(w_split, split - PIECES + PIECES1)
                step_gate_up(k, w)

            def shared(j_before, last):
                w = wsplit[:, 0, :]
                j = j_before + 1
                for c in range(CH):
                    k = j_before * CH + (CH + c)
                    step_gate_up(k, w)
                    nxt = (c + 1, j + 1) if c < CH - 1 else (None if last else (0, j + 2))
                    rest(k, j_before * CH + (CH + c - 1), nxt, w)

            def expert(e, last):
                before, s, more_steps = steps_of(pe, e)
                w, split = weights(e)
                w_before = wsplit[:, e % 2, :]
                rest(s, before, (1, SH + e + 1), w_before)
                step_gate_up(s + 1, w)
                with pe.If(more_steps > 1):
                    rest(s + 1, s, (2, loads_of(pe, e, 2) + 1), w, split)
                    step_gate_up(s + 2, w)
                    with pe.If(more_steps > 2):
                        rest(s + 2, s + 1, (3, loads_of(pe, e, 3) + 1), w)
                        step_gate_up(s + 3, w)
                    with pe.Else():
                        pass
                with pe.Else():
                    pass
                k = s + more_steps
                rest(k, before + more_steps, None if last else (0, SH + e + 2), w, split)
                if last:
                    step_down(k, w)
                else:
                    first_product(k + 1, e + 1)

            step_rows(0, 1)
            pe.wait_ge(w_split, PIECES)
            shared(-1, False)
            with pe.Fori(0, SH - 2) as j_before:
                shared(j_before, False)
            shared(SH - 2, True)
            pe.wait_ge(tabf_ready, 1)
            pe.transpose(psP[:, 0, 0, :], tab_f[:, :], ident[:, :]).then_inc(tabT_ps, 1)
            pe.wait_ge(meta_ready, 1)
            step_rows(0, SH + 1)
            first_product(SH * CH, 0)
            with pe.Fori(0, E - 1) as e:
                expert(e, False)
            expert(E - 1, True)

        @block.scalar
        def _(act):
            def input_square(b, t):
                tile = TPB * b + t
                wait(act, x_loaded, 16 * (b + 1))
                wait(act, rsx_done, tile - 1)
                wait(act, xsq_done, tile)
                act.activation(xsq[:, :], x_all[:, tile, :], ACT.Square, accum_out=ssx[:, t:t + 1]).then_inc(xsq_done, 1)

            def product_read(kind, b, t):
                tile = TPB * b + t
                if kind == "v":
                    wait(act, v_ps, tile + 1)
                    wait(act, v_moved, b)
                    act.activation(v_next[:, t, :], psF[:, :], ACT.Copy).then_inc(v_ready, 1)
                elif kind == "op":
                    wait(act, h_ps, tile + 1)
                    wait(act, xn_ready, two_before(tile, t))
                    act.activation(h_sb[:, t, :], psF[:, :], ACT.Copy).then_inc(h_copied, 1)
                    wait(act, h_copied, tile + 1)
                    wait(act, rsh_done, two_before(tile, t))
                    wait(act, hsq_done, tile)
                    act.activation(hsq[:, :], h_sb[:, t, :], ACT.Square, accum_out=ssh[:, t:t + 1]).then_inc(hsq_done, 1)
                else:
                    m = KQ_ORDER[kind, t]
                    n = n_kq(b) + m
                    wait(act, kq_ps, n + 1)
                    wait(act, kq_hat, n - 1)
                    act.activation(kq_sb[:, m % 2, :], psF[:, :], ACT.Copy).then_inc(kq_copied, 1)
                    wait(act, kq_copied, n + 1)
                    wait(act, kq_ss, n)
                    act.activation(sq[:, :], kq_sb[:, m % 2, :], ACT.Square).then_inc(kq_sq, 1)

            def small_read(kind, b, t, bank):
                tile = TPB * b + t
                if kind == "nT":
                    wait(act, nT_ps, tile + 1)
                    act.activation(xnT[:, :, :], psP[:, bank, :, :], ACT.Copy).then_inc(nT_ready, 1)
                if kind == "qk":
                    wait(act, qk_ps, KC * b + t + 1)
                    act.activation(qT[:, :, t, :], psP[:, bank, 0:TPB, :], ACT.Copy, scale=gqk[:, 2:3])
                    act.activation(kT[:, t, :, :], psP[:, bank, TPB:2 * TPB, :], ACT.Copy).then_inc(qk_ready, 1)

            input_square(0, 0)
            input_square(0, 1)
            act.wait_ge(embT_ps, 1)
            act.activation(embT[:, :, :], psP[:, 0, :, 0:NB], ACT.Copy).then_inc(embT_sb, 1)
            act.wait_ge(gateT_ps, 1)
            act.activation(gateT[:, :, :], psP[:, 1, :, 0:E], ACT.Copy).then_inc(gateT_sb, 1)
            input_square(1, 0)
            act.wait_ge(gqk_ready, 1)
            for kind, _, t in BIG[2:]:
                product_read(kind, 0, t)
            small_read("qk", 0, 0, 0)

            def body(b, first, last, before_last):
                def exps(u):
                    n = UNITS * b + u
                    wait(act, max_ready, n + 1)
                    wait(act, pT_ps, n - 1)
                    wait(act, sums_read, n - 1)
                    for i in range(BLK):
                        ex = act.activation(probs[:, u % 2, i, :], psS[:, u % 2, i // TPB, i % TPB, :], ACT.Exp,
                                            bias=nmax[:, u % 2, i:i + 1], accum_out=sums[:, u % 2, i:i + 1])
                    ex.then_inc(exp_done, 1)

                def probs_read(u):
                    wait(act, pT_ps, UNITS * b + u + 1)
                    act.activation(probsT[:, 1, :, :].rearrange("p c n -> p (c n)"),
                                   psP[:, 1, :, :].rearrange("p c n -> p (c n)"), ACT.Copy).then_inc(pT_sb1, 1)

                def product_task(u):
                    kind, off, t = BIG[u]
                    if exists(b, off, first, last, before_last):
                        product_read(kind, b + off, t)

                exps(0)
                for u in range(UNITS):
                    if u == 0:
                        exps(u + 1)
                        product_task(u)
                        probs_read(u)
                    else:
                        probs_read(u)
                        if u + 1 < UNITS:
                            exps(u + 1)
                        product_task(u)
                    for kind, off, t, bank in SMALL[u]:
                        if exists(b, off, first, last, before_last):
                            small_read(kind, b + off, t, bank)
                    if u in XS and exists(b, XS[u][0], first, last, before_last):
                        input_square(b + XS[u][0], XS[u][1])
                    if last and u < PIECES:
                        if u == 0:
                            act.wait_ge(ws_loaded, 48)
                            act.wait_ge(v_ps, NT)
                        weights_hi(0, u)

            def weights_hi(f, i):
                raw, hi, _ = piece_of(f, i)
                act.activation(hi, raw, ACT.Copy).then_inc(w_hi, 1)

            batches(act, body)
            for t in range(TPB):
                product_read("op", NB - 1, t)
            for t in range(TPB):
                small_read("nT", NB - 1, t, 1)

            def rows_hi(k):
                act.wait_ge(xt_done, k + 1)
                act.activation(xT_hi[:, :, :], psXT, ACT.Copy).then_inc(xhi_done, 1)

            def out_rows(k, buf, stored):
                act.wait_ge(g2_done, k + 1)
                wait(act, orow_stored[buf], 16 * stored)
                act.activation(orow[:, buf, :], psG2, ACT.Copy).then_inc(orow_ready, 1)

            def front(k, more=True, split=None, pieces=()):
                act.wait_ge(g1_done, k + 1)
                act.activation(sg[:, :], psG1[:, 0:I], ACT.Silu).then_inc(sg_ready, 1)
                if more:
                    rows_hi(k + 1)
                for i in pieces:
                    weights_hi(split, i)

            def back(k, k_before, buf, stored, split=None, pieces=()):
                if buf is not None:
                    out_rows(k_before, buf, stored)
                act.wait_ge(ht_done, k + 1)
                act.activation(hidT_hi[:, :, :], psHT, ACT.Copy).then_inc(hhi_done, 1)
                for i in pieces:
                    weights_hi(split, i)

            def expert(e, last):
                before, s, more_steps = steps_of(act, e)
                pieces, f = (NO_PIECES, None) if last else (HI_PIECES, e + 2)
                if not last:
                    act.wait_ge(w_loaded, 32 * f)
                back(s, before, LAST, e + (SH - 1), f, pieces[0])
                with act.If(more_steps > 1):
                    front(s + 1, True, f, pieces[1])
                    back(s + 1, s, FIRST, SH + e, f, pieces[2])
                    mid1 = loads_of(act, e, 2)
                    with act.If(more_steps > 2):
                        mid2 = loads_of(act, e, 3)
                        front(s + 2)
                        back(s + 2, s + 1, MID1, mid1)
                        front(s + 3, not last)
                        back(s + 3, s + 2, MID2, mid2)
                    with act.Else():
                        front(s + 2, not last)
                        back(s + 2, s + 1, MID1, mid1)
                with act.Else():
                    front(s + 1, not last, f, pieces[1])
                    back(s + 1, s, FIRST, SH + e, f, pieces[2])
                if last:
                    out_rows(s + more_steps, LAST, SH + e)
                else:
                    front(s + more_steps + 1)

            def shared(j_before, first_expert):
                if first_expert:
                    act.wait_ge(w_loaded, 32)
                for c, buf in enumerate((LAST, FIRST, MID1, MID2)):
                    k = j_before * CH + (CH + c)
                    pieces = HI_PIECES if first_expert else NO_PIECES
                    front(k, not (first_expert and c == CH - 1), 1, pieces[1] if c == 1 else ())
                    if isinstance(k, int) and k == 0:
                        buf = None
                    back(k, j_before * CH + (CH + c - 1), buf, j_before + 1 if c else j_before, 1,
                         pieces[2 * c] if c < 2 else ())

            rows_hi(0)
            shared(-1, False)
            act.wait_ge(wexp_in, NB)
            act.activation(wexp[:, :, :], wexp[:, :, :], ACT.Exp).then_inc(wexp_done, 1)
            with act.Fori(0, SH - 2) as j_before:
                shared(j_before, False)
            shared(SH - 2, True)
            rows_hi(SH * CH)
            act.wait_ge(meta_ready, 1)
            front(SH * CH)
            with act.Fori(0, E - 1) as e:
                expert(e, False)
            expert(E - 1, True)

        @block.vector
        def _(dve):
            def input_scale(b, t):
                tile = TPB * b + t
                wait(dve, rsx_done, tile + 1)
                wait(dve, xT_ps, tile - 1)
                dve.tensor_scalar(xs[:, t, :], x_all[:, tile, :], rsx[:, t:t + 1], None, ALU.mult).then_inc(xs_ready, 1)

            def product_sums(kind, b, t):
                tile = TPB * b + t
                if kind == "op":
                    wait(dve, h_copied, tile + 1)
                    dve.tensor_tensor(x_all[:, tile, :], h_sb[:, t, :], x_all[:, tile, :], ALU.add).then_inc(h_added, 1)
                elif kind != "v":
                    n = n_kq(b) + KQ_ORDER[kind, t]
                    wait(dve, kq_sq, n + 1)
                    wait(dve, kq_rs, n)
                    dve.reduce_sum(ss[:, :], sq[:, :].rearrange("p (h d) -> p h d", d=DH), AX_X).then_inc(kq_ss, 1)

            def product_scale(kind, b, t):
                tile = TPB * b + t
                if kind == "op":
                    wait(dve, rsh_done, tile + 1)
                    wait(dve, xn_free, two_before(tile, t))
                    wait(dve, nT_ps, two_before(tile, t))
                    dve.scalar_tensor_tensor(out=xn[:, t, :], in0=h_sb[:, t, :], scalar=rsh[:, t:t + 1], in1=nw[:, :],
                                             op0=ALU.mult, op1=ALU.mult).then_inc(xn_ready, 1)
                elif kind != "v":
                    m = KQ_ORDER[kind, t]
                    n = n_kq(b) + m
                    wait(dve, kq_rs, n + 1)
                    wait(dve, qk_ps, KC * b)
                    dve.tensor_tensor(qk_hat[:, m, :].rearrange("p (h d) -> p h d", d=DH),
                                      kq_sb[:, m % 2, :].rearrange("p (h d) -> p h d", d=DH),
                                      rs[:, m % 2, :].unsqueeze(2).to_broadcast([P, HEADS, DH]), ALU.mult).then_inc(kq_hat, 1)

            def small_read(kind, b, t, bank):
                tile = TPB * b + t
                if kind == "xT":
                    wait(dve, xT_ps, tile + 1)
                    for k in range(KC):
                        ts = dve.tensor_scalar(xmT[:, t, k, :], psP[:, bank, k, :], scale_m[:, b, k:k + 1],
                                               shift_m[:, b, k:k + 1], ALU.mult, ALU.add)
                    ts.then_inc(xT_sb, 1)
                if kind == "rt":
                    wait(dve, rt_ps, tile + 1)
                    dve.tensor_copy(lg[:, t, :], psP[:, bank, 0, 0:E]).then_inc(lg_ready, 1)

            dve.memset(cum[:, 0, :], 0.0).then_inc(cum_next, 1)
            input_scale(0, 0)
            input_scale(0, 1)
            dve.wait_ge(small_loaded, 16 * (3 + 2 * HPC))
            dve.wait_ge(ss_ps, 1)
            dve.tensor_tensor(ss_emb[:, :, :], psF[:, 0:2 * KC * NB].rearrange("p (j b) -> p j b", b=NB),
                              bemb[:, :].unsqueeze(2).to_broadcast([P, 2 * KC, NB]), ALU.add).then_inc(ss_added, 1)
            dve.tensor_scalar(gnorm[:, :], gnorm[:, :], float(D) ** 0.5, None, ALU.mult).then_inc(mod_step, 1)
            dve.wait_ge(ss_added, 1)
            dve.wait_ge(mod_step, 1)
            dve.scalar_tensor_tensor(out=scale_m[:, :, :], in0=ss_emb[:, 0:KC, :].rearrange("p k b -> p b k"), scalar=1.0,
                                     in1=gnorm[:, :].unsqueeze(1).to_broadcast([P, NB, KC]),
                                     op0=ALU.add, op1=ALU.mult).then_inc(mod_ready, 1)
            dve.tensor_copy(shift_m[:, :, :], ss_emb[:, KC:2 * KC, :].rearrange("p k b -> p b k")).then_inc(mod_ready, 1)
            dve.tensor_scalar(nw[:, :], nw[:, :], float(D) ** 0.5, None, ALU.mult).then_inc(nw_ready, 1)
            dve.scalar_tensor_tensor(out=gqk[:, 2:3], in0=gqk[:, 0:1], scalar=float(DH) ** 0.5, in1=gqk[:, 1:2],
                                     op0=ALU.mult, op1=ALU.mult).then_inc(gqk_ready, 1)
            dve.wait_ge(mod_ready, 2)
            dve.wait_ge(nw_ready, 1)
            small_read("xT", 0, 0, 0)
            small_read("xT", 0, 1, 1)
            input_scale(1, 0)
            for kind, _, t in BIG[2:]:
                product_sums(kind, 0, t)
                product_scale(kind, 0, t)
            small_read("xT", 1, 0, 1)
            dve.wait_ge(wout_loaded, 16)
            dve.wait_ge(consts_ready, 2)
            for k in range(KC):
                tt = dve.tensor_tensor(wout[:, k, k * P:(k + 1) * P], wout[:, k, k * P:(k + 1) * P], ident[:, :], ALU.add)
            tt.then_inc(wout_ready, 1)

            def choose(b):
                steps, tile0 = ROUTE_STEPS * b, TPB * b
                wait(dve, lg_ready, tile0 + TPB)
                dve.sem_inc(dve_passed, 1)
                for t in range(TPB):
                    mx = dve.max(top8[:, t, :], lg[:, t, :])
                mx.then_inc(top_done, 1)
                wait(dve, top_done, b + 1)
                dve.sem_inc(dve_passed, 1)
                for t in range(TPB):
                    mi = dve.max_index(idx8[:, t, :], top8[:, t, :], lg[:, t, :])
                mi.then_inc(rt_step, 1)
                dve.tensor_tensor(wexp[:, bass.ds(tile0, TPB), :], top8[:, :, 0:TOPK], top8[:, :, 0:1].to_broadcast([P, TPB, TOPK]),
                                  ALU.subtract).then_inc(wexp_in, 1)
                wait(dve, rt_step, steps + 1)
                dve.tensor_copy(idxf[:, :, :], idx8[:, :, 0:TOPK]).then_inc(rt_step, 1)
                wait(dve, rt_step, steps + 2)
                dve.tensor_tensor(onehot[:, :, :, :].rearrange("p t k e -> p (t k) e"),
                                  iota_e[:, :].unsqueeze(1).to_broadcast([P, TPB * TOPK, E]),
                                  idxf[:, :, :].rearrange("p t k -> p (t k)").unsqueeze(2).to_broadcast([P, TPB * TOPK, E]),
                                  ALU.is_equal).then_inc(rt_step, 1)
                wait(dve, rt_step, steps + 3)
                dve.reduce_sum(mask[:, :, :], onehot[:, :, :, :].rearrange("p t k e -> p t e k"), AX_X).then_inc(mask_ready, 1)
                wait(dve, mask_ready, b + 1)
                wait(dve, cum_next, b + 1)
                dve.tensor_tensor(cum[:, 1, :], cum[:, 0, :], mask[:, 0, :], ALU.add).then_inc(cum_ready, 1)

            def place(b, bank):
                steps = ROUTE_STEPS * b
                wait(dve, pos_ps, b + 1)
                dve.tensor_tensor(onehot[:, :, :, :], onehot[:, :, :, :],
                                  psP[:, bank, 0, 0:TPB * E].rearrange("p (t e) -> p t e", e=E).unsqueeze(2).to_broadcast([P, TPB, TOPK, E]),
                                  ALU.mult).then_inc(rt_step, 1)
                if not (isinstance(b, int) and b == NB - 1):
                    dve.tensor_tensor(cum[:, 0, :], cum[:, 1, :], mask[:, 1, :], ALU.add).then_inc(cum_next, 1)
                wait(dve, rt_step, steps + POS_READ)
                dve.reduce_sum(posk[:, :, :], onehot[:, :, :, :], AX_X).then_inc(rt_step, 1)
                wait(dve, rt_step, steps + 5)
                dve.tensor_scalar(over[:, :, :], posk[:, :, :], float(CAP), float(SKIP), ALU.is_ge, ALU.mult).then_inc(rt_step, 1)
                dve.tensor_scalar(posk[:, :, :], posk[:, :, :], float(CAP - 1), None, ALU.min).then_inc(rt_step, 1)
                wait(dve, rt_step, steps + 7)
                dve.scalar_tensor_tensor(out=slot[:, :, :], in0=idxf[:, :, :], scalar=float(CAP), in1=posk[:, :, :],
                                         op0=ALU.mult, op1=ALU.add).then_inc(rt_step, 1)
                wait(dve, rt_step, steps + 8)
                wait(dve, scattered, 16 * TPB * TOPK * b)
                dve.tensor_tensor(scat_cur[:, :, :], slot[:, :, :], over[:, :, :], ALU.add).then_inc(scat_ready, 1)
                dve.tensor_copy(tok_cur[:, :], tok_id[:, bass.ds(TPB * b, TPB)]).then_inc(scat_ready, 1)
                dve.tensor_scalar(slot_i[:, bass.ds(TPB * b, TPB), :], slot[:, :, :], float(NTOK), None, ALU.add).then_inc(slots_ready, 1)

            def body(b, first, last, before_last):
                def row_max(u):
                    n = UNITS * b + u
                    wait(dve, scores_ready, n + 1)
                    wait(dve, exp_done, n - 1)
                    dve.tensor_reduce(nmax[:, u % 2, :].rearrange("p (a t) -> p a t", a=HPU), psS[:, u % 2, :, :, :],
                                      AX_X, ALU.max, negate=True).then_inc(max_ready, 1)

                def normalise(u):
                    n = UNITS * b + u
                    wait(dve, exp_done, n + 1)
                    wait(dve, probs_ready, n - 1)
                    dve.reciprocal(rsums[:, u % 2, :], sums[:, u % 2, :]).then_inc(sums_read, 1)
                    wait(dve, sums_read, n + 1)
                    for i in range(BLK):
                        ts = dve.tensor_scalar(probs[:, u % 2, i, :], probs[:, u % 2, i, :], rsums[:, u % 2, i:i + 1], None, ALU.mult)
                    ts.then_inc(probs_ready, 1)

                def probs_read(u):
                    wait(dve, pT_ps, UNITS * b + u + 1)
                    dve.tensor_copy(probsT[:, 0, :, :].rearrange("p c n -> p (c n)"),
                                    psP[:, 0, :, :].rearrange("p c n -> p (c n)")).then_inc(pT_sb0, 1)

                def product_task(do, u):
                    if u < 0:
                        return
                    kind, off, t = BIG[u]
                    if exists(b, off, first, last, before_last):
                        do(kind, b + off, t)

                row_max(0)
                normalise(0)
                for u in range(UNITS):
                    n = UNITS * b + u
                    if u:
                        probs_read(u)
                    if u + 1 < UNITS:
                        row_max(u + 1)
                    product_task(product_sums, u - 1)
                    if not u:
                        probs_read(u)
                    if u + 1 < UNITS:
                        normalise(u + 1)
                    for kind, off, t, bank in SMALL[u]:
                        if exists(b, off, first, last, before_last):
                            if kind == "pos":
                                place(b + off, bank)
                            else:
                                small_read(kind, b + off, t, bank)
                    if u == ROUTE_CHOICES and not first:
                        choose(b - 1)
                    if u % 2:
                        wait(dve, pv_done, n + 1)
                        dve.tensor_copy(oT[:, :, u // 2, :], psO[:, 0:SEQ].rearrange("p (t n) -> p t n", n=P)).then_inc(oT_ready, 1)
                    if last and u < PIECES:
                        weights_lo(0, u)
                    product_task(product_scale, u - 1)
                    if u in XS and exists(b, XS[u][0], first, last, before_last):
                        input_scale(b + XS[u][0], XS[u][1])

            def weights_lo(f, i):
                raw, hi, lo = piece_of(f, i)
                dve.wait_ge(w_hi, PIECES * f + i + 1)
                dve.tensor_tensor(lo, raw, hi, ALU.subtract).then_inc(w_split, 1)

            batches(dve, body)
            for t in range(TPB):
                product_sums("op", NB - 1, t)
                product_scale("op", NB - 1, t)
            for t in range(TPB):
                small_read("rt", NB - 1, t, 0)
            choose(NB - 1)
            place(NB - 1, 1)

            def hidden(k):
                wait(dve, sg_ready, k + 1)
                dve.tensor_tensor(hid[:, :], psG1[:, I:2 * I], sg[:, :], ALU.mult).then_inc(hid_ready, 1)

            def rows_lo(k):
                dve.wait_ge(xhi_done, k + 1)
                dve.tensor_tensor(xT_lo[:, :, :], psXT, xT_hi[:, :, :], ALU.subtract).then_inc(xTs_ready, 1)

            def front(k, more=True, split=None, pieces=()):
                hidden(k)
                if more:
                    rows_lo(k + 1)
                for i in pieces:
                    weights_lo(split, i)

            def back(k, split=None, pieces=()):
                dve.wait_ge(hhi_done, k + 1)
                dve.tensor_tensor(hidT_lo[:, :, :], psHT, hidT_hi[:, :, :], ALU.subtract).then_inc(hidT_ready, 1)
                for i in pieces:
                    weights_lo(split, i)

            rows_lo(0)
            def expert(e, last):
                before, s, more_steps = steps_of(dve, e)
                pieces, f = (NO_PIECES, None) if last else (LO_PIECES, e + 2)
                back(s, f, pieces[0])
                with dve.If(more_steps > 1):
                    front(s + 1, True, f, pieces[1])
                    back(s + 1, f, pieces[2])
                    with dve.If(more_steps > 2):
                        front(s + 2)
                        back(s + 2)
                    with dve.Else():
                        pass
                    front(s + more_steps, not last)
                    back(s + more_steps)
                with dve.Else():
                    front(s + 1, not last, f, pieces[1])
                    back(s + 1, f, pieces[2])
                if not last:
                    front(s + more_steps + 1)

            def shared(j, first_expert):
                for c in range(CH):
                    pieces = LO_PIECES if first_expert else NO_PIECES
                    front(j * CH + c, not (first_expert and c == CH - 1), 1, pieces[1] if c == 1 else ())
                    back(j * CH + c, 1, pieces[2 * c] if c < 2 else ())

            shared(0, False)
            dve.wait_ge(totals_ps, 1)
            total = psP[0:1, 0, 0, 0:E]
            dve.tensor_scalar(cnt[:, 0, 0, :], total, float(2 * P), None, ALU.is_gt).then_inc(cnt_step, 1)
            dve.tensor_scalar(cnt[:, 0, 1, :], total, float(3 * P), None, ALU.is_gt).then_inc(cnt_step, 1)
            dve.wait_ge(cnt_step, 2)
            dve.tensor_tensor(cnt_sum[:, 0, :], cnt[:, 0, 0, :], cnt[:, 0, 1, :], ALU.add).then_inc(cnt_step, 1)
            src, dst, spare, done = cnt[:, 0, :, :], cnt[:, 1, :, :], cnt[:, 2, :, :], 3
            sh = 1
            while sh < E:
                dve.wait_ge(cnt_step, done)
                dve.tensor_copy(dst[:, :, 0:sh], src[:, :, 0:sh]).then_inc(cnt_step, 1)
                dve.tensor_tensor(dst[:, :, sh:E], src[:, :, sh:E], src[:, :, 0:E - sh], ALU.add).then_inc(cnt_step, 1)
                done += 2
                src, dst, spare = dst, spare, src
                sh *= 2
            dve.wait_ge(cnt_step, done)
            dve.tensor_scalar(meta_f[:, :, 1], cnt_sum[:, 0, :], 1.0, None, ALU.add).then_inc(cnt_step, 1)
            dve.tensor_scalar(meta_f[:, :, 2:4].rearrange("p e k -> p k e"), src, float(SH - 1), None, ALU.add).then_inc(cnt_step, 1)
            dve.tensor_tensor(cnt_sum[:, 1, :], src[:, 0, :], src[:, 1, :], ALU.add).then_inc(cnt_step, 1)
            dve.wait_ge(cnt_step, done + 3)
            dve.scalar_tensor_tensor(out=cnt_sum[:, 1, :], in0=iota_e[0:1, :], scalar=2.0, in1=cnt_sum[:, 1, :],
                                     op0=ALU.mult, op1=ALU.add).then_inc(cnt_step, 1)
            dve.wait_ge(cnt_step, done + 4)
            dve.scalar_tensor_tensor(out=meta_f[:, :, 0], in0=cnt_sum[:, 1, :], scalar=float(SH * CH - 1), in1=cnt_sum[:, 0, :],
                                     op0=ALU.add, op1=ALU.subtract).then_inc(cnt_step, 1)
            dve.wait_ge(cnt_step, done + 5)
            dve.tensor_copy(meta[:, :, :], meta_f[:, :, :]).then_inc(meta_ready, 1)
            dve.wait_ge(wexp_done, 1)
            dve.reduce_sum(wsum[:, :], wexp[:, :, :], AX_X).then_inc(w_step, 1)
            dve.wait_ge(w_step, 1)
            dve.reciprocal(wrec[:, :], wsum[:, :]).then_inc(w_step, 1)
            dve.wait_ge(w_step, 2)
            dve.tensor_tensor(w_all[:, :, :], wexp[:, :, :], wrec[:, :].unsqueeze(2).to_broadcast([P, NT, TOPK]),
                              ALU.mult).then_inc(w_ready, 1)
            with dve.Fori(1, SH - 1) as j:
                shared(j, False)
            shared(SH - 1, True)
            dve.wait_ge(tab_loaded, 16)
            dve.tensor_copy(tab_f[:, :], tab_i[:, :]).then_inc(tabf_ready, 1)
            dve.wait_ge(tabT_ps, 1)
            dve.tensor_copy(idx_all[:, :], psP[:, 0, 0, :]).then_inc(idx_ready, 1)
            rows_lo(SH * CH)
            dve.wait_ge(meta_ready, 1)
            front(SH * CH)
            with dve.Fori(0, E - 1) as e:
                expert(e, False)
            expert(E - 1, True)

            dve.wait_ge(w_ready, 1)
            with dve.Fori(0, NT // 2) as i:
                for a in range(2):
                    tile = 2 * i + a
                    dve.wait_ge(rows_s_in[a], 16 * (i + 1))
                    dve.tensor_tensor(x_all[:, tile, :], x_all[:, tile, :], rows_s[:, a, :], ALU.add).then_inc(acc_step, 1)
                    dve.wait_ge(rows_c_in[a], 16 * TOPK * (i + 1))
                    for k in range(TOPK):
                        dve.wait_ge(acc_step, TOPK * tile + k + 1)
                        add = dve.scalar_tensor_tensor(out=x_all[:, tile, :], in0=rows_c[:, a, k, :], scalar=w_all[:, tile, k:k + 1],
                                                       in1=x_all[:, tile, :], op0=ALU.mult, op1=ALU.add)
                        add.then_inc(acc_step if k < TOPK - 1 else acc_done, 1)


_INS = ["x", "cond_2048", "L0_cond_W_emb", "L0_cond_b_emb", "L0_cond_g_norm", "L0_cond_W_qkv", "L0_cond_g_q", "L0_cond_g_k",
        "L0_cond_W_out", "L0_ffn_norm_w", "L0_ffn_gate_w", "L0_ffn_w13", "L0_ffn_w2", "L0_ffn_shared_gate_w",
        "L0_ffn_shared_up_w", "L0_ffn_shared_down_w"]


def kernel(**inputs):
    import numpy as np
    from concourse import bacc
    from concourse.bass_utils import run_bass_kernel_spmd

    nc = bacc.Bacc("TRN2", target_bir_lowering=False, num_devices=1)
    arrays, args = {}, []
    for name in _INS:
        a = np.ascontiguousarray(inputs[name])
        arrays[f"in_{name}"] = a
        args.append(nc.dram_tensor(f"in_{name}", a.shape, mybir.dt.from_np(a.dtype), kind="ExternalInput").ap())
    out = nc.dram_tensor("out_rows", (NB, SEQ, D), F32, kind="ExternalOutput").ap()
    adaln_moe_kernel(nc, *args, out)
    r = run_bass_kernel_spmd(nc, [arrays], core_ids=[0])
    return r.results[0]["out_rows"]
```

```python
from contextlib import ExitStack

import concourse.bass as bass
from concourse import mybir

F32 = mybir.dt.float32
F32R = mybir.dt.float32r
I32 = mybir.dt.int32
U32 = mybir.dt.uint32
ALU = mybir.AluOpType
ACT = mybir.ActivationFunctionType
AX_X = mybir.AxisListType.X

P = 128
NB, SEQ, D = 8, 256, 512
KC = D // P
HEADS, DH = 16, 32
TPB = SEQ // P
NT = NB * TPB
NTOK = NB * SEQ
HPC = P // DH
HPU = 2
UNITS = HEADS // HPU
BLK = HPU * TPB
E, I, TOPK = 32, 256, 4
IC = I // P
CAP = 2 * NTOK * TOPK // E
CH = CAP // P
SF = 2
SR = NT - SF * CH
W1N, W2N = KC * 2 * I, IC * D
WN = W1N + W2N
WBUF = 3
TAB_STEP = SF * CH - 2
GBUF = 4
OBUF = 4
FIRST, LAST, MID1, MID2 = range(OBUF)
PIECE = D
PIECES = WN // PIECE
PIECES1 = W1N // PIECE
EPS = 1e-6
SKIP = 1 << 20

BIG = [("op", -1, 0), ("op", -1, 1), ("k", 1, 0), ("q", 1, 0), ("k", 1, 1), ("q", 1, 1), ("v", 1, 0), ("v", 1, 1)]
SMALL = [
    [("qk", 0, 1, 0)],
    [("qk", 0, 2, 0), ("xT", 1, 1, 1)],
    [("qk", 0, 3, 0), ("nT", -1, 0, 1)],
    [("rt", -1, 0, 0), ("nT", -1, 1, 1)],
    [("rt", -1, 1, 0)],
    [("pos", -1, 0, 0)],
    [],
    [("qk", 1, 0, 0), ("xT", 2, 0, 1)],
]
XS = {0: (1, 1), 6: (2, 0)}
ROUTE_CHOICES, ROUTE_SCATTER = 4, 6
ROUTE_STEPS, POS_READ = 8, 4
KQ_ORDER = {("k", 0): 0, ("q", 0): 1, ("k", 1): 2, ("q", 1): 3}


def exists(b, off, first, last, before_last):
    if off == -1:
        return not first
    if off == 1:
        return not last
    if off == 2:
        return not (last or before_last)
    return True


def two_before(tile, t):
    return tile if t == 0 else tile - 1


def head_of(u, a):
    return u // 2, 2 * (u % 2) + a


def wait(eng, sem, value):
    if isinstance(value, int) and value <= 0:
        return
    eng.wait_ge(sem, value)


def adaln_moe_kernel(nc, x, cond, W_emb, b_emb, g_norm, W_qkv, g_q, g_k, W_out, norm_w, gate_w, w13, w2,
                     w_gate, w_up, w_down, out):
    xn_d = nc.dram_tensor("xn_scratch", [NTOK, D], F32).ap()
    tab_d = nc.dram_tensor("slot_table", [E * CAP, 1], I32).ap()
    eo_d = nc.dram_tensor("expert_rows", [E * CAP, D], F32).ap()

    x_t = x.rearrange("b (t p) d -> (b t) p d", p=P)
    out_t = out.rearrange("b (t p) d -> (b t) p d", p=P)
    xn_t = xn_d.rearrange("(t p) d -> t p d", p=P)
    eo_t = eo_d.rearrange("(t p) d -> t p d", p=P)

    with ExitStack() as ctx:
        def sb(name, shape, dt=F32):
            return ctx.enter_context(nc.sbuf_tensor(name, shape, dt))

        def pb(name, shape):
            return ctx.enter_context(nc.psum_tensor(name, shape, F32))

        def sem(name):
            return ctx.enter_context(nc.semaphore(name))

        x_all = sb("x_all", [P, NT, D])
        wbuf = sb("wbuf", [P, WBUF, WN])
        wemb = wbuf[:, :, :].rearrange("p a n -> p (a n)")[:, 0:KC * 2 * D].rearrange("p (k n) -> p k n", k=KC)
        emb = sb("emb", [NB, D])
        embT = sb("embT", [P, KC, NB])
        bemb = sb("bemb", [P, 2 * KC])
        gnorm = sb("gnorm", [P, KC])
        ss_emb = sb("ss_emb", [P, 2 * KC, NB])
        scale_m = sb("scale_m", [P, NB, KC])
        shift_m = sb("shift_m", [P, NB, KC])
        gqk = sb("gqk", [P, 3])
        nw = sb("nw", [P, D])
        gate_rows = sb("gate_rows", [E, D])
        gateT = sb("gateT", [P, KC, E])
        ident = sb("ident", [P, P])
        tri = sb("tri", [P, P])
        ones = sb("ones", [P, P])
        iota_e = sb("iota_e", [P, E + 1])
        tok_id = sb("tok_id", [P, NT], I32)
        zeros_f = sb("zeros_f", [P, 2, D])
        zeros_i = sb("zeros_i", [P, P], I32)
        xsq = sb("xsq", [P, D])
        ssx = sb("ssx", [P, 2])
        rsx = sb("rsx", [P, 2])
        sq = sb("sq", [P, D])
        ss = sb("ss", [P, HEADS])
        rs = sb("rs", [P, 2, HEADS])
        eps_x, eps_h, eps_kq = sb("eps_x", [P, 1]), sb("eps_h", [P, 1]), sb("eps_kq", [P, HEADS])
        minus_half = sb("minus_half", [P, HEADS])
        kq_sb = sb("kq_sb", [P, 2, D])
        nmax = sb("nmax", [P, 2, BLK])
        sums = sb("sums", [P, 2, BLK])
        rsums = sb("rsums", [P, 2, BLK])
        probs = sb("probs", [P, 2, BLK, SEQ])
        probsT = sb("probsT", [P, HPU, TPB, SEQ])
        oT = sb("oT", [P, TPB, KC, P])
        h_sb = sb("h_sb", [P, 2, D])
        hsq = sb("hsq", [P, D])
        ssh = sb("ssh", [P, 2])
        rsh = sb("rsh", [P, 2])
        xn = sb("xn", [P, 2, D])
        xnT = sb("xnT", [P, KC, P])
        lg = sb("lg", [P, TPB, E])
        top8 = sb("top8", [P, TPB, 8])
        idx8 = sb("idx8", [P, TPB, 8], U32)
        idxf = sb("idxf", [P, TPB, TOPK])
        wexp = sb("wexp", [P, NT, TOPK])
        wsum = sb("wsum", [P, NT])
        wrec = sb("wrec", [P, NT])
        w_all = sb("w_all", [P, NT, TOPK])
        onehot = sb("onehot", [P, TPB, TOPK, E])
        mask = sb("mask", [P, TPB, E])
        cum = sb("cum", [P, TPB, E])
        posk = sb("posk", [P, TPB, TOPK])
        over = sb("over", [P, TPB, TOPK])
        slot = sb("slot", [P, TPB, TOPK])
        slot_i = sb("slot_i", [P, NT, TOPK], I32)
        cnt = sb("cnt", [1, 3, 2, E + 1])
        cnt_sum = sb("cnt_sum", [1, E + 1])
        meta_f = sb("meta_f", [1, E + 1, 4])
        meta = sb("meta", [1, E + 1, 4], I32)
        tab_i = sb("tab_i", [P, P], I32)
        tab_f = sb("tab_f", [P, P])
        idx_all = sb("idx_all", [P, P], I32)
        idx_cur = sb("idx_cur", [P, CH], I32)
        scat_cur = sb("scat_cur", [P, TPB, TOPK], I32)
        tok_cur = sb("tok_cur", [P, TPB], I32)
        xT_hi = sb("xT_hi", [P, KC, P], F32R)
        xT_lo = sb("xT_lo", [P, KC, P], F32R)
        sg = sb("sg", [P, I])
        hid = sb("hid", [P, I])
        hidT_hi = sb("hidT_hi", [P, IC, P], F32R)
        hidT_lo = sb("hidT_lo", [P, IC, P], F32R)
        rows_c = wbuf[:, :, :].rearrange("p a n -> p (a n)")[:, 0:GBUF * TOPK * D].rearrange("p (a k n) -> p a k n", a=GBUF, k=TOPK)
        slot_cur = sb("slot_cur", [P, GBUF, TOPK], I32)

        def early(name, shape, dt=F32):
            return first_use.enter_context(nc.sbuf_tensor(name, shape, dt))

        with ExitStack() as first_use:
            wqkv = early("wqkv", [P, KC, 3 * D])
            wout = early("wout", [P, KC, D])
            qk_hat = early("qk_hat", [P, 4, D])
            qT = early("qT", [P, TPB, KC, P])
            kT = early("kT", [P, KC, TPB, P])
            xs = early("xs", [P, 2, D])
            xmT = early("xmT", [P, 2, KC, P])
            v_next = early("v_next", [P, TPB, D])
            v_sb = early("v_sb", [P, TPB, D])
        wsplit = sb("wsplit", [P, 2, 2 * WN], F32R)
        xrows = sb("xrows", [P, CH, D])
        orow = sb("orow", [P, OBUF, D])

        psS = pb("psS", [P, 2, HPU, TPB, SEQ])
        psP = pb("psP", [P, 2, KC, P])
        psO = pb("psO", [P, D])
        psF = pb("psF", [P, D])
        psG1 = psS[:, 0, 0, :, :].rearrange("p a n -> p (a n)")
        psXT = psS[:, 0, 1, :, :].rearrange("p a (c n) -> p (a c) n", n=P)
        psG2 = psS[:, 1, 0, :, :].rearrange("p a n -> p (a n)")
        psHT = psS[:, 1, 1, 0, :].rearrange("p (c n) -> p c n", n=P)

        x_loaded = sem("x_loaded")
        emb_loaded, wemb_loaded, wqkv_loaded, wout_loaded = (sem(f"{n}_loaded") for n in ("emb", "wemb", "wqkv", "wout"))
        mod_loaded, small_loaded, gate_loaded = sem("mod_loaded"), sem("small_loaded"), sem("gate_loaded")
        zeros_set, ident_raw, consts_ready, table_cleared = sem("zeros_set"), sem("ident_raw"), sem("consts_ready"), sem("table_cleared")
        embT_ps, embT_sb, ss_ps, ss_added, mod_step, mod_ready = (sem(n) for n in ("embT_ps", "embT_sb", "ss_ps", "ss_added", "mod_step", "mod_ready"))
        gateT_ps, gateT_sb, wout_ready, nw_ready = (sem(n) for n in ("gateT_ps", "gateT_sb", "wout_ready", "nw_ready"))
        xsq_done, rsx_done, xs_ready, xT_ps, xT_sb = (sem(n) for n in ("xsq_done", "rsx_done", "xs_ready", "xT_ps", "xT_sb"))
        kq_ps, kq_sq, kq_ss, kq_rs, kq_hat, v_ps, v_ready = (sem(n) for n in ("kq_ps", "kq_sq", "kq_ss", "kq_rs", "kq_hat", "v_ps", "v_ready"))
        kq_copied, h_copied, v_moved, qk_ps, qk_ready = (sem(n) for n in ("kq_copied", "h_copied", "v_moved", "qk_ps", "qk_ready"))
        scores_ready, max_ready, exp_done, sums_read = (sem(n) for n in ("scores_ready", "max_ready", "exp_done", "sums_read"))
        pT_ps, pT_sb0, pT_sb1, pv_done, probs_ready = (sem(n) for n in ("pT_ps", "pT_sb0", "pT_sb1", "pv_done", "probs_ready"))
        oT_ready, h_ps, hsq_done, rsh_done, xn_ready, h_added = (sem(n) for n in ("oT_ready", "h_ps", "hsq_done", "rsh_done", "xn_ready", "h_added"))
        nT_ps, nT_ready, rt_ps, lg_ready, xn_stored = (sem(n) for n in ("nT_ps", "nT_ready", "rt_ps", "lg_ready", "xn_stored"))
        top_done, rt_step, wexp_in, wexp_done, mask_ready, pos_ps, totals_ps, w_ready = (sem(n) for n in ("top_done", "rt_step", "wexp_in", "wexp_done", "mask_ready", "pos_ps", "totals_ps", "w_ready"))
        scat_ready, meta_ready, scattered, tab_loaded, tabf_ready, tabT_ps, idx_ready = (sem(n) for n in ("scat_ready", "meta_ready", "scattered", "tab_loaded", "tabf_ready", "tabT_ps", "idx_ready"))
        rows_in = [sem(f"rows_in{c}") for c in range(CH)]
        idx_copied, w_loaded = sem("idx_copied"), sem("w_loaded")
        xt_done, xTs_ready, g1_done, sg_ready, hid_ready, ht_done, hidT_ready, g2_done, orow_ready = (
            sem(n) for n in ("xt_done", "xTs_ready", "g1_done", "sg_ready", "hid_ready", "ht_done", "hidT_ready", "g2_done", "orow_ready"))
        orow_stored = [sem(f"orow_stored{i}") for i in range(OBUF)]
        slot_copied, acc_step, acc_done = sem("slot_copied"), sem("acc_step"), sem("acc_done")
        rows_c_in = [sem(f"rows_c_in{a}") for a in range(GBUF)]
        rows_rear = [sem(f"rows_rear{c}") for c in range(CH)]
        out_stored = sem("out_stored")
        eo_zeroed, pool_passed, xn_free = sem("eo_zeroed"), sem("pool_passed"), sem("xn_free")
        dve_passed = sem("dve_passed")
        x_eps, h_eps, kq_eps = sem("x_eps"), sem("h_eps"), sem("kq_eps")
        w_hi, w_split, xhi_done, hhi_done = (sem(n) for n in ("w_hi", "w_split", "xhi_done", "hhi_done"))
        ws_loaded, eo_complete, gqk_ready, cum_ready, cum_next, slots_ready, cnt_step, w_step = (
            sem(n) for n in ("ws_loaded", "eo_complete", "gqk_ready", "cum_ready", "cum_next", "slots_ready", "cnt_step", "w_step"))

        block = ctx.enter_context(nc.Block())

        def batches(eng, body):
            body(0, True, False, False)
            with eng.Fori(1, NB - 2) as b:
                body(b, False, False, False)
            body(NB - 2, False, False, True)
            body(NB - 1, False, True, False)

        def steps_of(eng, e):
            before = eng.value_load(meta[0:1, e, 0:1], min_val=SF * CH - 1, max_val=(SF + E) * CH)
            return before, before + 1, eng.value_load(meta[0:1, e, 1:2], min_val=0, max_val=CH - 1)

        def extra_before(eng, e, c):
            return eng.value_load(meta[0:1, e, c:c + 1], min_val=0, max_val=E)

        def piece_of(f, i):
            cols = slice(i * PIECE, (i + 1) * PIECE)
            lows = slice(WN + i * PIECE, WN + (i + 1) * PIECE)
            return wbuf[:, f % WBUF, cols], wsplit[:, f % 2, cols], wsplit[:, f % 2, lows]

        HI_PIECES = (range(0, 3), range(3, 4), range(4, PIECES))
        LO_PIECES = (range(0, 2), range(2, 4), range(4, PIECES))
        NO_PIECES = ((), (), ())

        def n_kq(b):
            return 4 * b

        @block.sync
        def _(sp):
            sp.dma_start(x_all[:, 0:TPB, :], x_t[0:TPB].rearrange("t p d -> p t d")).then_inc(x_loaded, 16)
            sp.dma_start(emb[:, :], cond).then_inc(emb_loaded, 16)
            sp.dma_start(wemb, W_emb.rearrange("(k p) n -> p k n", p=P)).then_inc(wemb_loaded, 16)
            sp.dma_start(wqkv[:, :, :], W_qkv.rearrange("(k p) n -> p k n", p=P)).then_inc(wqkv_loaded, 16)
            sp.dma_start(wout[:, :, :], W_out.rearrange("(k p) n -> p k n", p=P)).then_inc(wout_loaded, 16)
            for b in range(1, NB):
                sp.wait_ge(x_loaded, 16 * b)
                sp.dma_start(x_all[:, TPB * b:TPB * (b + 1), :],
                             x_t[TPB * b:TPB * (b + 1)].rearrange("t p d -> p t d")).then_inc(x_loaded, 16)

            def load_expert(e):
                dst = wbuf[:, (e + 1) % WBUF, :]
                sp.dma_start(dst[:, 0:W1N].rearrange("p (k n) -> p k n", k=KC),
                             w13[e].rearrange("(k p) n -> p k n", p=P)).then_inc(w_loaded, 16)
                sp.dma_start(dst[:, W1N:WN].rearrange("p (k n) -> p k n", k=IC),
                             w2[e].rearrange("(k p) n -> p k n", p=P)).then_inc(w_loaded, 16)

            sp.wait_ge(ss_ps, 1)

            def load_shared():
                w1_shared = wbuf[:, 0, 0:W1N].rearrange("p (k n) -> p k n", k=KC)
                sp.dma_start(w1_shared[:, :, 0:I], w_gate.rearrange("(k p) n -> p k n", p=P)).then_inc(ws_loaded, 16)
                sp.dma_start(w1_shared[:, :, I:2 * I], w_up.rearrange("(k p) n -> p k n", p=P)).then_inc(ws_loaded, 16)
                sp.dma_start(wbuf[:, 0, W1N:WN].rearrange("p (k n) -> p k n", k=IC),
                             w_down.rearrange("(k p) n -> p k n", p=P)).then_inc(ws_loaded, 16)

            load_shared()
            load_expert(0)
            sp.wait_ge(w_loaded, 32)
            load_expert(1)

            sp.wait_ge(zeros_set, 2)
            eo_cap = eo_d.rearrange("(e c p) d -> e p c d", c=CH, p=P)
            with sp.Fori(0, E) as e:
                sp.dma_start(eo_cap[e, :, 2:CH, :], zeros_f[:, :, :]).then_inc(eo_zeroed, 16)
            sp.wait_ge(eo_zeroed, 16 * E)

            with sp.Fori(0, NB) as b:
                for t in range(TPB):
                    sp.wait_ge(xn_ready, TPB * b + t + 1)
                    sp.dma_start(xn_t[TPB * b + t], xn[:, t, :]).then_inc(xn_stored, 16)
                    sp.wait_ge(xn_stored, 16 * (TPB * b + t + 1))
                    sp.sem_inc(xn_free, 1)

            sp.wait_ge(w_split, PIECES)
            sp.wait_ge(w_loaded, 64)
            load_expert(2)

            def store(step, row_tile, buf):
                sp.wait_ge(orow_ready, step + 1)
                sp.dma_start(eo_t[row_tile], orow[:, buf, :]).then_inc(orow_stored[buf], 16)

            def expert(e, fetch):
                before, s, more_steps = steps_of(sp, e)
                if fetch:
                    sp.wait_ge(w_split, PIECES * (e + 2))
                    sp.wait_ge(w_loaded, 32 * (e + 3))
                    load_expert(e + WBUF)
                store(s, e * CH, FIRST)
                with sp.If(more_steps > 1):
                    store(s + 1, e * CH + 1, MID1)
                    with sp.If(more_steps > 2):
                        store(s + 2, e * CH + 2, MID2)
                    with sp.Else():
                        pass
                with sp.Else():
                    pass
                return s + more_steps, e * CH + more_steps

            sp.wait_ge(meta_ready, 1)
            with sp.Fori(0, E - WBUF) as e:
                store(*expert(e, True), LAST)
            sp.wait_ge(w_split, PIECES * (E - WBUF + 2))
            load_shared()
            for e in range(E - WBUF, E - 1):
                store(*expert(e, False), LAST)
            before_last, _, _ = steps_of(sp, E - 1)
            before_rear, _, _ = steps_of(sp, E)
            stored_mids = [extra_before(sp, E, c) for c in (2, 3)]

            def load_rows(i, turned):
                sp.wait_ge(xt_done, turned)
                sp.dma_start(xrows[:, i % CH, :], xn_t[SF * CH + i]).then_inc(rows_rear[i % CH], 16)

            load_rows(0, before_last + 2)
            load_rows(1, before_last + 3)
            last_of_all = expert(E - 1, False)
            for i in range(2, CH):
                load_rows(i, before_rear + 1)
            store(*last_of_all, LAST)
            for buf in (FIRST, LAST):
                sp.wait_ge(orow_stored[buf], 16 * E)
            for buf, count in zip((MID1, MID2), stored_mids):
                sp.wait_ge(orow_stored[buf], 16 * count)
                sp.sem_inc(eo_complete, 1)
            for i in range(CH, SR):
                load_rows(i, before_rear + (2 + i - CH))

            with sp.Fori(0, NT) as tile:
                sp.wait_ge(acc_done, tile + 1)
                sp.dma_start(out_t[tile], x_all[:, tile, :]).then_inc(out_stored, 16)
            sp.wait_ge(out_stored, 16 * NT)

        @block.gpsimd
        def _(pool):
            def pool_wait(sem, value):
                wait(pool, sem, value)
                if not isinstance(value, int):
                    pool.sem_inc(pool_passed, 1)

            pool.memset(ident[:, :], 0.0).then_inc(ident_raw, 1)
            pool_wait(ident_raw, 1)
            pool.affine_select(out=ident[:, :], in_=ident[:, :], compare_op=ALU.not_equal, fill=1.0, base=0,
                               pattern=[[-1, P]], channel_multiplier=1).then_inc(consts_ready, 1)
            pool.memset(minus_half[:, :], -0.5).then_inc(ident_raw, 1)
            pool.dma_start(bemb[:, :], b_emb.rearrange("(k p) -> p k", p=P),
                           allow_slow_non_contiguous=True).then_inc(mod_loaded, 16)
            pool.dma_start(gnorm[:, :], g_norm.rearrange("(k p) -> p k", p=P),
                           allow_slow_non_contiguous=True).then_inc(mod_loaded, 16)
            pool_wait(ident_raw, 2)

            def rsqrt(out, squares, width, plus_eps, eps_added, done, n):
                pool_wait(done, n)
                pool.tensor_scalar(plus_eps[:, :], squares, width * EPS, None, ALU.add).then_inc(eps_added, 1)
                pool_wait(eps_added, n + 1)
                pool.tensor_tensor(out, plus_eps[:, :], minus_half[:, 0:plus_eps.shape[1]], ALU.pow).then_inc(done, 1)

            def input_rs(b, t):
                tile = TPB * b + t
                pool_wait(xsq_done, tile + 1)
                pool_wait(xs_ready, tile - 1)
                rsqrt(rsx[:, t:t + 1], ssx[:, t:t + 1], D, eps_x, x_eps, rsx_done, tile)

            def product_rs(kind, b, t):
                tile = TPB * b + t
                if kind == "op":
                    pool_wait(hsq_done, tile + 1)
                    pool_wait(xn_ready, two_before(tile, t))
                    rsqrt(rsh[:, t:t + 1], ssh[:, t:t + 1], D, eps_h, h_eps, rsh_done, tile)
                elif kind != "v":
                    m = KQ_ORDER[kind, t]
                    n = n_kq(b) + m
                    pool_wait(kq_ss, n + 1)
                    pool_wait(kq_hat, n - 1)
                    rsqrt(rs[:, m % 2, :], ss[:, :], DH, eps_kq, kq_eps, kq_rs, n)

            input_rs(0, 0)
            input_rs(0, 1)
            for i in range(HPC):
                pool.dma_start(gqk[i * DH:(i + 1) * DH, 0:1], g_q.rearrange("(p a) -> p a", a=1)).then_inc(small_loaded, 16)
                pool.dma_start(gqk[i * DH:(i + 1) * DH, 1:2], g_k.rearrange("(p a) -> p a", a=1)).then_inc(small_loaded, 16)
            pool.dma_start(nw[:, :], norm_w.rearrange("(a d) -> a d", a=1).to_broadcast([P, D])).then_inc(small_loaded, 16)
            pool.dma_start(gate_rows[:, :], gate_w).then_inc(gate_loaded, 16)
            pool.memset(ones[:, :], 1.0).then_inc(ident_raw, 1)
            pool.iota(iota_e[:, :], [[1, E + 1]], base=0, channel_multiplier=0,
                      allow_small_or_imprecise_dtypes=True).then_inc(ident_raw, 1)
            pool.iota(tok_id[:, :], [[P, NT]], base=0, channel_multiplier=1).then_inc(ident_raw, 1)
            pool_wait(ident_raw, 5)
            pool.affine_select(out=tri[:, :], in_=ones[:, :], compare_op=ALU.is_ge, fill=0.0, base=-1,
                               pattern=[[1, P]], channel_multiplier=-1).then_inc(consts_ready, 1)
            for i, (kind, _, t) in enumerate(BIG[2:]):
                product_rs(kind, 0, t)
                if i == 1:
                    input_rs(1, 0)
            pool.memset(zeros_i[:, :], 0).then_inc(zeros_set, 1)
            pool.memset(zeros_f[:, :, :], 0.0).then_inc(zeros_set, 1)
            pool_wait(zeros_set, 2)
            pool.dma_start(tab_d.rearrange("(p n) a -> p (n a)", p=P), zeros_i[:, :]).then_inc(table_cleared, 16)

            def shared_rows(j):
                for c in range(CH):
                    if not (isinstance(j, int) and j == 0):
                        pool_wait(xt_done, (j - 1) * CH + c + 1)
                    pool.dma_start(xrows[:, c, :], xn_t[j * CH + c]).then_inc(rows_in[c], 16)

            def scatter(b):
                pool_wait(scat_ready, 2 * (b + 1))
                for g in range(TPB):
                    for k in range(TOPK):
                        pool.indirect_dma_start(
                            out=tab_d, out_offset=bass.IndirectOffsetOnAxis(ap=scat_cur[:, g, k:k + 1], axis=0),
                            in_=tok_cur[:, g:g + 1], in_offset=None,
                            bounds_check=E * CAP - 1, oob_is_err=False).then_inc(scattered, 16)

            pool_wait(table_cleared, 16)

            def body(b, first, last, before_last):
                pool_wait(v_ready, TPB * (b + 1))
                pool_wait(pv_done, UNITS * b)
                pool.tensor_copy(v_sb[:, :, :], v_next[:, :, :]).then_inc(v_moved, 1)
                for u in range(UNITS):
                    if u in XS and exists(b, XS[u][0], first, last, before_last):
                        input_rs(b + XS[u][0], XS[u][1])
                    kind, off, t = BIG[u]
                    if exists(b, off, first, last, before_last):
                        product_rs(kind, b + off, t)
                    if u == ROUTE_SCATTER and not first:
                        scatter(b - 1)
                    if last and u == 0:
                        pool_wait(v_ready, NT)
                        pool_wait(xn_stored, 16 * CH)
                        shared_rows(0)

            batches(pool, body)
            for t in range(TPB):
                product_rs("op", NB - 1, t)

            scatter(NB - 1)
            pool_wait(xn_stored, 16 * NT)
            for j in range(1, SF):
                shared_rows(j)
            pool_wait(scattered, 16 * NT * TOPK)
            pool.dma_start(tab_i[:, :], tab_d.rearrange("(p n) a -> p (n a)", p=P)).then_inc(tab_loaded, 16)

            def gather(e):
                for c in range(CH):
                    loads = e + SF if c < 2 else extra_before(pool, e, c) + SF
                    pool_wait(rows_in[c], 16 * loads)
                pool.tensor_copy(idx_cur[:, :], idx_all[:, bass.ds(e * CH, CH)]).then_inc(idx_copied, 1)
                pool_wait(idx_copied, e + 1)
                if isinstance(e, int) and e == 0:
                    prev = (SF - 1) * CH - 1
                else:
                    prev = pool.value_load(meta[0:1, e - 1, 0:1], min_val=SF * CH - 1, max_val=(SF + E) * CH)
                before = pool.value_load(meta[0:1, e, 0:1], min_val=SF * CH - 1, max_val=(SF + E) * CH)
                more_steps = pool.value_load(meta[0:1, e, 1:2], min_val=1, max_val=CH - 1)

                def rows(c):
                    pool_wait(xt_done, (prev + c + 2) if c < 2 else before + 1)
                    pool.indirect_dma_start(
                        out=xrows[:, c, :], out_offset=None, in_=xn_d,
                        in_offset=bass.IndirectOffsetOnAxis(ap=idx_cur[:, c:c + 1], axis=0)).then_inc(rows_in[c], 16)

                rows(0)
                rows(1)
                with pool.If(more_steps > 1):
                    rows(2)
                    with pool.If(more_steps > 2):
                        rows(3)
                    with pool.Else():
                        pass
                with pool.Else():
                    pass

            pool_wait(idx_ready, 1)
            pool_wait(meta_ready, 1)
            gather(0)
            with pool.Fori(1, E) as e:
                gather(e)

            pool_wait(eo_complete, 2)
            pool_wait(w_split, PIECES * (E + 2))

            def gather_slots(tile, a, combined=None):
                if combined is not None:
                    pool_wait(acc_done, combined)
                pool.tensor_copy(slot_cur[:, a, :], slot_i[:, tile, :]).then_inc(slot_copied, 1)
                pool_wait(slot_copied, tile + 1)
                for k in range(TOPK):
                    pool.indirect_dma_start(
                        out=rows_c[:, a, k, :], out_offset=None, in_=eo_d,
                        in_offset=bass.IndirectOffsetOnAxis(ap=slot_cur[:, a, k:k + 1], axis=0)).then_inc(rows_c_in[a], 16)

            for a in range(GBUF):
                gather_slots(a, a)
            with pool.Fori(0, NT // GBUF - 1) as i:
                for a in range(GBUF):
                    gather_slots(GBUF * i + GBUF + a, a, GBUF * i + a + 1)

        @block.tensor
        def _(pe):
            def transposes(dst, src, k=KC, rows=P, width=P):
                for i in range(k):
                    last = pe.transpose(dst[:, i, 0:rows], src[:, i * width:(i + 1) * width], ident[0:rows, 0:rows])
                return last

            pe.wait_ge(consts_ready, 1)
            pe.wait_ge(emb_loaded, 16)
            transposes(psP[:, 0, :, :], emb[:, :], rows=NB).then_inc(embT_ps, 1)
            pe.wait_ge(embT_sb, 1)
            pe.wait_ge(wemb_loaded, 16)
            for j in range(2 * KC):
                for k in range(KC):
                    mm = pe.matmul(psF[:, j * NB:(j + 1) * NB], wemb[:, k, j * P:(j + 1) * P], embT[:, k, :],
                                   start=(k == 0), stop=(k == KC - 1))
            mm.then_inc(ss_ps, 1)

            def scores(b, u):
                n = UNITS * b + u
                wait(pe, qk_ready, KC * b + u // 2 + 1)
                wait(pe, exp_done, n - 1)
                for t in range(TPB):
                    for a in range(HPU):
                        g, row = head_of(u, a)
                        rows = slice(row * DH, (row + 1) * DH)
                        mm = pe.matmul(psS[:, u % 2, a, t, :], qT[rows, t, g, :],
                                       kT[rows, g, :, :].rearrange("p t n -> p (t n)"), start=True, stop=True)
                mm.then_inc(scores_ready, 1)

            def small(task, b, u, in_loop=True):
                kind, off, t, bank = task
                tile = TPB * (b + off) + t
                n = UNITS * b + u
                if in_loop:
                    wait(pe, pT_sb0 if bank == 0 else pT_sb1, n + 1)
                if kind == "xT":
                    wait(pe, xs_ready, tile + 1)
                    transposes(psP[:, bank, :, :], xs[:, t, :]).then_inc(xT_ps, 1)
                if kind == "nT":
                    wait(pe, xn_ready, tile + 1)
                    transposes(psP[:, bank, :, :], xn[:, t, :]).then_inc(nT_ps, 1)
                if kind == "qk":
                    wait(pe, kq_hat, n_kq(b + off) + 4)
                    for i, m in enumerate((KQ_ORDER["q", 0], KQ_ORDER["q", 1], KQ_ORDER["k", 0], KQ_ORDER["k", 1])):
                        tr = pe.transpose(psP[:, bank, i, :], qk_hat[:, m, t * P:(t + 1) * P], ident[:, :])
                    tr.then_inc(qk_ps, 1)
                if kind == "pos":
                    wait(pe, cum_ready, b + off + 1)
                    dst = psP[:, bank, 0, 0:TPB * E]
                    pe.matmul(dst, tri[:, :], mask[:, :, :].rearrange("p t e -> p (t e)"), start=True, stop=False)
                    pe.matmul(dst, ones[:, :], cum[:, :, :].rearrange("p t e -> p (t e)"), start=False, stop=True).then_inc(pos_ps, 1)
                if kind == "rt":
                    wait(pe, nT_ready, tile + 1)
                    wait(pe, lg_ready, tile)
                    for k in range(KC):
                        mm = pe.matmul(psP[:, bank, 0, 0:E], xnT[:, k, :], gateT[:, k, :], start=(k == 0), stop=(k == KC - 1))
                    mm.then_inc(rt_ps, 1)

            def product(lhsT, rhs, dst):
                for k in range(KC):
                    mm = pe.matmul(dst[:, :], lhsT[:, k, :], rhs[:, k, :], start=(k == 0), stop=(k == KC - 1))
                return mm

            def big(task, b, psF_free, dst=psF):
                kind, off, t = task
                tile = TPB * (b + off) + t
                for s, v in psF_free:
                    wait(pe, s, v)
                if kind == "op":
                    wait(pe, wout_ready, 1)
                    wait(pe, oT_ready, KC * (b + off + 1))
                    product(oT[:, t, :, :], wout, dst).then_inc(h_ps, 1)
                else:
                    wait(pe, xT_sb, tile + 1)
                    j = "qkv".index(kind)
                    product(xmT[:, t, :, :], wqkv[:, :, j * D:(j + 1) * D], dst).then_inc(v_ps if kind == "v" else kq_ps, 1)

            def psF_copied(b, u, first, last):
                while True:
                    u -= 1
                    if u < 0:
                        return [(v_ready, TPB * (b + 1))]
                    kind, off, t = BIG[u]
                    if exists(b, off, first, last, False):
                        return [copy_of(kind, b + off, t)]

            def copy_of(kind, b, t):
                if kind == "op":
                    return h_copied, TPB * b + t + 1
                if kind == "v":
                    return v_ready, TPB * b + t + 1
                return kq_copied, n_kq(b) + KQ_ORDER[kind, t] + 1

            for t in range(TPB):
                small(("xT", 0, t, t), 0, 0, in_loop=False)
            pe.wait_ge(wqkv_loaded, 16)
            frees = [[(ss_added, 1)], []]
            for i, (kind, _, t) in enumerate(BIG[2:]):
                big((kind, 0, t), 0, frees[i % 2], (psF, psO)[i % 2])
                frees[i % 2] = [copy_of(kind, 0, t)]
            pe.wait_ge(gate_loaded, 16)
            pe.wait_ge(xT_sb, TPB)
            transposes(psP[:, 0, :, :], gate_rows[:, :], rows=E).then_inc(gateT_ps, 1)
            small(("xT", 1, 0, 1), 0, 0, in_loop=False)
            pe.wait_ge(gateT_sb, 1)
            small(("qk", 0, 0, 0), 0, 0, in_loop=False)

            def body(b, first, last, before_last):
                def transposed_probs(u):
                    n = UNITS * b + u
                    wait(pe, probs_ready, n + 1)
                    if u:
                        held = [(k, b + off, t) for k, off, t, _ in SMALL[u - 1] if exists(b, off, first, last, before_last)]
                    else:
                        held = [("qk", b, 0)] + ([] if last else [("xT", b + 1, 0)])
                    for kind, bb, t in held:
                        if kind == "pos":
                            wait(pe, rt_step, ROUTE_STEPS * bb + POS_READ)
                            continue
                        done = {"xT": xT_sb, "nT": nT_ready, "qk": qk_ready, "rt": lg_ready}[kind]
                        wait(pe, done, (KC if kind == "qk" else TPB) * bb + t + 1)
                    for a in range(HPU):
                        for t in range(TPB):
                            for c in range(TPB):
                                tr = pe.transpose(psP[:, a, c * TPB + t, :], probs[:, u % 2, a * TPB + t, c * P:(c + 1) * P], ident[:, :])
                    tr.then_inc(pT_ps, 1)

                def product_of(u):
                    if exists(b, BIG[u][1], first, last, before_last):
                        big(BIG[u], b, psF_copied(b, u, first, last))

                scores(b, 0)
                for u in range(UNITS):
                    n = UNITS * b + u
                    if u + 1 < UNITS:
                        scores(b, u + 1)
                    if u == 0:
                        product_of(u)
                        transposed_probs(u)
                    else:
                        transposed_probs(u)
                        product_of(u)
                    for task in SMALL[u]:
                        if exists(b, task[1], first, last, before_last):
                            small(task, b, u)
                    wait(pe, pT_sb0, n + 1)
                    wait(pe, pT_sb1, n + 1)
                    wait(pe, v_moved, b + 1)
                    wait(pe, oT_ready, KC * b + u // 2)
                    for a in range(HPU):
                        g, row = head_of(u, a)
                        h = g * HPC + row
                        for c in range(TPB):
                            mm = pe.matmul(psO[row * DH:(row + 1) * DH, 0:SEQ], v_sb[:, c, h * DH:(h + 1) * DH],
                                           probsT[:, a, c, :], start=(c == 0), stop=(c == TPB - 1))
                    mm.then_inc(pv_done, 1)

            batches(pe, body)
            big(("op", -1, 0), NB, [(h_copied, NT - TPB)])
            big(("op", -1, 1), NB, [], psO)
            def split_parts(x_hi, x_lo, base, n):
                for c in range(n):
                    hi, lo = slice(base + c * D, base + (c + 1) * D), slice(WN + base + c * D, WN + base + (c + 1) * D)
                    yield x_hi[:, c, :], hi, c == 0, False
                    yield x_hi[:, c, :], lo, False, False
                    yield x_lo[:, c, :], hi, False, c == n - 1

            def step_gate_up(k, w):
                wait(pe, xTs_ready, k + 1)
                for xT, cols, start, stop in split_parts(xT_hi, xT_lo, 0, KC):
                    mm = pe.matmul(psG1, xT, w[:, cols], start=start, stop=stop)
                mm.then_inc(g1_done, 1)

            def step_rows(c, count, loaded=rows_in):
                wait(pe, loaded[c], 16 * count)
                transposes(psXT, xrows[:, c, :]).then_inc(xt_done, 1)

            def step_down(k, w):
                if isinstance(k, int) and k < 0:
                    return
                wait(pe, hidT_ready, k + 1)
                wait(pe, orow_ready, k)
                for hT, cols, start, stop in split_parts(hidT_hi, hidT_lo, W1N, IC):
                    mm = pe.matmul(psG2, hT, w[:, cols], start=start, stop=stop)
                mm.then_inc(g2_done, 1)

            def step_hidden(k):
                wait(pe, hid_ready, k + 1)
                transposes(psHT, hid[:, :], k=IC).then_inc(ht_done, 1)

            def rest(k, k_before, rows, w_before, w_wait=None):
                if rows is not None:
                    step_rows(*rows)
                if w_wait is not None:
                    pe.wait_ge(w_split, w_wait)
                step_down(k_before, w_before)
                step_hidden(k)

            def weights(e):
                return wsplit[:, (e + 1) % 2, :], PIECES * (e + 2)

            def first_product(k, e):
                w, split = weights(e)
                pe.wait_ge(w_split, split - PIECES + PIECES1)
                step_gate_up(k, w)

            def shared(k, nxt, w_before=None):
                w = wsplit[:, 0, :]
                if k:
                    step_gate_up(k, w)
                rest(k, k - 1, nxt, w)

            def expert(e, last):
                before, s, more_steps = steps_of(pe, e)
                w, split = weights(e)
                w_before = wsplit[:, e % 2, :]
                rest(s, before, (1, e + (SF + 1)), w_before)
                step_gate_up(s + 1, w)
                with pe.If(more_steps > 1):
                    rest(s + 1, s, (2, extra_before(pe, e, 2) + (SF + 1)), w, split)
                    step_gate_up(s + 2, w)
                    with pe.If(more_steps > 2):
                        rest(s + 2, s + 1, (3, extra_before(pe, e, 3) + (SF + 1)), w)
                        step_gate_up(s + 3, w)
                    with pe.Else():
                        pass
                with pe.Else():
                    pass
                k = s + more_steps
                rest(k, before + more_steps, (0, 1, rows_rear) if last else (0, e + (SF + 2)), w, split)
                first_product(k + 1, e + 1)

            def rear():
                before, k, _ = steps_of(pe, E)
                w, split = weights(E)
                for i in range(SR):
                    nxt = ((i + 1) % CH, (i + 1) // CH + 1, rows_rear) if i + 1 < SR else None
                    rest(k + i, before + i, nxt, w if i else wsplit[:, E % 2, :], None if i == 0 else split)
                    if i + 1 < SR:
                        step_gate_up(k + i + 1, w)
                step_down(k + (SR - 1), w)

            step_rows(0, 1)
            small(("nT", -1, 0, 1), NB, 0, in_loop=False)
            small(("rt", -1, 0, 0), NB, 0, in_loop=False)
            small(("nT", -1, 1, 1), NB, 0, in_loop=False)
            small(("rt", -1, 1, 0), NB, 0, in_loop=False)
            pe.wait_ge(w_split, PIECES)
            step_gate_up(0, wsplit[:, 0, :])
            small(("pos", -1, 0, 1), NB, 0, in_loop=False)
            pe.wait_ge(lg_ready, NT)
            pe.matmul(psP[:, 0, 0, 0:E], ones[:, :], cum[:, TPB - 1, :], start=True, stop=False)
            pe.matmul(psP[:, 0, 0, 0:E], ones[:, :], mask[:, TPB - 1, :], start=False, stop=True).then_inc(totals_ps, 1)
            for k in range(SF * CH):
                c, j = (k + 1) % CH, (k + 1) // CH
                shared(k, (c, j + 1))
                if k == TAB_STEP:
                    pe.wait_ge(tabf_ready, 1)
                    pe.transpose(psP[:, 0, 0, :], tab_f[:, :], ident[:, :]).then_inc(tabT_ps, 1)
            pe.wait_ge(meta_ready, 1)
            first_product(SF * CH, 0)
            with pe.Fori(0, E - 1) as e:
                expert(e, False)
            expert(E - 1, True)
            rear()

        @block.scalar
        def _(act):
            def input_square(b, t):
                tile = TPB * b + t
                wait(act, x_loaded, 16 * (b + 1))
                wait(act, rsx_done, tile - 1)
                wait(act, xsq_done, tile)
                act.activation(xsq[:, :], x_all[:, tile, :], ACT.Square, accum_out=ssx[:, t:t + 1]).then_inc(xsq_done, 1)

            def product_read(kind, b, t, src=psF):
                tile = TPB * b + t
                if kind == "v":
                    wait(act, v_ps, tile + 1)
                    wait(act, v_moved, b)
                    act.activation(v_next[:, t, :], src[:, :], ACT.Copy).then_inc(v_ready, 1)
                elif kind == "op":
                    wait(act, h_ps, tile + 1)
                    wait(act, xn_ready, two_before(tile, t))
                    act.activation(h_sb[:, t, :], src[:, :], ACT.Copy).then_inc(h_copied, 1)
                    wait(act, h_copied, tile + 1)
                    wait(act, rsh_done, two_before(tile, t))
                    wait(act, hsq_done, tile)
                    act.activation(hsq[:, :], h_sb[:, t, :], ACT.Square, accum_out=ssh[:, t:t + 1]).then_inc(hsq_done, 1)
                else:
                    m = KQ_ORDER[kind, t]
                    n = n_kq(b) + m
                    wait(act, kq_ps, n + 1)
                    wait(act, kq_hat, n - 1)
                    act.activation(kq_sb[:, m % 2, :], src[:, :], ACT.Copy).then_inc(kq_copied, 1)
                    wait(act, kq_copied, n + 1)
                    wait(act, kq_ss, n)
                    act.activation(sq[:, :], kq_sb[:, m % 2, :], ACT.Square).then_inc(kq_sq, 1)

            def small_read(kind, b, t, bank):
                tile = TPB * b + t
                if kind == "nT":
                    wait(act, nT_ps, tile + 1)
                    act.activation(xnT[:, :, :], psP[:, bank, :, :], ACT.Copy).then_inc(nT_ready, 1)
                if kind == "qk":
                    wait(act, qk_ps, KC * b + t + 1)
                    act.activation(qT[:, :, t, :], psP[:, bank, 0:TPB, :], ACT.Copy, scale=gqk[:, 2:3])
                    act.activation(kT[:, t, :, :], psP[:, bank, TPB:2 * TPB, :], ACT.Copy).then_inc(qk_ready, 1)

            input_square(0, 0)
            input_square(0, 1)
            act.wait_ge(embT_ps, 1)
            act.activation(embT[:, :, :], psP[:, 0, :, 0:NB], ACT.Copy).then_inc(embT_sb, 1)
            for i, (kind, _, t) in enumerate(BIG[2:]):
                product_read(kind, 0, t, (psF, psO)[i % 2])
                if i == 1:
                    input_square(1, 0)
            act.wait_ge(gateT_ps, 1)
            act.activation(gateT[:, :, :], psP[:, 0, :, 0:E], ACT.Copy).then_inc(gateT_sb, 1)
            act.wait_ge(gqk_ready, 1)
            small_read("qk", 0, 0, 0)

            def body(b, first, last, before_last):
                def exps(u):
                    n = UNITS * b + u
                    wait(act, max_ready, n + 1)
                    wait(act, pT_ps, n - 1)
                    wait(act, sums_read, n - 1)
                    for i in range(BLK):
                        ex = act.activation(probs[:, u % 2, i, :], psS[:, u % 2, i // TPB, i % TPB, :], ACT.Exp,
                                            bias=nmax[:, u % 2, i:i + 1], accum_out=sums[:, u % 2, i:i + 1])
                    ex.then_inc(exp_done, 1)

                def probs_read(u):
                    wait(act, pT_ps, UNITS * b + u + 1)
                    act.activation(probsT[:, 1, :, :].rearrange("p c n -> p (c n)"),
                                   psP[:, 1, :, :].rearrange("p c n -> p (c n)"), ACT.Copy).then_inc(pT_sb1, 1)

                def product_task(u):
                    kind, off, t = BIG[u]
                    if exists(b, off, first, last, before_last):
                        product_read(kind, b + off, t)

                exps(0)
                for u in range(UNITS):
                    if u == 0:
                        exps(u + 1)
                        product_task(u)
                        probs_read(u)
                    else:
                        probs_read(u)
                        if u + 1 < UNITS:
                            exps(u + 1)
                        product_task(u)
                    for kind, off, t, bank in SMALL[u]:
                        if exists(b, off, first, last, before_last):
                            small_read(kind, b + off, t, bank)
                    if u in XS and exists(b, XS[u][0], first, last, before_last):
                        input_square(b + XS[u][0], XS[u][1])
                    if last and u < PIECES:
                        if u == 0:
                            act.wait_ge(ws_loaded, 48)
                            act.wait_ge(v_ps, NT)
                        weights_hi(0, u)

            def weights_hi(f, i):
                raw, hi, _ = piece_of(f, i)
                act.activation(hi, raw, ACT.Copy).then_inc(w_hi, 1)

            def rows_hi(k):
                act.wait_ge(xt_done, k + 1)
                act.activation(xT_hi[:, :, :], psXT, ACT.Copy).then_inc(xhi_done, 1)

            batches(act, body)
            for t in range(TPB):
                product_read("op", NB - 1, t, (psF, psO)[t])
            rows_hi(0)
            for t in range(TPB):
                small_read("nT", NB - 1, t, 1)

            def out_rows(k, buf, stored):
                act.wait_ge(g2_done, k + 1)
                wait(act, orow_stored[buf], 16 * stored)
                act.activation(orow[:, buf, :], psG2, ACT.Copy).then_inc(orow_ready, 1)

            def front(k, more=True, split=None, pieces=()):
                act.wait_ge(g1_done, k + 1)
                act.activation(sg[:, :], psG1[:, 0:I], ACT.Silu).then_inc(sg_ready, 1)
                if more:
                    rows_hi(k + 1)
                for i in pieces:
                    weights_hi(split, i)

            def back(k, k_before, buf, stored, split=None, pieces=()):
                if buf is None:
                    if not (isinstance(k, int) and k == 0):
                        act.wait_ge(g2_done, k)
                else:
                    out_rows(k_before, buf, stored)
                act.wait_ge(ht_done, k + 1)
                act.activation(hidT_hi[:, :, :], psHT, ACT.Copy).then_inc(hhi_done, 1)
                for i in pieces:
                    weights_hi(split, i)

            def expert(e, first, last):
                before, s, more_steps = steps_of(act, e)
                f = e + 2
                if last:
                    act.wait_ge(ws_loaded, 96)
                else:
                    act.wait_ge(w_loaded, 32 * f)
                if first:
                    back(s, before, None, 0, f, HI_PIECES[0])
                else:
                    back(s, before, LAST, e - 1, f, HI_PIECES[0])
                with act.If(more_steps > 1):
                    front(s + 1, True, f, HI_PIECES[1])
                    back(s + 1, s, FIRST, e, f, HI_PIECES[2])
                    mid1 = extra_before(act, e, 2)
                    with act.If(more_steps > 2):
                        mid2 = extra_before(act, e, 3)
                        front(s + 2)
                        back(s + 2, s + 1, MID1, mid1)
                        front(s + 3)
                        back(s + 3, s + 2, MID2, mid2)
                    with act.Else():
                        front(s + 2)
                        back(s + 2, s + 1, MID1, mid1)
                with act.Else():
                    front(s + 1, True, f, HI_PIECES[1])
                    back(s + 1, s, FIRST, e, f, HI_PIECES[2])
                front(s + more_steps + 1)

            def shared(k, pieces_front=(), pieces_back=()):
                front(k, True, 1, pieces_front)
                back(k, k - 1, None, 0, 1, pieces_back)

            def rear():
                before, k, _ = steps_of(act, E)
                for i in range(SR):
                    back(k + i, before + i, None if i else LAST, E - 1)
                    if i + 1 < SR:
                        front(k + i + 1, i + 2 < SR)

            for k in range((SF - 1) * CH):
                shared(k)
            act.wait_ge(wexp_in, NB)
            act.activation(wexp[:, :, :], wexp[:, :, :], ACT.Exp).then_inc(wexp_done, 1)
            act.wait_ge(w_loaded, 32)
            for c in range(CH):
                shared((SF - 1) * CH + c, HI_PIECES[1] if c == 1 else (), HI_PIECES[2 * c] if c < 2 else ())
            act.wait_ge(meta_ready, 1)
            front(SF * CH)
            expert(0, True, False)
            with act.Fori(1, E - 1) as e:
                expert(e, False, False)
            expert(E - 1, False, True)
            rear()

        @block.vector
        def _(dve):
            def input_scale(b, t):
                tile = TPB * b + t
                wait(dve, rsx_done, tile + 1)
                wait(dve, xT_ps, tile - 1)
                dve.tensor_scalar(xs[:, t, :], x_all[:, tile, :], rsx[:, t:t + 1], None, ALU.mult).then_inc(xs_ready, 1)

            def product_sums(kind, b, t):
                tile = TPB * b + t
                if kind == "op":
                    wait(dve, h_copied, tile + 1)
                    dve.tensor_tensor(x_all[:, tile, :], h_sb[:, t, :], x_all[:, tile, :], ALU.add).then_inc(h_added, 1)
                elif kind != "v":
                    n = n_kq(b) + KQ_ORDER[kind, t]
                    wait(dve, kq_sq, n + 1)
                    wait(dve, kq_rs, n)
                    dve.reduce_sum(ss[:, :], sq[:, :].rearrange("p (h d) -> p h d", d=DH), AX_X).then_inc(kq_ss, 1)

            def product_scale(kind, b, t):
                tile = TPB * b + t
                if kind == "op":
                    wait(dve, rsh_done, tile + 1)
                    wait(dve, xn_free, two_before(tile, t))
                    wait(dve, nT_ps, two_before(tile, t))
                    dve.scalar_tensor_tensor(out=xn[:, t, :], in0=h_sb[:, t, :], scalar=rsh[:, t:t + 1], in1=nw[:, :],
                                             op0=ALU.mult, op1=ALU.mult).then_inc(xn_ready, 1)
                elif kind != "v":
                    m = KQ_ORDER[kind, t]
                    n = n_kq(b) + m
                    wait(dve, kq_rs, n + 1)
                    wait(dve, qk_ps, KC * b)
                    dve.tensor_tensor(qk_hat[:, m, :].rearrange("p (h d) -> p h d", d=DH),
                                      kq_sb[:, m % 2, :].rearrange("p (h d) -> p h d", d=DH),
                                      rs[:, m % 2, :].unsqueeze(2).to_broadcast([P, HEADS, DH]), ALU.mult).then_inc(kq_hat, 1)

            def small_read(kind, b, t, bank):
                tile = TPB * b + t
                if kind == "xT":
                    wait(dve, xT_ps, tile + 1)
                    for k in range(KC):
                        ts = dve.tensor_scalar(xmT[:, t, k, :], psP[:, bank, k, :], scale_m[:, b, k:k + 1],
                                               shift_m[:, b, k:k + 1], ALU.mult, ALU.add)
                    ts.then_inc(xT_sb, 1)
                if kind == "rt":
                    wait(dve, rt_ps, tile + 1)
                    dve.tensor_copy(lg[:, t, :], psP[:, bank, 0, 0:E]).then_inc(lg_ready, 1)

            dve.memset(cum[:, 0, :], 0.0).then_inc(cum_next, 1)
            input_scale(0, 0)
            input_scale(0, 1)
            dve.wait_ge(mod_loaded, 32)
            dve.wait_ge(ss_ps, 1)
            dve.tensor_tensor(ss_emb[:, :, :], psF[:, 0:2 * KC * NB].rearrange("p (j b) -> p j b", b=NB),
                              bemb[:, :].unsqueeze(2).to_broadcast([P, 2 * KC, NB]), ALU.add).then_inc(ss_added, 1)
            dve.tensor_scalar(gnorm[:, :], gnorm[:, :], float(D) ** 0.5, None, ALU.mult).then_inc(mod_step, 1)
            dve.wait_ge(ss_added, 1)
            dve.wait_ge(mod_step, 1)
            dve.scalar_tensor_tensor(out=scale_m[:, :, :], in0=ss_emb[:, 0:KC, :].rearrange("p k b -> p b k"), scalar=1.0,
                                     in1=gnorm[:, :].unsqueeze(1).to_broadcast([P, NB, KC]),
                                     op0=ALU.add, op1=ALU.mult).then_inc(mod_ready, 1)
            dve.tensor_copy(shift_m[:, :, :], ss_emb[:, KC:2 * KC, :].rearrange("p k b -> p b k")).then_inc(mod_ready, 1)
            dve.wait_ge(mod_ready, 2)
            small_read("xT", 0, 0, 0)
            small_read("xT", 0, 1, 1)
            for i, (kind, _, t) in enumerate(BIG[2:]):
                product_sums(kind, 0, t)
                product_scale(kind, 0, t)
                if i == 1:
                    input_scale(1, 0)
            dve.wait_ge(small_loaded, 16 * (1 + 2 * HPC))
            dve.tensor_scalar(nw[:, :], nw[:, :], float(D) ** 0.5, None, ALU.mult).then_inc(nw_ready, 1)
            dve.scalar_tensor_tensor(out=gqk[:, 2:3], in0=gqk[:, 0:1], scalar=float(DH) ** 0.5, in1=gqk[:, 1:2],
                                     op0=ALU.mult, op1=ALU.mult).then_inc(gqk_ready, 1)
            dve.wait_ge(nw_ready, 1)
            small_read("xT", 1, 0, 1)
            dve.wait_ge(wout_loaded, 16)
            dve.wait_ge(consts_ready, 2)
            for k in range(KC):
                tt = dve.tensor_tensor(wout[:, k, k * P:(k + 1) * P], wout[:, k, k * P:(k + 1) * P], ident[:, :], ALU.add)
            tt.then_inc(wout_ready, 1)

            def choose(b):
                steps, tile0 = ROUTE_STEPS * b, TPB * b
                wait(dve, lg_ready, tile0 + TPB)
                dve.sem_inc(dve_passed, 1)
                for t in range(TPB):
                    mx = dve.max(top8[:, t, :], lg[:, t, :])
                mx.then_inc(top_done, 1)
                wait(dve, top_done, b + 1)
                dve.sem_inc(dve_passed, 1)
                for t in range(TPB):
                    mi = dve.max_index(idx8[:, t, :], top8[:, t, :], lg[:, t, :])
                mi.then_inc(rt_step, 1)
                dve.tensor_tensor(wexp[:, bass.ds(tile0, TPB), :], top8[:, :, 0:TOPK], top8[:, :, 0:1].to_broadcast([P, TPB, TOPK]),
                                  ALU.subtract).then_inc(wexp_in, 1)
                wait(dve, rt_step, steps + 1)
                dve.tensor_copy(idxf[:, :, :], idx8[:, :, 0:TOPK]).then_inc(rt_step, 1)
                wait(dve, rt_step, steps + 2)
                dve.tensor_tensor(onehot[:, :, :, :].rearrange("p t k e -> p (t k) e"),
                                  iota_e[:, 0:E].unsqueeze(1).to_broadcast([P, TPB * TOPK, E]),
                                  idxf[:, :, :].rearrange("p t k -> p (t k)").unsqueeze(2).to_broadcast([P, TPB * TOPK, E]),
                                  ALU.is_equal).then_inc(rt_step, 1)
                wait(dve, rt_step, steps + 3)
                dve.reduce_sum(mask[:, :, :], onehot[:, :, :, :].rearrange("p t k e -> p t e k"), AX_X).then_inc(mask_ready, 1)
                wait(dve, mask_ready, b + 1)
                wait(dve, cum_next, b + 1)
                dve.tensor_tensor(cum[:, 1, :], cum[:, 0, :], mask[:, 0, :], ALU.add).then_inc(cum_ready, 1)

            def place(b, bank):
                steps = ROUTE_STEPS * b
                wait(dve, pos_ps, b + 1)
                dve.tensor_tensor(onehot[:, :, :, :], onehot[:, :, :, :],
                                  psP[:, bank, 0, 0:TPB * E].rearrange("p (t e) -> p t e", e=E).unsqueeze(2).to_broadcast([P, TPB, TOPK, E]),
                                  ALU.mult).then_inc(rt_step, 1)
                if not (isinstance(b, int) and b == NB - 1):
                    dve.tensor_tensor(cum[:, 0, :], cum[:, 1, :], mask[:, 1, :], ALU.add).then_inc(cum_next, 1)
                wait(dve, rt_step, steps + POS_READ)
                dve.reduce_sum(posk[:, :, :], onehot[:, :, :, :], AX_X).then_inc(rt_step, 1)
                wait(dve, rt_step, steps + 5)
                dve.tensor_scalar(over[:, :, :], posk[:, :, :], float(CAP), float(SKIP), ALU.is_ge, ALU.mult).then_inc(rt_step, 1)
                dve.tensor_scalar(posk[:, :, :], posk[:, :, :], float(CAP - 1), None, ALU.min).then_inc(rt_step, 1)
                wait(dve, rt_step, steps + 7)
                dve.scalar_tensor_tensor(out=slot[:, :, :], in0=idxf[:, :, :], scalar=float(CAP), in1=posk[:, :, :],
                                         op0=ALU.mult, op1=ALU.add).then_inc(rt_step, 1)
                wait(dve, rt_step, steps + 8)
                wait(dve, scattered, 16 * TPB * TOPK * b)
                dve.tensor_tensor(scat_cur[:, :, :], slot[:, :, :], over[:, :, :], ALU.add).then_inc(scat_ready, 1)
                dve.tensor_copy(tok_cur[:, :], tok_id[:, bass.ds(TPB * b, TPB)]).then_inc(scat_ready, 1)
                dve.tensor_copy(slot_i[:, bass.ds(TPB * b, TPB), :], slot[:, :, :]).then_inc(slots_ready, 1)

            def body(b, first, last, before_last):
                def row_max(u):
                    n = UNITS * b + u
                    wait(dve, scores_ready, n + 1)
                    wait(dve, exp_done, n - 1)
                    dve.tensor_reduce(nmax[:, u % 2, :].rearrange("p (a t) -> p a t", a=HPU), psS[:, u % 2, :, :, :],
                                      AX_X, ALU.max, negate=True).then_inc(max_ready, 1)

                def normalise(u):
                    n = UNITS * b + u
                    wait(dve, exp_done, n + 1)
                    wait(dve, probs_ready, n - 1)
                    dve.reciprocal(rsums[:, u % 2, :], sums[:, u % 2, :]).then_inc(sums_read, 1)
                    wait(dve, sums_read, n + 1)
                    for i in range(BLK):
                        ts = dve.tensor_scalar(probs[:, u % 2, i, :], probs[:, u % 2, i, :], rsums[:, u % 2, i:i + 1], None, ALU.mult)
                    ts.then_inc(probs_ready, 1)

                def probs_read(u):
                    wait(dve, pT_ps, UNITS * b + u + 1)
                    dve.tensor_copy(probsT[:, 0, :, :].rearrange("p c n -> p (c n)"),
                                    psP[:, 0, :, :].rearrange("p c n -> p (c n)")).then_inc(pT_sb0, 1)

                def product_task(do, u):
                    if u < 0:
                        return
                    kind, off, t = BIG[u]
                    if exists(b, off, first, last, before_last):
                        do(kind, b + off, t)

                row_max(0)
                normalise(0)
                for u in range(UNITS):
                    n = UNITS * b + u
                    if u:
                        probs_read(u)
                    if u + 1 < UNITS:
                        row_max(u + 1)
                    product_task(product_sums, u - 1)
                    if not u:
                        probs_read(u)
                    if u + 1 < UNITS:
                        normalise(u + 1)
                    for kind, off, t, bank in SMALL[u]:
                        if exists(b, off, first, last, before_last):
                            if kind == "pos":
                                place(b + off, bank)
                            else:
                                small_read(kind, b + off, t, bank)
                    if u == ROUTE_CHOICES and not first:
                        choose(b - 1)
                    if u % 2:
                        wait(dve, pv_done, n + 1)
                        dve.tensor_copy(oT[:, :, u // 2, :], psO[:, 0:SEQ].rearrange("p (t n) -> p t n", n=P)).then_inc(oT_ready, 1)
                    if last and u < PIECES:
                        weights_lo(0, u)
                    product_task(product_scale, u - 1)
                    if u in XS and exists(b, XS[u][0], first, last, before_last):
                        input_scale(b + XS[u][0], XS[u][1])

            def weights_lo(f, i):
                raw, hi, lo = piece_of(f, i)
                dve.wait_ge(w_hi, PIECES * f + i + 1)
                dve.tensor_tensor(lo, raw, hi, ALU.subtract).then_inc(w_split, 1)

            def rows_lo(k):
                dve.wait_ge(xhi_done, k + 1)
                dve.tensor_tensor(xT_lo[:, :, :], psXT, xT_hi[:, :, :], ALU.subtract).then_inc(xTs_ready, 1)

            batches(dve, body)
            for t in range(TPB):
                product_sums("op", NB - 1, t)
                product_scale("op", NB - 1, t)
            rows_lo(0)
            for t in range(TPB):
                small_read("rt", NB - 1, t, 0)
            choose(NB - 1)
            place(NB - 1, 1)

            def hidden(k):
                wait(dve, sg_ready, k + 1)
                dve.tensor_tensor(hid[:, :], psG1[:, I:2 * I], sg[:, :], ALU.mult).then_inc(hid_ready, 1)

            def front(k, more=True, split=None, pieces=()):
                hidden(k)
                if more:
                    rows_lo(k + 1)
                for i in pieces:
                    weights_lo(split, i)

            def add_shared(k, tile):
                dve.wait_ge(g2_done, k + 1)
                dve.wait_ge(h_added, tile + 1)
                dve.tensor_tensor(x_all[:, tile, :], psG2, x_all[:, tile, :], ALU.add).then_inc(orow_ready, 1)

            def back(k, split=None, pieces=(), add=None):
                if add is not None:
                    add_shared(*add)
                dve.wait_ge(hhi_done, k + 1)
                dve.tensor_tensor(hidT_lo[:, :, :], psHT, hidT_hi[:, :, :], ALU.subtract).then_inc(hidT_ready, 1)
                for i in pieces:
                    weights_lo(split, i)

            def shared(k, pieces_front=(), pieces_back=()):
                front(k, True, 1, pieces_front)
                back(k, 1, pieces_back, (k - 1, k - 1) if k else None)
                if k == TAB_STEP:
                    dve.wait_ge(tab_loaded, 16)
                    dve.tensor_copy(tab_f[:, :], tab_i[:, :]).then_inc(tabf_ready, 1)
                    dve.wait_ge(tabT_ps, 1)
                    dve.tensor_copy(idx_all[:, :], psP[:, 0, 0, :]).then_inc(idx_ready, 1)

            def expert(e, first):
                before, s, more_steps = steps_of(dve, e)
                f = e + 2
                back(s, f, LO_PIECES[0], (SF * CH - 1, SF * CH - 1) if first else None)
                with dve.If(more_steps > 1):
                    front(s + 1, True, f, LO_PIECES[1])
                    back(s + 1, f, LO_PIECES[2])
                    with dve.If(more_steps > 2):
                        front(s + 2)
                        back(s + 2)
                    with dve.Else():
                        pass
                    front(s + more_steps)
                    back(s + more_steps)
                with dve.Else():
                    front(s + 1, True, f, LO_PIECES[1])
                    back(s + 1, f, LO_PIECES[2])
                front(s + more_steps + 1)

            def combine(tile, a, loads):
                dve.wait_ge(rows_c_in[a], 16 * TOPK * loads)
                for k in range(TOPK):
                    if k:
                        wait(dve, acc_step, (TOPK - 1) * tile + k)
                    add = dve.scalar_tensor_tensor(out=x_all[:, tile, :], in0=rows_c[:, a, k, :], scalar=w_all[:, tile, k:k + 1],
                                                   in1=x_all[:, tile, :], op0=ALU.mult, op1=ALU.add)
                    add.then_inc(acc_step if k < TOPK - 1 else acc_done, 1)

            def rear():
                before, k, _ = steps_of(dve, E)
                for i in range(SR):
                    back(k + i, add=(before + i, SF * CH + i - 1) if i else None)
                    if i + 1 < SR:
                        front(k + i + 1, i + 2 < SR)
                    combine(i, i % GBUF, i // GBUF + 1)
                add_shared(before + SR, NT - 1)
                dve.wait_ge(orow_ready, k + SR)
                dve.sem_inc(dve_passed, 1)

            for k in range((SF - 1) * CH):
                shared(k)
            dve.wait_ge(totals_ps, 1)
            total = psP[0:1, 0, 0, 0:E]
            dve.memset(cnt[:, 0, :, 0:1], 0.0).then_inc(cnt_step, 1)
            dve.memset(meta_f[:, E, 1:2], 0.0).then_inc(cnt_step, 1)
            dve.tensor_scalar(cnt[:, 0, 0, 1:E + 1], total, float(2 * P), None, ALU.is_gt).then_inc(cnt_step, 1)
            dve.tensor_scalar(cnt[:, 0, 1, 1:E + 1], total, float(3 * P), None, ALU.is_gt).then_inc(cnt_step, 1)
            dve.wait_ge(cnt_step, 4)
            dve.scalar_tensor_tensor(out=meta_f[:, 0:E, 1], in0=cnt[:, 0, 0, 1:E + 1], scalar=1.0, in1=cnt[:, 0, 1, 1:E + 1],
                                     op0=ALU.add, op1=ALU.add).then_inc(cnt_step, 1)
            src, dst, spare, done = cnt[:, 0, :, :], cnt[:, 1, :, :], cnt[:, 2, :, :], 5
            sh = 1
            while sh < E + 1:
                dve.wait_ge(cnt_step, done)
                dve.tensor_copy(dst[:, :, 0:sh], src[:, :, 0:sh]).then_inc(cnt_step, 1)
                dve.tensor_tensor(dst[:, :, sh:E + 1], src[:, :, sh:E + 1], src[:, :, 0:E + 1 - sh], ALU.add).then_inc(cnt_step, 1)
                done += 2
                src, dst, spare = dst, spare, src
                sh *= 2
            dve.wait_ge(cnt_step, done)
            dve.tensor_copy(meta_f[:, :, 2:4].rearrange("p e k -> p k e"), src).then_inc(cnt_step, 1)
            dve.tensor_tensor(cnt_sum[:, :], src[:, 0, :], src[:, 1, :], ALU.add).then_inc(cnt_step, 1)
            dve.wait_ge(cnt_step, done + 2)
            dve.scalar_tensor_tensor(out=cnt_sum[:, :], in0=iota_e[0:1, :], scalar=2.0, in1=cnt_sum[:, :],
                                     op0=ALU.mult, op1=ALU.add).then_inc(cnt_step, 1)
            dve.wait_ge(cnt_step, done + 3)
            dve.tensor_scalar(meta_f[:, :, 0], cnt_sum[:, :], float(SF * CH - 1), None, ALU.add).then_inc(cnt_step, 1)
            dve.wait_ge(cnt_step, done + 4)
            dve.tensor_copy(meta[:, :, :], meta_f[:, :, :]).then_inc(meta_ready, 1)
            dve.wait_ge(wexp_done, 1)
            dve.reduce_sum(wsum[:, :], wexp[:, :, :], AX_X).then_inc(w_step, 1)
            dve.wait_ge(w_step, 1)
            dve.reciprocal(wrec[:, :], wsum[:, :]).then_inc(w_step, 1)
            dve.wait_ge(w_step, 2)
            dve.tensor_tensor(w_all[:, :, :], wexp[:, :, :], wrec[:, :].unsqueeze(2).to_broadcast([P, NT, TOPK]),
                              ALU.mult).then_inc(w_ready, 1)
            for c in range(CH):
                shared((SF - 1) * CH + c, LO_PIECES[1] if c == 1 else (), LO_PIECES[2 * c] if c < 2 else ())
            dve.wait_ge(meta_ready, 1)
            front(SF * CH)
            expert(0, True)
            with dve.Fori(1, E) as e:
                expert(e, False)
            dve.wait_ge(w_ready, 1)
            dve.wait_ge(orow_ready, SF * CH)
            rear()
            with dve.Fori(SR // GBUF, NT // GBUF) as i:
                for a in range(GBUF):
                    combine(GBUF * i + a, a, i + 1)


_INS = ["x", "cond_2048", "L0_cond_W_emb", "L0_cond_b_emb", "L0_cond_g_norm", "L0_cond_W_qkv", "L0_cond_g_q", "L0_cond_g_k",
        "L0_cond_W_out", "L0_ffn_norm_w", "L0_ffn_gate_w", "L0_ffn_w13", "L0_ffn_w2", "L0_ffn_shared_gate_w",
        "L0_ffn_shared_up_w", "L0_ffn_shared_down_w"]


def kernel(**inputs):
    import numpy as np
    from concourse import bacc
    from concourse.bass_utils import run_bass_kernel_spmd

    nc = bacc.Bacc("TRN2", target_bir_lowering=False, num_devices=1)
    arrays, args = {}, []
    for name in _INS:
        a = np.ascontiguousarray(inputs[name])
        arrays[f"in_{name}"] = a
        args.append(nc.dram_tensor(f"in_{name}", a.shape, mybir.dt.from_np(a.dtype), kind="ExternalInput").ap())
    out = nc.dram_tensor("out_rows", (NB, SEQ, D), F32, kind="ExternalOutput").ap()
    adaln_moe_kernel(nc, *args, out)
    r = run_bass_kernel_spmd(nc, [arrays], core_ids=[0])
    return r.results[0]["out_rows"]
```
